# Optimizing a Trainium2 kernel written in Bass

```python
import numpy as np
import jax
import jax.numpy as jnp

def _softmax(x, axis=-1):
    return jax.nn.softmax(x, axis=axis)

def _gelu(x):
    return jax.nn.gelu(x, approximate=True)

def _silu(x):
    return jax.nn.silu(x)

def _sigmoid(x):
    return jax.nn.sigmoid(x)

def _layernorm(x, axis=-1, eps=1e-05):
    m = jnp.mean(x, axis=axis, keepdims=True)
    v = jnp.var(x, axis=axis, keepdims=True)
    return (x - m) / jnp.sqrt(v + eps)

def _scatter_add(tgt, idx, src, axis=0):
    return tgt.at[idx].add(src)

def _segment_sum(src, seg, n):
    return jax.ops.segment_sum(src, seg, n)
kernel_name = 'mk_xattn_ffn_d1_seqx_r4_89651b'

def setup_inputs(seed: int=0):
    np.random.seed(seed)
    _w = jnp.asarray

    def _rec_inputs():
        import jax
        import jax.numpy as jnp
        _rk = jax.random.key(seed)
        x = -0.0003929 + 0.9999 * jax.random.normal(jax.random.fold_in(_rk, 1), (4, 512, 256), jnp.float32)
        _lenS = 512 - jax.random.randint(jax.random.fold_in(_rk, 7), (4,), 0, max(1, 512 // 4) + 1, jnp.int32)
        _lenS2 = 512 - jax.random.randint(jax.random.fold_in(_rk, 8), (4,), 0, max(1, 512 // 4) + 1, jnp.int32)
        _ctx_1024P = jax.random.normal(jax.random.fold_in(_rk, 11), (4, 16, 256), jnp.float32)
        _ctx_1024c = jax.random.dirichlet(jax.random.fold_in(_rk, 511), 0.3 * jnp.ones((16,), jnp.float32), (4, 512))
        _ctx_1024t = jnp.einsum('bsk,bkd->bsd', _ctx_1024c, _ctx_1024P)
        _ctx_1024t = _ctx_1024t * jax.lax.rsqrt(jnp.mean(jnp.square(_ctx_1024t)) + 1e-12) * 0.953939
        ctx_1024 = 2.81802e-05 + 1.00001 * (_ctx_1024t + 0.3 * jax.random.normal(jax.random.fold_in(_rk, 611), (4, 512, 256), jnp.float32))
        return (x, ctx_1024)
    x, ctx_1024 = _rec_inputs()

    def _L0_xattn_setup():
        import jax, jax.numpy as jnp
        import numpy as np
        D_MODEL = 256
        N_HEADS = 16
        TOP_K = 3
        key = jax.random.key(seed)
        ks = jax.random.split(key, 12)
        B, L = (4, 1024)
        s = 0.02
        inp = {'q': jax.random.normal(ks[0], (B, L, D_MODEL), jnp.float32), 'k': jax.random.normal(ks[1], (B, L, D_MODEL), jnp.float32), 'v': jax.random.normal(ks[2], (B, L, D_MODEL), jnp.float32), 'Wq': jax.random.normal(ks[3], (D_MODEL, D_MODEL), jnp.float32) * s, 'bq': jax.random.normal(ks[4], (D_MODEL,), jnp.float32) * s, 'Wk': jax.random.normal(ks[5], (D_MODEL, D_MODEL), jnp.float32) * s, 'bk': jax.random.normal(ks[6], (D_MODEL,), jnp.float32) * s, 'Wv': jax.random.normal(ks[7], (D_MODEL, D_MODEL), jnp.float32) * s, 'bv': jax.random.normal(ks[8], (D_MODEL,), jnp.float32) * s, 'Wo': jax.random.normal(ks[9], (D_MODEL, D_MODEL), jnp.float32) * s, 'bo': jax.random.normal(ks[10], (D_MODEL,), jnp.float32) * s}
        return inp
    _L0_xattn_all = _L0_xattn_setup()
    _L0_xattn_in = {k: v for k, v in _L0_xattn_all.items() if k in ('Wq', 'bq', 'Wk', 'bk', 'Wv', 'bv', 'Wo', 'bo')}
    del _L0_xattn_all

    def _L0_ffn_setup():
        import jax, jax.numpy as jnp
        import numpy as np
        E, TOP_K, D, H = (8, 2, 256, 512)
        B, S = (2, 512)
        key = jax.random.key(seed)
        ks = jax.random.split(key, 10)
        s = 0.02
        return {'x': jax.random.normal(ks[0], (B, S, D), dtype=jnp.float32), 'gate_w': jax.random.normal(ks[1], (E, D), dtype=jnp.float32) * s, 'gate_b': jnp.zeros((E,), dtype=jnp.float32), 'w0': jax.random.normal(ks[2], (E, H, D), dtype=jnp.float32) * s, 'b0': jnp.zeros((E, H), dtype=jnp.float32), 'w1': jax.random.normal(ks[3], (E, H, D), dtype=jnp.float32) * s, 'b1': jnp.zeros((E, H), dtype=jnp.float32), 'w2': jax.random.normal(ks[4], (E, D, H), dtype=jnp.float32) * s, 'b2': jnp.zeros((E, D), dtype=jnp.float32)}
    _L0_ffn_all = _L0_ffn_setup()
    _L0_ffn_in = {k: v for k, v in _L0_ffn_all.items() if k in ('gate_w', 'gate_b', 'w0', 'b0', 'w1', 'b1', 'w2', 'b2')}
    del _L0_ffn_all
    return {'x': x, 'ctx_1024': ctx_1024, 'L0_xattn_Wq': _L0_xattn_in['Wq'], 'L0_xattn_bq': _L0_xattn_in['bq'], 'L0_xattn_Wk': _L0_xattn_in['Wk'], 'L0_xattn_bk': _L0_xattn_in['bk'], 'L0_xattn_Wv': _L0_xattn_in['Wv'], 'L0_xattn_bv': _L0_xattn_in['bv'], 'L0_xattn_Wo': _L0_xattn_in['Wo'], 'L0_xattn_bo': _L0_xattn_in['bo'], 'L0_ffn_gate_w': _L0_ffn_in['gate_w'], 'L0_ffn_gate_b': _L0_ffn_in['gate_b'], 'L0_ffn_w0': _L0_ffn_in['w0'], 'L0_ffn_b0': _L0_ffn_in['b0'], 'L0_ffn_w1': _L0_ffn_in['w1'], 'L0_ffn_b1': _L0_ffn_in['b1'], 'L0_ffn_w2': _L0_ffn_in['w2'], 'L0_ffn_b2': _L0_ffn_in['b2']}

def reference(x, ctx_1024, L0_xattn_Wq, L0_xattn_bq, L0_xattn_Wk, L0_xattn_bk, L0_xattn_Wv, L0_xattn_bv, L0_xattn_Wo, L0_xattn_bo, L0_ffn_gate_w, L0_ffn_gate_b, L0_ffn_w0, L0_ffn_b0, L0_ffn_w1, L0_ffn_b1, L0_ffn_w2, L0_ffn_b2):
    import jax
    import jax.numpy as jnp

    def _L0_xattn_ref(q, k, v, Wq, bq, Wk, bk, Wv, bv, Wo, bo):
        import jax, jax.numpy as jnp
        import numpy as np
        D_MODEL = 256
        N_HEADS = 16
        TOP_K = 3
        B, L, _ = q.shape
        H, D = (N_HEADS, D_MODEL // N_HEADS)
        tk = min(TOP_K, L)

        def proj(x, W, b):
            return (x @ W.T + b).reshape(B, L, H, D).transpose(0, 2, 1, 3)
        Q = proj(q, Wq, bq)
        K = proj(k, Wk, bk)
        V = proj(v, Wv, bv)
        Qf = jnp.fft.rfft(Q, axis=2)
        Kf = jnp.fft.rfft(K, axis=2)
        corr = jnp.fft.irfft(Qf * jnp.conj(Kf), n=L, axis=2)
        corr_mean = corr.mean(axis=-1)
        weights, delays = jax.lax.top_k(corr_mean, tk)
        w = jax.nn.softmax(weights, axis=-1)
        idx = (jnp.arange(L)[None, None, None, :] - delays[..., None]) % L
        rolled = jnp.take_along_axis(V[:, :, None, :, :], idx[..., None], axis=3)
        out = jnp.einsum('bhk,bhkld->bhld', w, rolled)
        out = out.transpose(0, 2, 1, 3).reshape(B, L, H * D)
        return out @ Wo.T + bo

    def _L0_ffn_ref(x, gate_w, gate_b, w0, b0, w1, b1, w2, b2):
        import jax, jax.numpy as jnp
        import numpy as np
        E, TOP_K, D, H = (8, 2, 256, 512)
        B, S = (2, 512)
        Bn, Sq, Dv = x.shape
        xt = x.reshape(-1, Dv)
        logits = xt @ gate_w.T + gate_b
        top_v, top_i = jax.lax.top_k(logits, TOP_K)
        h0 = jnp.einsum('td,ehd->eth', xt, w0) + b0[:, None, :]
        h1 = jnp.einsum('td,ehd->eth', xt, w1) + b1[:, None, :]
        act = h0 * jax.nn.silu(h1)
        out_all = jnp.einsum('eth,edh->etd', act, w2) + b2[:, None, :]
        out_te = jnp.transpose(out_all, (1, 0, 2))
        sel = jnp.take_along_axis(out_te, top_i[:, :, None], axis=1)
        w = jax.nn.softmax(top_v, axis=-1)[:, :, None]
        out = (w * sel).sum(axis=1)
        return out.reshape(Bn, Sq, Dv)
    x = x + _L0_xattn_ref(_layernorm(x, axis=-1), ctx_1024, ctx_1024, L0_xattn_Wq, L0_xattn_bq, L0_xattn_Wk, L0_xattn_bk, L0_xattn_Wv, L0_xattn_bv, L0_xattn_Wo, L0_xattn_bo)
    x = x + _L0_ffn_ref(_layernorm(x, axis=-1), L0_ffn_gate_w, L0_ffn_gate_b, L0_ffn_w0, L0_ffn_b0, L0_ffn_w1, L0_ffn_b1, L0_ffn_w2, L0_ffn_b2)
    return x

_drawn_inputs = setup_inputs


def setup_inputs(seed=0):
    import zlib

    import numpy as np

    out = dict(_drawn_inputs(seed))
    spreads = {'L0_ffn_gate_b': (0.0, 0.1),
     'L0_ffn_b0': (0.0, 0.8),
     'L0_ffn_b1': (0.0, 0.8),
     'L0_ffn_b2': (0.0, 0.1)}
    factors = {'L0_xattn_bq': 200.0,
     'L0_xattn_bk': 200.0,
     'L0_xattn_bv': 6.212,
     'L0_ffn_w0': 3.155,
     'L0_ffn_w1': 3.177,
     'L0_ffn_w2': 3.009}
    for name, (base, spread) in spreads.items():
        noise = np.random.default_rng([zlib.crc32(name.encode()), seed]).standard_normal(out[name].shape)
        drawn = base * np.exp(spread * noise) if base else spread * noise
        out[name] = jnp.asarray(drawn.astype(out[name].dtype))
    for name, factor in factors.items():
        out[name] = (out[name] * factor).astype(out[name].dtype)
    return out
```

```python
from contextlib import ExitStack

import concourse.bass as bass
from concourse import mybir

P = 128
ALU = mybir.AluOpType
ACT = mybir.ActivationFunctionType
F32 = mybir.dt.float32
BF16 = mybir.dt.bfloat16
I32 = mybir.dt.int32
U32 = mybir.dt.uint32
AX_X = mybir.AxisListType.X

B, L, D = 4, 512, 256
H, HD = 16, 16
E, FH = 8, 512
TOPK = 3
HALF = L // 2
DT = D // P
TILES = B * L // P
TPB = L // P
NPAIR = B * H
EPS = 1e-5
KINDS = 4

BLOCKS = (2 * B * L + E * (P - 1)) // P
RING = 3
BLOCKS_PAD = BLOCKS + 2
ROW = D + E
WCOLS = 2 * DT * FH + (FH // P) * D
W2_AT = 2 * DT * FH
BCOLS = 2 * FH + D
FAR = 4096.0
PAD = -3.0e38

C_FWD = 0
C_INV = C_FWD + 4 * 256
C_ID = C_INV + KINDS * 256
C_IND = C_ID + P
C_TRI = C_IND + 16
C_ONE = C_TRI + P
C_IOTA = C_ONE + P
C_PART = C_IOTA + P
C_THR = C_PART + 1
C_TILE = C_THR + TILES
C_END = C_TILE + TILES


def build(nc, x, ctx_in, wqkvo, bqk, bvo, gate_w, gate_b, w_ffn, b_ffn, const, out):
    with ExitStack() as ctx:
        def sb(name, shape, dt=F32):
            return ctx.enter_context(nc.sbuf_tensor(name, shape, dt))

        def sem(name):
            return ctx.enter_context(nc.semaphore(name))

        cst = sb("cst", [P, C_END])
        fwd = cst[:, C_FWD:C_INV].rearrange("p (o c n) -> p o c n", o=2, c=2)
        inv = cst[:, C_INV:C_ID].rearrange("p (k n) -> p k n", k=KINDS)
        ident = cst[:, C_ID:C_IND]
        head_sum = cst[:, C_IND:C_TRI]
        before = cst[:, C_TRI:C_ONE]
        ones = cst[:, C_ONE:C_IOTA]
        iota = cst[:, C_IOTA:C_PART]
        part_no = cst[:, C_PART:C_THR]
        thresholds = cst[:, C_THR:C_TILE]
        tile_no = cst[:, C_TILE:C_END]

        wts = sb("wts", [P, E * WCOLS])
        w_att = sb("w_att", [P, 4, DT, D])
        wq, wk, wv, wo = (w_att[:, n] for n in range(4))
        gw = sb("gw", [P, DT, E])
        gb = sb("gb", [P, E])
        qk_bias = sb("qk_bias", [P, 2, DT])
        v_bias = sb("v_bias", [1, D])
        o_bias = sb("o_bias", [P, D])
        f_bias = sb("f_bias", [E, BCOLS])

        xs = sb("xs", [P, TILES, D])
        buf_b = sb("buf_b", [P, TILES * ROW])
        buf_c = sb("buf_c", [P, TILES * D])
        buf_d = sb("buf_d", [P, TILES * D])
        buf_g = sb("buf_g", [P, RING * (FH + D)])
        LATE = 3
        buf_f = wts[:, (E - LATE) * WCOLS:(E - LATE) * WCOLS + TILES * D]
        buf_e = wts[:, (E - LATE) * WCOLS + TILES * D:(E - LATE) * WCOLS + 2 * TILES * D]

        xn = buf_b[:, 0:TILES * D].rearrange("p (t d) -> p t d", d=D)
        v_spec = buf_b[:, 0:B * KINDS * D].rearrange("p (b k j) -> p b k j", b=B, k=KINDS)
        xn2 = buf_b[:, :].rearrange("p (t r) -> p t r", r=ROW)
        cs = buf_c[:, :].rearrange("p (t d) -> p t d", d=D)
        x_spec = buf_c[:, :].rearrange("p (c b f) -> p c b f", c=DT, b=B)
        uv_x = buf_d[:, :].rearrange("p (b o c d) -> p b o c d", b=B, o=2, c=2)
        q_spec = [buf_d[:, n * 2048:n * 2048 + 1024].rearrange("p (c f) -> p c f", c=DT) for n in range(2)]
        k_spec = [buf_d[:, n * 2048 + 1024:n * 2048 + 2048].rearrange("p (c f) -> p c f", c=DT) for n in range(2)]
        y_tmp = [buf_d[:, n * 512:n * 512 + 512] for n in range(4)]
        c_spec = buf_e[:, :].rearrange("p (c b f) -> p c b f", c=DT, b=B)
        zt = buf_e[:, :].rearrange("p (c b t) -> p c b t", c=DT, b=B)
        uv_c = buf_f[:, :].rearrange("p (b o c d) -> p b o c d", b=B, o=2, c=2)
        prod = [[buf_f[:, (n * 2 + m) * 1024:(n * 2 + m + 1) * 1024].rearrange("p (c f) -> p c f", c=DT)
                 for m in range(2)] for n in range(2)]
        y_spec = [buf_f[:, n * 1024:n * 1024 + 1024].rearrange("p (k j) -> p k j", k=KINDS) for n in range(2)]
        z_tmp = [buf_c[:, n * 512:n * 512 + 512] for n in range(2)]

        W_ = L + 8
        corr = buf_e[0:NPAIR, 0:W_]
        rest = buf_e[0:NPAIR, W_:2 * W_]
        c_eo = buf_e[0:NPAIR, 2 * W_:2 * W_ + L]
        c_exp = buf_e[0:NPAIR, 3 * W_:3 * W_ + L]
        c_mask = buf_e[0:NPAIR, 4 * W_:4 * W_ + L]
        c_w = buf_e[0:NPAIR, 5 * W_:5 * W_ + L]
        w_uv = buf_e[0:NPAIR, 6 * W_:6 * W_ + L]
        top8 = sb("top8", [P, 8])
        top3 = sb("top3", [P, 8])
        t_neg = sb("t_neg", [P, 4])
        t_exp = sb("t_exp", [P, 4])
        pt = sb("pt", [P, KINDS, NPAIR])
        w_t = sb("w_t", [P, 4, NPAIR])
        w_spec = sb("w_spec", [P, KINDS, NPAIR])
        w_re2 = sb("w_re2", [P, 2, NPAIR])
        nyq = sb("nyq", [P, DT])

        stats = sb("stats", [P, TILES, 6])
        ln = sb("ln", [P, 6, TILES])
        mean, var, sd, rstd, nmr, ltmp = (ln[:, n] for n in range(6))

        rt = buf_d[:, 2560:4096].rearrange("p (n t) -> p n t", n=12)
        lg, lg2, m1, m2, cum_a, cum_b, tot, rank, rtmp, cand = (rt[:, n] for n in range(10))
        r16 = sb("r16", [P, 8, TILES])
        r8 = sb("r8", [P, 6, E])
        nbt = sb("nbt", [P, E * TILES])
        slot_f = sb("slot_f", [P, 2 * TILES])
        slot_i = sb("slot_i", [P, 3, 2 * TILES], I32)
        slot_b = sb("slot_b", [P, 2, 2 * TILES])
        pos_hot = buf_d[:, 0:2 * TILES * P // 2].bitcast(BF16).rearrange("p (n s) -> p n s", s=P)
        blk_hot = buf_g[:, 0:2 * TILES * 3 * BLOCKS // 2].bitcast(BF16).rearrange(
            "p (n v s) -> p n v s", v=3, s=BLOCKS)
        eb_t = buf_d[:, 2048:2048 + BLOCKS_PAD * E]
        eb = sb("eb", [P, BLOCKS_PAD])
        eb_i = sb("eb_i", [P, BLOCKS_PAD], I32)
        e_hot = sb("e_hot", [P, BLOCKS_PAD])
        idx_f = sb("idx_f", [P, 3, BLOCKS])
        idx = sb("idx", [P, 2, BLOCKS_PAD], I32)
        gate_t = buf_c[:, 0:2048].rearrange("p (n c t) -> p n c t", n=4, c=DT * 2)

        xg = [buf_c[:, 2048 + n * ROW:2048 + (n + 1) * ROW] for n in range(RING)]
        xt = [buf_c[:, n * D:(n + 1) * D].rearrange("p (c t) -> p c t", c=DT) for n in range(RING)]
        bhot = [buf_c[0:E, 1024 + n * P:1024 + (n + 1) * P] for n in range(RING)]
        sil = [buf_d[:, n * FH:(n + 1) * FH] for n in range(RING)]
        act_ = [buf_d[:, 2048 + n * FH:2048 + (n + 1) * FH] for n in range(RING)]
        act_t = [buf_g[:, n * FH:(n + 1) * FH].rearrange("p (c t) -> p c t", c=FH // P) for n in range(RING)]
        yb = [buf_g[:, RING * FH + n * D:RING * FH + (n + 1) * D] for n in range(RING)]

        xn2_dram = nc.dram_tensor("xn2_dram", [B * L, ROW], F32).ap()
        out_rows = out.rearrange("b l d -> (b l) d")
        ps = [ctx.enter_context(nc.psum_tensor(f"ps{n}", [P, 512], F32)) for n in range(8)]

        s_cst, s_watt, s_small, s_wffn = sem("s_cst"), sem("s_watt"), sem("s_small"), sem("s_wffn")
        s_x = [sem(f"s_xin{b}") for b in range(B)]
        s_c = [sem(f"s_cin{b}") for b in range(B)]
        s_uvc, s_uvx = sem("s_uvc"), sem("s_uvx")
        s_xn, s_xbo = sem("s_xn"), sem("s_xbo")
        s_var, s_sd = sem("s_var"), sem("s_sd")
        s_fill, s_evac = sem("s_fill"), sem("s_evac")
        s_bias = sem("s_bias")
        s_prod, s_heads, s_pt = sem("s_prod"), sem("s_heads"), sem("s_pt")
        s_corr, s_ceo = sem("s_corr"), sem("s_ceo")
        s_neg, s_exp, s_wuv = sem("s_neg"), sem("s_exp"), sem("s_wuv")
        s_wtr, s_wt, s_wsp, s_wse, s_wtab = sem("s_wtr"), sem("s_wt"), sem("s_wsp"), sem("s_wse"), sem("s_wtab")
        s_yre, s_yim, s_vb = sem("s_yre"), sem("s_yim"), sem("s_vb")
        s_z, s_zc, s_zt, s_o, s_x1 = sem("s_z"), sem("s_zc"), sem("s_zt"), sem("s_o"), sem("s_x1")
        s_xn2, s_gt, s_gtc, s_lg = sem("s_xn2"), sem("s_gt"), sem("s_gtc"), sem("s_lg")
        s_m12, s_rexp, s_hot, s_rank = sem("s_m12"), sem("s_rexp"), sem("s_hot"), sem("s_rank")
        s_wcol, s_rowd, s_outd = sem("s_wcol"), sem("s_rowd"), sem("s_outd")
        s_slot, s_idxp, s_idx = sem("s_slot"), sem("s_idxp"), sem("s_idx")
        v_step, p_step = sem("v_step"), sem("p_step")
        s_xg = [sem(f"s_xg{n}") for n in range(RING)]
        s_xtp, s_xtc, s_bh = sem("s_xtp"), sem("s_xtc"), sem("s_bh")
        s_h1, s_h0, s_sil, s_act = sem("s_h1"), sem("s_h0"), sem("s_sil"), sem("s_act")
        s_atp, s_atc, s_yp, s_yb = sem("s_atp"), sem("s_atc"), sem("s_yp"), sem("s_yb")
        s_sc = sem("s_sc")

        block = ctx.enter_context(nc.Block())

        def chain(eng, step):
            n = [0]

            def link(ins):
                n[0] += 1
                ins.then_inc(step, 1)
                eng.wait_ge(step, n[0])
            return link

        N_C, N_X, N_V = DT * B, 2 * DT * B, 2 * DT * B + 2 * B
        FILLS = N_V + 2 * DT * B

        @block.sync
        def _(sp):
            sp.dma_start(cst[:, :], const).then_inc(s_cst, 16)
            cv = ctx_in.rearrange("b (a p) d -> b p a d", p=P)
            xv = x.rearrange("b (a p) d -> b p a d", p=P)
            for b in range(B):
                sp.dma_start(cs[:, b * TPB:(b + 1) * TPB, :], cv[b]).then_inc(s_c[b], 16)
                sp.dma_start(xs[:, b * TPB:(b + 1) * TPB, :], xv[b]).then_inc(s_x[b], 16)
            ov = out.rearrange("b (a p) d -> b p a d", p=P)
            for b in range(B):
                sp.wait_ge(s_x1, 2 * (b + 1))
                sp.dma_start(ov[b], xs[:, b * TPB:(b + 1) * TPB, :]).then_inc(s_outd, 16)
            sp.wait_ge(s_o, TILES // 2)
            for e in range(E - LATE, E):
                sp.dma_start(wts[:, e * WCOLS:(e + 1) * WCOLS], w_ffn[e]).then_inc(s_wffn, 16)
            sp.wait_ge(s_wcol, 1)
            sp.dma_start(xn2_dram.rearrange("(t p) r -> p t r", p=P), xn2).then_inc(s_rowd, 16)

        @block.gpsimd
        def _(pool):
            link = chain(pool, p_step)
            for b in range(B):
                pool.wait_ge(s_c[b], 16)
                lo, hi = cs[:, b * TPB:b * TPB + 2, :], cs[:, b * TPB + 2:b * TPB + 4, :]
                nc.gpsimd.tensor_tensor(uv_c[:, b, 0], lo, hi, ALU.add).then_inc(s_uvc, 1)
                nc.gpsimd.tensor_tensor(uv_c[:, b, 1], lo, hi, ALU.subtract).then_inc(s_uvc, 1)
            pool.wait_ge(s_small, 16 * 6)
            nc.gpsimd.tensor_scalar(qk_bias[:, :, :], qk_bias[:, :, :], float(L), None, ALU.mult).then_inc(s_bias, 1)
            nc.gpsimd.tensor_scalar(v_bias[:, :], v_bias[:, :], float(L), None, ALU.mult).then_inc(s_bias, 1)
            pool.wait_ge(s_xn, B)
            for t in range(TILES):
                nc.gpsimd.tensor_tensor(xs[:, t, :], xs[:, t, :], o_bias[:, :], ALU.add).then_inc(s_xbo, 1)
            pool.wait_ge(s_wtab, 1)
            pool.wait_ge(s_vb, 1)
            for b in range(B):
                v = v_spec[:, b].rearrange("p (o r) (h e) -> p o r h e", o=2, e=HD)
                w = w_spec[:, :, b * H:(b + 1) * H].rearrange("p (o r) h -> p o r h", o=2)
                wim = w[:, :, 1, :].unsqueeze(3).broadcast_to([P, 2, H, HD])
                wre2 = w_re2[:, :, b * H:(b + 1) * H].unsqueeze(3).broadcast_to([P, 2, H, HD])
                t3 = y_tmp[2].rearrange("p (o h e) -> p o h e", o=2, e=HD)
                t4 = y_tmp[3].rearrange("p (o h e) -> p o h e", o=2, e=HD)
                yim = y_spec[b % 2].rearrange("p (o r) (h e) -> p o r h e", o=2, e=HD)[:, :, 1]
                for o in range(2):
                    nc.gpsimd.tensor_tensor(t3[:, o], v[:, o, 0], wim[:, o], ALU.mult)
                    ins = nc.gpsimd.tensor_tensor(t4[:, o], v[:, o, 1], wre2[:, o], ALU.mult)
                link(ins)
                if b >= 2:
                    pool.wait_ge(s_z, DT * (b - 1))
                for o in range(2):
                    ins = nc.gpsimd.tensor_tensor(yim[:, o], t3[:, o], t4[:, o], ALU.add)
                ins.then_inc(s_yim, 1)
                if b < B - 1:
                    pool.wait_ge(s_yim, b + 1)

            def gather(i):
                nc.gpsimd.indirect_dma_start(
                    out=xg[i % RING], out_offset=None, in_=xn2_dram,
                    in_offset=bass.IndirectOffsetOnAxis(idx[:, 0, i:i + 1], axis=0)).then_inc(s_xg[i % RING], 16)

            pool.wait_ge(s_idx, 1)
            pool.wait_ge(s_rowd, 16)
            for i in range(RING):
                gather(i)
            pool.wait_ge(s_outd, 16 * B)
            for i in range(BLOCKS):
                pool.wait_ge(s_yb, i + 1)
                if i:
                    pool.wait_ge(s_sc, 16 * i)
                nc.gpsimd.indirect_dma_start(
                    out=out_rows, out_offset=bass.IndirectOffsetOnAxis(idx[:, 1, i:i + 1], axis=0),
                    in_=yb[i % RING], in_offset=None, bounds_check=B * L - 1, oob_is_err=False,
                    compute_op=ALU.add).then_inc(s_sc, 16)
                if i + RING < BLOCKS:
                    gather(i + RING)
            pool.wait_ge(s_sc, 16 * BLOCKS)

        @block.scalar
        def _(act):
            act.dma_start(w_att[:, :, :, :].rearrange("p n c j -> p n (c j)"),
                          wqkvo.rearrange("n p m -> p n m")).then_inc(s_watt, 16)
            act.dma_start(qk_bias[:, :, :].rearrange("p n c -> p (n c)"), bqk).then_inc(s_small, 16)
            act.dma_start(v_bias[:, :], bvo[0:1, :]).then_inc(s_small, 16)
            act.dma_start(o_bias[:, :], bvo[1:2, :].broadcast_to([P, D])).then_inc(s_small, 16)
            act.dma_start(gw[:, :, :], gate_w.rearrange("(c p) e -> p c e", p=P)).then_inc(s_small, 16)
            act.dma_start(gb[:, :], gate_b.broadcast_to([P, E])).then_inc(s_small, 16)
            act.dma_start(f_bias[:, :], b_ffn).then_inc(s_small, 16)
            for e in range(E - LATE):
                act.dma_start(wts[:, e * WCOLS:(e + 1) * WCOLS], w_ffn[e]).then_inc(s_wffn, 16)

            def copy(o, i):
                return nc.scalar.activation(o, i, ACT.Copy)

            def root(n):
                act.wait_ge(s_var, n + 1)
                b = n % B
                nc.scalar.activation(sd[:, b * TPB:(b + 1) * TPB], var[:, b * TPB:(b + 1) * TPB],
                                     ACT.Sqrt).then_inc(s_sd, 1)

            for b in range(B):
                root(b)
            for n in range(FILLS):
                act.wait_ge(s_fill, n + 1)
                bank = ps[n % 4]
                if n < N_C:
                    dst, src = c_spec[:, n % DT, n // DT, :], bank[:, :]
                elif n < N_X:
                    m = n - N_C
                    if m == 0:
                        act.wait_ge(s_uvc, 2 * B)
                    dst, src = x_spec[:, m % DT, m // DT, :], bank[:, :]
                elif n < N_V:
                    m = n - N_X
                    if m == 0:
                        act.wait_ge(s_uvx, 2 * B)
                    dst = v_spec[:, m // 2, 2 * (m % 2):2 * (m % 2) + 2, :].rearrange("p k j -> p (k j)")
                    src = bank[:, :]
                else:
                    b, m = divmod(n - N_V, 2 * DT)
                    if b >= 2 and m == 0:
                        act.wait_ge(s_prod, 2 * (b - 1))
                    dst = (k_spec, q_spec)[m // DT][b % 2][:, m % DT, :]
                    src = bank[:, :]
                copy(dst, src).then_inc(s_evac, 1)
            act.wait_ge(s_heads, B)
            copy(pt[:, :, :].rearrange("p k n -> p (k n)"), ps[4][:, 0:KINDS * NPAIR]).then_inc(s_pt, 1)
            act.wait_ge(s_corr, 1)
            nc.scalar.activation(c_eo, ps[5][0:NPAIR, :], ACT.Copy, scale=1.0 / HD).then_inc(s_ceo, 1)
            act.wait_ge(s_neg, 1)
            nc.scalar.activation(c_exp, corr[:, 0:L], ACT.Exp, bias=t_neg[0:NPAIR, 0:1]).then_inc(s_exp, 1)
            nc.scalar.activation(t_exp[0:NPAIR, 0:TOPK], top8[0:NPAIR, 0:TOPK], ACT.Exp,
                                 bias=t_neg[0:NPAIR, 0:1]).then_inc(s_exp, 1)
            act.wait_ge(s_wtr, 1)
            copy(w_t[:, :, :].rearrange("p c n -> p (c n)"), ps[6][:, 0:4 * NPAIR]).then_inc(s_wt, 1)
            act.wait_ge(s_wsp, 1)
            copy(w_spec[:, :, :].rearrange("p k n -> p (k n)"), ps[7][:, 0:KINDS * NPAIR]).then_inc(s_wse, 1)
            for n in range(DT * B):
                act.wait_ge(s_z, n + 1)
                if n >= 2:
                    act.wait_ge(s_zt, 2 * (n - 1))
                copy(z_tmp[n % 2], ps[n % 4][:, :]).then_inc(s_zc, 1)
            for b in range(B):
                root(B + b)
            for n in range(TILES // 2):
                act.wait_ge(s_gt, n + 1)
                if n >= 4:
                    act.wait_ge(s_lg, n - 3)
                copy(gate_t[:, n % 4].rearrange("p c t -> p (c t)"), ps[n % 2][:, :]).then_inc(s_gtc, 1)
            act.wait_ge(s_m12, 1)
            nc.scalar.activation(r16[:, 3, :], r16[:, 2, :], ACT.Exp).then_inc(s_rexp, 1)

            def xt_out(i, n):
                act.wait_ge(s_xtp, i + 1)
                copy(xt[n].rearrange("p c t -> p (c t)"), ps[4][:, 0:D]).then_inc(s_xtc, 1)

            def silu(i, n):
                act.wait_ge(s_h1, i + 1)
                nc.scalar.activation(sil[n], ps[0][:, :], ACT.Silu).then_inc(s_sil, 1)

            def y_out(i, n):
                e = act.value_load(eb_i[0:1, bass.ds(i, 1)], min_val=0, max_val=E - 1)
                act.wait_ge(s_yp, i + 1)
                nc.scalar.activation(yb[n], ps[6][:, 0:D], ACT.Copy, scale=xg[n][:, bass.ds(D + e, 1)]).then_inc(s_yb, 1)

            act.wait_ge(s_slot, 2)
            xt_out(0, 0)
            silu(0, 0)
            xt_out(1, 1)

            def step(i, n, ahead=RING, reused=True):
                if ahead > 1:
                    silu(i + 1, (n + 1) % RING)
                if ahead > 2:
                    xt_out(i + 2, (n + 2) % RING)
                if reused:
                    act.wait_ge(s_sc, 16 * (i + 1 - RING))
                y_out(i, n)

            for n in range(RING):
                step(n, n, reused=False)
            with act.Fori(RING, BLOCKS - RING, RING) as i0:
                for n in range(RING):
                    step(i0 + n, n)
            for n in range(RING):
                step(BLOCKS - RING + n, n, ahead=RING - n)

        @block.vector
        def _(dve):
            link = chain(dve, v_step)
            tt, ts = nc.vector.tensor_tensor, nc.vector.tensor_scalar

            def ln_stats(b, src, n):
                for t in range(b * TPB, (b + 1) * TPB):
                    ins = nc.vector.bn_stats(stats[:, t, :], src[:, t, :])
                link(ins)
                c = slice(b * TPB, (b + 1) * TPB)
                me, mo = stats[:, c, 1], stats[:, c, 4]
                se, so = stats[:, c, 2], stats[:, c, 5]
                tt(mean[:, c], me, mo, ALU.add)
                tt(ltmp[:, c], me, mo, ALU.subtract)
                link(tt(var[:, c], se, so, ALU.add))
                ts(mean[:, c], mean[:, c], 0.5, None, ALU.mult)
                link(nc.vector.scalar_tensor_tensor(out=ltmp[:, c], in0=ltmp[:, c], scalar=0.25,
                                                    in1=ltmp[:, c], op0=ALU.mult, op1=ALU.mult))
                link(nc.vector.scalar_tensor_tensor(out=var[:, c], in0=var[:, c], scalar=1.0 / D,
                                                    in1=ltmp[:, c], op0=ALU.mult, op1=ALU.add))
                ts(var[:, c], var[:, c], EPS, None, ALU.add).then_inc(s_var, 1)

            def ln_norm(b, src, dst, n):
                c = slice(b * TPB, (b + 1) * TPB)
                dve.wait_ge(s_sd, n + 1)
                link(nc.vector.reciprocal(rstd[:, c], sd[:, c]))
                link(tt(ltmp[:, c], rstd[:, c], rstd[:, c], ALU.mult))
                link(tt(ltmp[:, c], ltmp[:, c], var[:, c], ALU.mult))
                link(ts(ltmp[:, c], ltmp[:, c], -0.5, 1.5, ALU.mult, ALU.add))
                link(tt(rstd[:, c], rstd[:, c], ltmp[:, c], ALU.mult))
                link(nc.vector.scalar_tensor_tensor(out=nmr[:, c], in0=mean[:, c], scalar=-1.0,
                                                    in1=rstd[:, c], op0=ALU.mult, op1=ALU.mult))
                for t in range(b * TPB, (b + 1) * TPB):
                    ins = ts(dst[:, t, 0:D], src[:, t, :], rstd[:, t:t + 1], nmr[:, t:t + 1], ALU.mult, ALU.add)
                return ins

            def uv(b):
                lo, hi = xn[:, b * TPB:b * TPB + 2, :], xn[:, b * TPB + 2:b * TPB + 4, :]
                tt(uv_x[:, b, 0], lo, hi, ALU.add).then_inc(s_uvx, 1)
                tt(uv_x[:, b, 1], lo, hi, ALU.subtract).then_inc(s_uvx, 1)

            for b in range(B):
                dve.wait_ge(s_x[b], 16)
                ln_stats(b, xs, b)
                if b:
                    ln_norm(b - 1, xs, xn, b - 1).then_inc(s_xn, 1)
                    dve.wait_ge(s_xn, b)
                    uv(b - 1)
            ln_norm(B - 1, xs, xn, B - 1).then_inc(s_xn, 1)
            dve.wait_ge(s_xn, B)
            uv(B - 1)

            dve.wait_ge(s_bias, 2)
            for b in range(B):
                dve.wait_ge(s_evac, N_V + 2 * DT * (b + 1))
                q, k = q_spec[b % 2], k_spec[b % 2]
                tt(q[:, :, 0], q[:, :, 0], qk_bias[:, 0, :], ALU.add)
                tt(k[:, :, 0], k[:, :, 0], qk_bias[:, 1, :], ALU.add)
                link(nc.vector.tensor_copy(nyq[:, :], k[:, :, P]))
                link(nc.vector.memset(k[:, :, P:P + 1], 0.0))
                if b >= 2:
                    dve.wait_ge(s_heads, b - 1)
                tt(prod[b % 2][0], q, k, ALU.mult).then_inc(s_prod, 1)
                dve.wait_ge(s_prod, 2 * b + 1)
                link(nc.vector.tensor_copy(k[:, :, 0], nyq[:, :]))
                for jt in range(DT):
                    qs = q[:, jt].rearrange("p (o r f) -> p o r f", o=2, r=2)
                    ks = k[:, jt].rearrange("p (o r f) -> p o r f", o=2, r=2)
                    ss = prod[b % 2][1][:, jt].rearrange("p (o r f) -> p o r f", o=2, r=2)
                    tt(ss[:, :, 0], qs[:, :, 1], ks[:, :, 0], ALU.mult)
                    ins = tt(ss[:, :, 1], qs[:, :, 0], ks[:, :, 1], ALU.mult)
                ins.then_inc(s_prod, 1)

            for b in range(B):
                ins = tt(v_spec[0:1, b, 0, :], v_spec[0:1, b, 0, :], v_bias[:, :], ALU.add)
            ins.then_inc(s_vb, 1)
            nc.vector.memset(corr[:, L:W_], PAD)
            nc.vector.memset(top3[0:NPAIR, :], PAD)
            dve.wait_ge(s_ceo, 1)
            tt(corr[:, 0:HALF], c_eo[:, 0:HALF], c_eo[:, HALF:L], ALU.add)
            link(tt(corr[:, HALF:L], c_eo[:, 0:HALF], c_eo[:, HALF:L], ALU.subtract))
            link(nc.vector.max(top8[0:NPAIR, :], corr[:, 0:L]))
            ts(t_neg[0:NPAIR, 0:1], top8[0:NPAIR, 0:1], -1.0, None, ALU.mult).then_inc(s_neg, 1)
            link(nc.vector.tensor_copy(top3[0:NPAIR, 0:TOPK], top8[0:NPAIR, 0:TOPK]))
            link(nc.vector.match_replace(rest, top3[0:NPAIR, :], corr, 3.0e38))
            tt(c_mask, rest[:, 0:L], corr[:, 0:L], ALU.not_equal)
            dve.wait_ge(s_exp, 2)
            link(nc.vector.tensor_reduce(t_exp[0:NPAIR, 3:4], t_exp[0:NPAIR, 0:TOPK], AX_X, ALU.add))
            link(nc.vector.reciprocal(t_neg[0:NPAIR, 1:2], t_exp[0:NPAIR, 3:4]))
            link(nc.vector.scalar_tensor_tensor(out=c_w, in0=c_mask, scalar=t_neg[0:NPAIR, 1:2], in1=c_exp,
                                                op0=ALU.mult, op1=ALU.mult))
            tt(w_uv[:, 0:HALF], c_w[:, 0:HALF], c_w[:, HALF:L], ALU.add).then_inc(s_wuv, 1)
            tt(w_uv[:, HALF:L], c_w[:, 0:HALF], c_w[:, HALF:L], ALU.subtract).then_inc(s_wuv, 1)
            dve.wait_ge(s_wse, 1)
            link(nc.vector.tensor_copy(w_re2[:, :, :],
                                       w_spec[:, :, :].rearrange("p (o r) n -> p o r n", o=2)[:, :, 0]))
            link(nc.vector.tensor_copy(w_re2[0:1, 0, :], w_spec[0:1, 1, :]))
            nc.vector.memset(w_spec[0:1, 1, :], 0.0).then_inc(s_wtab, 1)
            dve.wait_ge(s_wtab, 1)
            dve.wait_ge(s_vb, 1)

            def y_re(b):
                v = v_spec[:, b].rearrange("p (o r) (h e) -> p o r h e", o=2, e=HD)
                w = w_spec[:, :, b * H:(b + 1) * H].rearrange("p (o r) h -> p o r h", o=2)
                t1 = y_tmp[0].rearrange("p (o h e) -> p o h e", o=2, e=HD)
                t2 = y_tmp[1].rearrange("p (o h e) -> p o h e", o=2, e=HD)
                yre = y_spec[b % 2].rearrange("p (o r) (h e) -> p o r h e", o=2, e=HD)[:, :, 0]
                for o in range(2):
                    wre = w[:, o, 0, :].unsqueeze(2).broadcast_to([P, H, HD])
                    wim = w[:, o, 1, :].unsqueeze(2).broadcast_to([P, H, HD])
                    tt(t1[:, o], v[:, o, 0], wre, ALU.mult)
                    ins = tt(t2[:, o], v[:, o, 1], wim, ALU.mult)
                link(ins)
                if b >= 2:
                    dve.wait_ge(s_z, DT * (b - 1))
                for o in range(2):
                    ins = tt(yre[:, o], t1[:, o], t2[:, o], ALU.subtract)
                ins.then_inc(s_yre, 1)
                dve.wait_ge(s_yre, b + 1)

            def z_halves(b):
                for jt in range(DT):
                    n = b * DT + jt
                    dve.wait_ge(s_zc, n + 1)
                    z = z_tmp[n % 2]
                    tt(zt[:, jt, b, 0:HALF], z[:, 0:HALF], z[:, HALF:L], ALU.add).then_inc(s_zt, 1)
                    tt(zt[:, jt, b, HALF:L], z[:, 0:HALF], z[:, HALF:L], ALU.subtract).then_inc(s_zt, 1)

            def residual(b):
                for m in range(2):
                    n = 2 * b + m
                    dve.wait_ge(s_o, n + 1)
                    v = xs[:, 2 * n:2 * n + 2, :].rearrange("p t d -> p (t d)")
                    tt(v, v, ps[4 + n % 4][:, :], ALU.add).then_inc(s_x1, 1)

            y_re(0)
            for b in range(B):
                if b + 1 < B:
                    y_re(b + 1)
                z_halves(b)
            dve.wait_ge(s_xbo, TILES)
            for b in range(B):
                residual(b)
                dve.wait_ge(s_x1, 2 * (b + 1))
                ln_stats(b, xs, B + b)
                if b:
                    ln_norm(b - 1, xs, xn2, B + b - 1).then_inc(s_xn2, 1)
            ln_norm(B - 1, xs, xn2, 2 * B - 1).then_inc(s_xn2, 1)

            def te(a):
                return a.rearrange("p (t e) -> p t e", e=E)

            def over_e(a):
                return a.unsqueeze(2).broadcast_to([P, TILES, E])

            def over_t(a):
                return a.unsqueeze(1).broadcast_to([P, TILES, E])

            dve.wait_ge(s_lg, TILES // 2)
            link(tt(te(lg), te(ps[2][:, 0:TILES * E]), over_t(gb[:, :]), ALU.add))
            for src, mask, k in ((lg, m1, 0), (lg2, m2, 1)):
                link(nc.vector.tensor_reduce(r16[:, k, :], te(src), AX_X, ALU.max))
                link(tt(te(rtmp), te(src), over_e(r16[:, k, :]), ALU.is_equal))
                link(nc.vector.scalar_tensor_tensor(out=te(cand), in0=te(rtmp), scalar=-float(E),
                                                    in1=over_t(iota[:, 0:E]), op0=ALU.mult, op1=ALU.add))
                link(nc.vector.tensor_reduce(r16[:, 4 + k, :], te(cand), AX_X, ALU.min))
                link(tt(te(mask), te(cand), over_e(r16[:, 4 + k, :]), ALU.is_equal))
                if k == 0:
                    link(nc.vector.scalar_tensor_tensor(out=lg2, in0=mask, scalar=PAD, in1=lg,
                                                        op0=ALU.mult, op1=ALU.add))
            tt(r16[:, 2, :], r16[:, 1, :], r16[:, 0, :], ALU.subtract).then_inc(s_m12, 1)
            link(tt(rtmp, m1, m2, ALU.add))
            nc.vector.tensor_copy(cand, rtmp).then_inc(s_hot, 1)
            dve.wait_ge(s_rexp, 1)
            link(ts(r16[:, 4, :], r16[:, 3, :], 1.0, None, ALU.add))
            link(nc.vector.reciprocal(r16[:, 5, :], r16[:, 4, :]))
            link(tt(r16[:, 6, :], r16[:, 3, :], r16[:, 5, :], ALU.mult))
            tt(te(cum_a), te(m1), over_e(r16[:, 5, :]), ALU.mult)
            link(tt(te(cum_b), te(m2), over_e(r16[:, 6, :]), ALU.mult))
            dve.wait_ge(s_xn2, B)
            tt(xn2[:, :, D:ROW], te(cum_a), te(cum_b), ALU.add).then_inc(s_wcol, 1)
            dve.wait_ge(s_wcol, 1)
            dve.wait_ge(s_rank, 1)
            nc.vector.tensor_copy(rank, ps[3][:, 0:P])
            nc.vector.tensor_copy(tot, ps[3][:, P:2 * P])
            link(nc.vector.tensor_copy(cum_a, ps[3][:, P:2 * P]))
            src, dst = cum_a, cum_b
            sh = 1
            while sh < TILES:
                w = sh * E
                nc.vector.tensor_copy(dst[:, 0:w], src[:, 0:w])
                link(tt(dst[:, w:], src[:, w:], src[:, 0:TILES * E - w], ALU.add))
                src, dst = dst, src
                sh *= 2
            n_e = src[:, (TILES - 1) * E:TILES * E]
            nb3 = nbt[:, :].rearrange("p (e t) -> p e t", e=E)
            link(tt(nb3, n_e.unsqueeze(2).broadcast_to([P, E, TILES]),
                    thresholds.unsqueeze(1).broadcast_to([P, E, TILES]), ALU.is_gt))
            link(nc.vector.tensor_reduce(r8[:, 0, :], nb3, AX_X, ALU.add))
            a, o = r8[:, 1, :], r8[:, 2, :]
            link(nc.vector.tensor_copy(a, r8[:, 0, :]))
            sh = 1
            while sh < E:
                nc.vector.tensor_copy(o[:, 0:sh], a[:, 0:sh])
                link(tt(o[:, sh:], a[:, sh:], a[:, 0:E - sh], ALU.add))
                a, o = o, a
                sh *= 2
            ends = a
            eb3 = eb_t.rearrange("p (n e) -> p n e", e=E)
            tt(eb3, ends.unsqueeze(1).broadcast_to([P, BLOCKS_PAD, E]),
               iota[:, 0:BLOCKS_PAD].unsqueeze(2).broadcast_to([P, BLOCKS_PAD, E]), ALU.is_le)
            link(tt(r8[:, 3, :], ends, r8[:, 0, :], ALU.subtract))
            link(nc.vector.tensor_reduce(eb[:, :], eb3, AX_X, ALU.add))
            link(ts(eb[:, :], eb[:, :], float(E - 1), None, ALU.min))
            nc.vector.tensor_copy(eb_i[:, :], eb[:, :]).then_inc(s_slot, 1)
            ts(e_hot[:, :], eb[:, :], part_no, None, ALU.is_equal).then_inc(s_slot, 1)
            link(tt(rank, rank, src, ALU.add))
            link(tt(rank, rank, tot, ALU.subtract))
            link(nc.vector.scalar_tensor_tensor(out=te(rank), in0=over_t(r8[:, 3, :]), scalar=float(P),
                                                in1=te(rank), op0=ALU.mult, op1=ALU.add))
            for k, mask in enumerate((m1, m2)):
                link(tt(rtmp, mask, rank, ALU.mult))
                link(nc.vector.tensor_reduce(slot_f[:, k * TILES:(k + 1) * TILES], te(rtmp), AX_X, ALU.add))
            link(nc.vector.tensor_copy(slot_i[:, 0, :], slot_f[:, :]))
            nc.vector.tensor_single_scalar(slot_i[:, 1, :], slot_i[:, 0, :], 7, ALU.arith_shift_right)
            link(nc.vector.tensor_single_scalar(slot_i[:, 2, :], slot_i[:, 0, :], P - 1, ALU.bitwise_and))
            link(nc.vector.tensor_copy(slot_b[:, :, :], slot_i[:, 1:3, :]))
            NS = 2 * TILES
            link(tt(blk_hot[:, :, 0, :], slot_b[:, 0, :].unsqueeze(2).broadcast_to([P, NS, BLOCKS]),
                    iota[:, 0:BLOCKS].unsqueeze(1).broadcast_to([P, NS, BLOCKS]), ALU.is_equal))
            ts(blk_hot[:, :, 1, :], blk_hot[:, :, 0, :], part_no, None, ALU.mult)
            for k in range(2):
                sl = slice(k * TILES, (k + 1) * TILES)
                tt(blk_hot[:, sl, 2, :], blk_hot[:, sl, 0, :],
                   tile_no.unsqueeze(2).broadcast_to([P, TILES, BLOCKS]), ALU.mult)
            for k in range(2):
                sl = slice(k * TILES, (k + 1) * TILES)
                tt(pos_hot[:, sl, :], slot_b[:, 1, sl].unsqueeze(2).broadcast_to([P, TILES, P]),
                   iota.unsqueeze(1).broadcast_to([P, TILES, P]), ALU.is_equal).then_inc(s_slot, 1)
            nc.vector.memset(idx[:, :, BLOCKS:BLOCKS_PAD], 0)
            dve.wait_ge(s_idxp, 1)
            link(nc.vector.tensor_copy(idx_f[:, :, :].rearrange("p v s -> p (v s)"), ps[3][:, 0:3 * BLOCKS]))
            link(nc.vector.scalar_tensor_tensor(out=idx_f[:, 1, :], in0=idx_f[:, 2, :], scalar=float(P),
                                                in1=idx_f[:, 1, :], op0=ALU.mult, op1=ALU.add))
            nc.vector.tensor_copy(idx[:, 0, 0:BLOCKS], idx_f[:, 1, :])
            link(ts(idx_f[:, 0, :], idx_f[:, 0, :], -FAR, FAR, ALU.mult, ALU.add))
            link(tt(idx_f[:, 1, :], idx_f[:, 1, :], idx_f[:, 0, :], ALU.add))
            nc.vector.tensor_copy(idx[:, 1, 0:BLOCKS], idx_f[:, 1, :]).then_inc(s_idx, 1)

            def bias_hot(i, n):
                ts(bhot[n], ones[0:E, :], e_hot[0:E, bass.ds(i, 1)], None, ALU.mult).then_inc(s_bh, 1)

            def gate(i, n):
                dve.wait_ge(s_sil, i + 1)
                dve.wait_ge(s_h0, i + 1)
                tt(act_[n], sil[n], ps[2][:, :], ALU.mult).then_inc(s_act, 1)

            def act_out(i, n):
                dve.wait_ge(s_atp, i + 1)
                nc.vector.tensor_copy(act_t[n].rearrange("p c t -> p (c t)"), ps[5][:, :]).then_inc(s_atc, 1)

            bias_hot(0, 0)
            gate(0, 0)
            bias_hot(1, 1)
            with dve.Fori(0, BLOCKS - RING, RING) as i0:
                for n in range(RING):
                    i = i0 + n
                    act_out(i, n)
                    gate(i + 1, (n + 1) % RING)
                    bias_hot(i + 2, (n + 2) % RING)
            for n in range(RING):
                i = BLOCKS - RING + n
                act_out(i, n)
                if n < RING - 1:
                    gate(i + 1, (n + 1) % RING)
                if n < RING - 2:
                    bias_hot(i + 2, (n + 2) % RING)

        @block.tensor
        def _(pe):
            mm = nc.tensor.matmul
            fills = [0]

            def fill_start():
                if fills[0] >= 4:
                    pe.wait_ge(s_evac, fills[0] - 3)
                bank = ps[fills[0] % 4]
                fills[0] += 1
                return bank

            def spectra(uv, ready):
                for b in range(B):
                    pe.wait_ge(ready, 2 * (b + 1))
                    for dt in range(DT):
                        bank = fill_start()
                        for o in range(2):
                            for c in range(2):
                                ins = mm(bank[:, o * 256:(o + 1) * 256], uv[:, b, o, c, dt * P:(dt + 1) * P],
                                         fwd[:, o, c, :], start=(c == 0), stop=(c == 1))
                        ins.then_inc(s_fill, 1)

            pe.wait_ge(s_cst, 16)
            spectra(uv_c, s_uvc)
            spectra(uv_x, s_uvx)
            pe.wait_ge(s_watt, 16)
            pe.wait_ge(s_evac, N_C)
            for b in range(B):
                for o in range(2):
                    bank = fill_start()
                    for r in range(2):
                        k = 2 * o + r
                        for dt in range(DT):
                            ins = mm(bank[:, r * 256:(r + 1) * 256], c_spec[:, dt, b, k * P:(k + 1) * P],
                                     wv[:, dt, :], start=(dt == 0), stop=(dt == DT - 1))
                    ins.then_inc(s_fill, 1)

            def heads(b):
                for k in range(KINDS):
                    o, r = divmod(k, 2)
                    for jt in range(DT):
                        dst = ps[4][:, k * NPAIR + b * H + jt * 8:k * NPAIR + b * H + jt * 8 + 8]
                        pr = prod[b % 2][r][:, jt]
                        pe.wait_ge(s_prod, 2 * b + 1 + r)
                        for m in range(2):
                            sign = 8 * (r * m)
                            at = (2 * o + m) * P
                            ins = mm(dst, pr[:, at:at + P], head_sum[:, sign:sign + 8], start=(m == 0), stop=(m == 1))
                ins.then_inc(s_heads, 1)

            pe.wait_ge(s_evac, N_X)
            for b in range(B):
                for w, spec in ((wk, c_spec), (wq, x_spec)):
                    for jt in range(DT):
                        bank = fill_start()
                        for dt in range(DT):
                            ins = mm(bank[:, :], w[:, dt, jt * P:(jt + 1) * P], spec[:, dt, b, :],
                                     start=(dt == 0), stop=(dt == DT - 1))
                        ins.then_inc(s_fill, 1)
                if b:
                    heads(b - 1)
            heads(B - 1)
            pe.wait_ge(s_pt, 1)
            for o in range(2):
                for r in range(2):
                    ins = mm(ps[5][0:NPAIR, o * 256:(o + 1) * 256], pt[:, 2 * o + r, :], inv[:, 2 * o + r, :],
                             start=(r == 0), stop=(r == 1))
            ins.then_inc(s_corr, 1)
            pe.wait_ge(s_wuv, 2)
            for c in range(4):
                ins = nc.tensor.transpose(ps[6][:, c * NPAIR:(c + 1) * NPAIR], w_uv[:, c * P:(c + 1) * P],
                                          ident[0:NPAIR, 0:NPAIR])
            ins.then_inc(s_wtr, 1)
            pe.wait_ge(s_wt, 1)
            for k in range(KINDS):
                o, r = divmod(k, 2)
                for c in range(2):
                    ins = mm(ps[7][:, k * NPAIR:(k + 1) * NPAIR], fwd[:, o, c, r * P:(r + 1) * P],
                             w_t[:, 2 * o + c, :], start=(c == 0), stop=(c == 1))
            ins.then_inc(s_wsp, 1)

            def back(b):
                pe.wait_ge(s_yre, b + 1)
                pe.wait_ge(s_yim, b + 1)
                for jt in range(DT):
                    n = b * DT + jt
                    if n >= 4:
                        pe.wait_ge(s_zc, n - 3)
                    for o in range(2):
                        for r in range(2):
                            ins = mm(ps[n % 4][:, o * 256:(o + 1) * 256],
                                     y_spec[b % 2][:, 2 * o + r, jt * P:(jt + 1) * P], inv[:, 2 * o + r, :],
                                     start=(r == 0), stop=(r == 1))
                    ins.then_inc(s_z, 1)

            def out_proj(b):
                pe.wait_ge(s_zt, 2 * DT * (b + 1))
                for m in range(2):
                    n = 2 * b + m
                    if n == 3:
                        pe.wait_ge(s_wse, 1)
                    if n >= 4:
                        pe.wait_ge(s_x1, n - 3)
                    for t in range(2):
                        for jt in range(DT):
                            at = (2 * m + t) * P
                            ins = mm(ps[4 + n % 4][:, t * 256:(t + 1) * 256], zt[:, jt, b, at:at + P], wo[:, jt, :],
                                     start=(jt == 0), stop=(jt == DT - 1))
                    ins.then_inc(s_o, 1)

            for b in range(B):
                back(b)
                if b:
                    out_proj(b - 1)
            out_proj(B - 1)

            def gate_rows(n):
                pe.wait_ge(s_gtc, n + 1)
                for t in range(2):
                    for c in range(DT):
                        ins = mm(ps[2][:, (2 * n + t) * E:(2 * n + t + 1) * E], gate_t[:, n % 4, t * DT + c, :],
                                 gw[:, c, :], start=(c == 0), stop=(c == DT - 1))
                ins.then_inc(s_lg, 1)

            pe.wait_ge(s_zc, DT * B)
            pe.wait_ge(s_small, 16 * 6)
            for n in range(TILES // 2):
                pe.wait_ge(s_xn2, n // 2 + 1)
                if n >= 2:
                    pe.wait_ge(s_gtc, n - 1)
                for t in range(2):
                    for c in range(DT):
                        ins = nc.tensor.transpose(ps[n % 2][:, (t * DT + c) * P:(t * DT + c + 1) * P],
                                                  xn2[:, 2 * n + t, c * P:(c + 1) * P], ident)
                ins.then_inc(s_gt, 1)
                if n:
                    gate_rows(n - 1)
            gate_rows(TILES // 2 - 1)
            pe.wait_ge(s_hot, 1)
            mm(ps[3][:, 0:P], before, cand, start=True, stop=True)
            mm(ps[3][:, P:2 * P], ones, cand, start=True, stop=True).then_inc(s_rank, 1)
            NS = 2 * TILES
            for n in range(NS):
                if n % TILES == 0:
                    pe.wait_ge(s_slot, 3 + n // TILES)
                ins = mm(ps[3][:, 0:3 * BLOCKS], pos_hot[:, n, :], blk_hot[:, n].rearrange("p v s -> p (v s)"),
                         start=(n == 0), stop=(n == NS - 1))
            ins.then_inc(s_idxp, 1)

            def xt_in(i, n, turn):
                pe.wait_ge(s_xg[n], 16 * (turn + 1))
                if not (isinstance(i, int) and i == 0):
                    pe.wait_ge(s_xtc, i)
                for c in range(DT):
                    ins = nc.tensor.transpose(ps[4][:, c * P:(c + 1) * P], xg[n][:, c * P:(c + 1) * P], ident)
                ins.then_inc(s_xtp, 1)

            def hidden(half, n, bank, base, done):
                mm(bank[:, :], bhot[n], f_bias[:, half * FH:(half + 1) * FH], start=True, stop=False)
                for c in range(DT):
                    ins = mm(bank[:, :], xt[n][:, c, :], wts[:, bass.ds(base + (half * DT + c) * FH, FH)],
                             start=False, stop=(c == DT - 1))
                ins.then_inc(done, 1)

            def act_in(i, n):
                pe.wait_ge(s_act, i + 1)
                for c in range(FH // P):
                    ins = nc.tensor.transpose(ps[5][:, c * P:(c + 1) * P], act_[n][:, c * P:(c + 1) * P], ident)
                ins.then_inc(s_atp, 1)

            def y_in(i, n, base):
                pe.wait_ge(s_atc, i + 1)
                if not (isinstance(i, int) and i == 0):
                    pe.wait_ge(s_yb, i)
                mm(ps[6][:, 0:D], bhot[n], f_bias[:, 2 * FH:BCOLS], start=True, stop=False)
                for c in range(FH // P):
                    ins = mm(ps[6][:, 0:D], act_t[n][:, c, :], wts[:, bass.ds(base + W2_AT + c * D, D)],
                             start=False, stop=(c == FH // P - 1))
                ins.then_inc(s_yp, 1)

            def weights_at(i):
                return pe.value_load(eb_i[0:1, bass.ds(i, 1)], min_val=0, max_val=E - 1) * WCOLS

            def h1_part(i, n, base):
                pe.wait_ge(s_bh, i + 1)
                pe.wait_ge(s_xtc, i + 1)
                if not (isinstance(i, int) and i == 0):
                    pe.wait_ge(s_sil, i)
                hidden(1, n, ps[0], base, s_h1)

            def h0_part(i, n, base):
                if not (isinstance(i, int) and i == 0):
                    pe.wait_ge(s_act, i)
                hidden(0, n, ps[2], base, s_h0)

            pe.wait_ge(s_wffn, 16 * E)
            pe.wait_ge(s_slot, 2)
            xt_in(0, 0, 0)
            base = weights_at(0)
            h1_part(0, 0, base)
            h0_part(0, 0, base)
            xt_in(1, 1, 0)

            def step(i, n, turn, ahead, ahead2):
                m, k = (n + 1) % RING, (n + 2) % RING
                if ahead:
                    base = weights_at(i + 1)
                    h1_part(i + 1, m, base)
                act_in(i, n)
                if ahead:
                    h0_part(i + 1, m, base)
                if ahead2:
                    xt_in(i + 2, k, turn + (1 if n + 2 >= RING else 0))
                y_in(i, n, weights_at(i))

            for n in range(RING):
                step(n, n, 0, True, True)
            with pe.Fori(RING, BLOCKS - RING, RING) as i0:
                for n in range(RING):
                    i = i0 + n
                    m, k = (n + 1) % RING, (n + 2) % RING
                    base = weights_at(i + 1)
                    h1_part(i + 1, m, base)
                    act_in(i, n)
                    h0_part(i + 1, m, base)
                    pe.wait_ge(s_xg[k], 16 * ((i0 // RING) + (2 if n + 2 >= RING else 1)))
                    pe.wait_ge(s_xtc, i + 2)
                    for c in range(DT):
                        ins = nc.tensor.transpose(ps[4][:, c * P:(c + 1) * P], xg[k][:, c * P:(c + 1) * P], ident)
                    ins.then_inc(s_xtp, 1)
                    y_in(i, n, weights_at(i))
            for n in range(RING):
                step(BLOCKS - RING + n, n, BLOCKS // RING - 1, n < RING - 1, n < RING - 2)


_OUTS = [((B, L, D), "float32")]


def tables():
    import numpy as np
    c = np.zeros((P, C_END))
    f, t = np.arange(P), np.arange(HALF)
    fe, fo = 2 * f, 2 * f + 1
    fwd = np.zeros((2, HALF, 2, P))
    inv = np.zeros((KINDS, P, HALF))
    for o, fr in ((0, fe), (1, fo)):
        ang = 2 * np.pi * ((t[:, None] * fr[None, :]) % L) / L
        fwd[o, :, 0], fwd[o, :, 1] = np.cos(ang), -np.sin(ang)
        inv[2 * o], inv[2 * o + 1] = 2 * np.cos(ang.T) / L, -2 * np.sin(ang.T) / L
    alt = (-1.0) ** t
    fwd[0, :, 1, 0] = alt
    inv[0, 0] = 1.0 / L
    inv[1, 0] = alt / L
    c[:, C_FWD:C_INV] = fwd.reshape(2, 2, P, 2 * P).transpose(2, 0, 1, 3).reshape(P, -1)
    c[:, C_INV:C_ID] = inv.transpose(1, 0, 2).reshape(P, -1)
    c[:, C_ID:C_IND] = np.eye(P)
    c[:, C_IND:C_IND + 8] = np.arange(P)[:, None] // HD == np.arange(8)[None]
    c[:, C_IND + 8:C_TRI] = -c[:, C_IND:C_IND + 8]
    c[:, C_TRI:C_ONE] = np.arange(P)[:, None] < np.arange(P)[None]
    c[:, C_ONE:C_IOTA] = 1
    c[:, C_IOTA:C_PART] = np.arange(P)[None]
    c[:, C_PART] = np.arange(P)
    c[:, C_THR:C_TILE] = np.arange(TILES)[None] * P
    c[:, C_TILE:C_END] = np.arange(TILES)[None]
    return c.astype(np.float32)


def kernel(**inputs):
    import numpy as _np
    import concourse.bacc as _bacc
    from concourse import mybir as _mybir
    from concourse.bass_utils import run_bass_kernel_spmd as _run

    a = {k: _np.asarray(v) for k, v in inputs.items()}

    def rows(w):
        return w.T.reshape(-1, P, w.shape[0]).transpose(1, 0, 2).reshape(P, -1)

    ffn = _np.stack([_np.concatenate([rows(a["L0_ffn_w0"][e]), rows(a["L0_ffn_w1"][e]), rows(a["L0_ffn_w2"][e])], 1)
                     for e in range(E)])
    arrays = {
        "x": a["x"], "ctx": a["ctx_1024"],
        "wqkvo": _np.stack([rows(a[f"L0_xattn_W{n}"]) for n in "qkvo"]),
        "bqk": _np.stack([a["L0_xattn_bq"].reshape(DT, P), a["L0_xattn_bk"].reshape(DT, P)]).reshape(2 * DT, P).T,
        "bvo": _np.stack([a["L0_xattn_bv"], a["L0_xattn_bo"]]),
        "gate_w": a["L0_ffn_gate_w"].T, "gate_b": a["L0_ffn_gate_b"].reshape(1, E),
        "w_ffn": ffn,
        "b_ffn": _np.concatenate([a["L0_ffn_b0"], a["L0_ffn_b1"], a["L0_ffn_b2"]], 1),
        "const": tables(),
    }
    nc = _bacc.Bacc("TRN2", target_bir_lowering=False, num_devices=1)
    feed, args = {}, []
    for name, arr in arrays.items():
        arr = _np.ascontiguousarray(arr)
        feed[f"in_{name}"] = arr
        args.append(nc.dram_tensor(f"in_{name}", arr.shape, _mybir.dt.from_np(arr.dtype), kind="ExternalInput").ap())
    for i, (shape, dtype) in enumerate(_OUTS):
        args.append(nc.dram_tensor(f"out_{i}", shape, _mybir.dt.from_np(_np.dtype(dtype)), kind="ExternalOutput").ap())
    build(nc, *args)
    r = _run(nc, [feed], core_ids=[0])
    return r.results[0]["out_0"]
```

```python
from contextlib import ExitStack

import concourse.bass as bass
from concourse import mybir

P = 128
ALU = mybir.AluOpType
ACT = mybir.ActivationFunctionType
F32 = mybir.dt.float32
F32R = mybir.dt.float32r
BF16 = mybir.dt.bfloat16
I32 = mybir.dt.int32
U32 = mybir.dt.uint32
AX_X = mybir.AxisListType.X

B, L, D = 4, 512, 256
H, HD = 16, 16
E, FH = 8, 512
TOPK = 3
HALF = L // 2
DT = D // P
TILES = B * L // P
TPB = L // P
NPAIR = B * H
EPS = 1e-5
KINDS = 4

BLOCKS = (2 * B * L + E * (P - 1)) // P
RING = 3
BLOCKS_PAD = BLOCKS + 2
ROW = D + E
W01 = 2 * DT * FH
W2 = (FH // P) * D
BCOLS = 2 * FH + D
FAR = 4096.0
PAD = -3.0e38

C_FWD = 0
C_INV = C_FWD + 4 * 256
C_TABS = C_INV + KINDS * 256
C_ID = 0
C_IND = C_ID + P
C_TRI = C_IND + 16
C_ONE = C_TRI + P
C_IOTA = C_ONE + P
C_PART = C_IOTA + P
C_THR = C_PART + 1
C_TILE = C_THR + TILES
C_ROW = C_TILE + TILES
C_END = C_ROW + 1


def build(nc, x, ctx_in, wqkvo, bqk, bvo, gate_w, gate_b, w_01, w_2, b_ffn, tabs, const, out):
    with ExitStack() as ctx:
        def sem(name):
            return ctx.enter_context(nc.semaphore(name))

        KB16 = TILES * D * 4
        AT_WH, AT_WL, AT_W2 = 0, E * W01 * 4, 2 * E * W01 * 4
        AT_C, AT_F = AT_WH + E * W01 * 2, AT_WH + E * W01 * 2 + KB16
        AT_D, AT_E = AT_WL + E * W01 * 2, AT_WL + E * W01 * 2 + KB16
        AT_XS, AT_G = AT_W2, AT_W2 + KB16
        AT_B = AT_W2 + E * W2 * 4
        AT_TABS = AT_B + TILES * ROW * 4
        AT_WATT = AT_TABS + C_TABS * 4
        AT_RT = AT_WATT + 4 * DT * D * 4
        AT_BHOT = AT_RT + 12 * TILES * E * 4
        AT_CST = AT_BHOT + RING * P * 4
        AT_SMALL = (AT_CST + C_END * 4 + 31) // 32 * 32
        base = (nc.sbuf_base + 31) // 32 * 32

        def at(name, offset, shape, dt=F32):
            return nc.alloc_sbuf_tensor_at(name, shape, dt, offset=base + offset)

        small_at = [AT_SMALL]

        def small(name, shape, dt=F32):
            t = at(name, small_at[0], shape, dt)
            n = 4
            for m in shape[1:]:
                n *= m
            small_at[0] += (n + 31) // 32 * 32
            return t

        wh = at("wh", AT_WH, [P, E * W01], F32R)
        wl = at("wl", AT_WL, [P, E * W01], F32R)
        w2 = at("w2", AT_W2, [P, E * W2])
        tab = at("tab", AT_TABS, [P, C_TABS])
        cst = at("cst", AT_CST, [P, C_END])
        fwd = tab[:, C_FWD:C_INV].rearrange("p (o c n) -> p o c n", o=2, c=2)
        inv = tab[:, C_INV:C_TABS].rearrange("p (k n) -> p k n", k=KINDS)
        ident = cst[:, C_ID:C_IND]
        head_sum = cst[:, C_IND:C_TRI]
        before = cst[:, C_TRI:C_ONE]
        ones = cst[:, C_ONE:C_IOTA]
        iota = cst[:, C_IOTA:C_PART]
        part_no = cst[:, C_PART:C_THR]
        thresholds = cst[:, C_THR:C_TILE]
        tile_no = cst[:, C_TILE:C_ROW]
        bias_row = cst[:, C_ROW:C_END]

        w_att = at("w_att", AT_WATT, [P, 4, DT, D])
        wq, wk, wv, wo = (w_att[:, n] for n in range(4))
        gw = small("gw", [P, DT, E])
        gb = small("gb", [P, E])
        qk_bias = small("qk_bias", [P, 2, DT])
        v_bias = at("v_bias", AT_RT, [1, D])
        o_bias = at("o_bias", AT_RT + 1024, [P, D])
        pt = at("pt", AT_RT + 2048, [P, KINDS, NPAIR])
        w_t = at("w_t", AT_RT + 3072, [P, 4, NPAIR])
        w_spec = at("w_spec", AT_RT + 4096, [P, KINDS, NPAIR])
        w_re2 = at("w_re2", AT_RT + 5120, [P, 2, NPAIR])

        xs = at("xs", AT_XS, [P, TILES, D])
        buf_b = at("buf_b", AT_B, [P, TILES * ROW])
        buf_c = at("buf_c", AT_C, [P, TILES * D])
        buf_d = at("buf_d", AT_D, [P, TILES * D])
        buf_e = at("buf_e", AT_E, [P, TILES * D])
        buf_f = at("buf_f", AT_F, [P, TILES * D])
        buf_g = at("buf_g", AT_G, [P, TILES * D])
        HALF_E = DT * FH
        EARLY = 4
        raw_a = [at(f"raw_a{n}", AT_G + n * HALF_E * 4, [P, HALF_E])[:, :] for n in range(4)]
        raw_b = [at(f"raw_b{n}", AT_WATT + n * HALF_E * 4, [P, HALF_E])[:, :] for n in range(2)]

        xn = buf_b[:, 0:TILES * D].rearrange("p (t d) -> p t d", d=D)
        v_spec = buf_b[:, 0:B * KINDS * D].rearrange("p (b k j) -> p b k j", b=B, k=KINDS)
        xn2 = buf_b[:, :].rearrange("p (t r) -> p t r", r=ROW)
        cs = buf_c[:, :].rearrange("p (t d) -> p t d", d=D)
        x_spec = buf_c[:, :].rearrange("p (c b f) -> p c b f", c=DT, b=B)
        uv_x = buf_d[:, :].rearrange("p (b o c d) -> p b o c d", b=B, o=2, c=2)
        q_spec = [buf_d[:, n * 2048:n * 2048 + 1024].rearrange("p (c f) -> p c f", c=DT) for n in range(2)]
        k_spec = [buf_d[:, n * 2048 + 1024:n * 2048 + 2048].rearrange("p (c f) -> p c f", c=DT) for n in range(2)]
        y_tmp = [buf_d[:, n * 512:n * 512 + 512] for n in range(4)]
        c_spec = buf_e[:, :].rearrange("p (c b f) -> p c b f", c=DT, b=B)
        zt = buf_e[:, :].rearrange("p (c b t) -> p c b t", c=DT, b=B)
        uv_c = buf_f[:, :].rearrange("p (b o c d) -> p b o c d", b=B, o=2, c=2)
        same, cross = (buf_f[:, n * 1024:n * 1024 + 1024].rearrange("p (c f) -> p c f", c=DT) for n in range(2))
        prod = [buf_f[:, 2048 + n * 1024:3072 + n * 1024].rearrange("p (c k f) -> p c k f", c=DT, k=KINDS)
                for n in range(2)]
        y_spec = [buf_f[:, n * 1024:n * 1024 + 1024].rearrange("p (k j) -> p k j", k=KINDS) for n in range(2)]
        z_tmp = [buf_c[:, n * 512:n * 512 + 512] for n in range(4)]

        W_ = L + 8
        corr = buf_d[0:NPAIR, 0:W_]
        rest = buf_d[0:NPAIR, W_:2 * W_]
        c_eo = buf_d[0:NPAIR, 2 * W_:2 * W_ + L]
        c_exp = buf_d[0:NPAIR, 3 * W_:3 * W_ + L]
        c_mask = buf_d[0:NPAIR, 4 * W_:4 * W_ + L]
        c_w = buf_d[0:NPAIR, 5 * W_:5 * W_ + L]
        w_uv = buf_d[0:NPAIR, 6 * W_:6 * W_ + L]
        top8 = small("top8", [P, 8])
        top3 = small("top3", [P, 8])
        t_neg = small("t_neg", [P, 4])
        t_exp = small("t_exp", [P, 4])
        nyq = small("nyq", [P, DT])

        stats = small("stats", [P, TILES, 6])
        moments = small("moments", [P, TILES, 2])
        ln = small("ln", [P, 5, TILES])
        var, sd, rstd, nmr, ltmp = (ln[:, n] for n in range(5))
        warm = small("warm", [P, 1])

        rt = at("rt", AT_RT, [P, 12, TILES * E])
        lg, lg2, m1, m2, cum_a, cum_b, tot, rank, rtmp, cand = (rt[:, n] for n in range(10))
        r16 = small("r16", [P, 8, TILES])
        r8 = small("r8", [P, 6, E])
        nbt = small("nbt", [P, E * TILES])
        slot_f = small("slot_f", [P, 2 * TILES])
        slot_i = small("slot_i", [P, 3, 2 * TILES], I32)
        slot_b = small("slot_b", [P, 2, 2 * TILES])
        pos_hot = buf_g[:, 0:2 * TILES * P // 2].bitcast(BF16).rearrange("p (n s) -> p n s", s=P)
        blk_hot = buf_g[:, TILES * P:TILES * P + 2 * TILES * 3 * BLOCKS // 2].bitcast(BF16).rearrange(
            "p (n v s) -> p n v s", v=3, s=BLOCKS)
        eb_t = buf_g[:, 0:BLOCKS_PAD * E]
        eb = small("eb", [P, BLOCKS_PAD])
        eb_i = small("eb_i", [P, BLOCKS_PAD], I32)
        e_hot = small("e_hot", [P, BLOCKS_PAD])
        idx_f = small("idx_f", [P, 3, BLOCKS])
        idx = small("idx", [P, 2, BLOCKS_PAD], I32)
        gate_t = buf_g[:, 0:1024].rearrange("p (n c t) -> p n c t", n=2, c=DT * 2)
        bias_raw = buf_g[0:64, 1024:1024 + BCOLS]
        bias_hi = at("bias_hi", AT_G + 4 * (1024 + BCOLS), [64, BCOLS], F32R)

        gate_w_of = [small(f"gate_w_of{n}", [P, 1]) for n in range(RING)]
        ring = at("ring", AT_B, [P, RING * (FH + D + ROW) + FH])
        sil = [ring[:, n * FH:(n + 1) * FH] for n in range(RING)]
        act_t = ring[:, RING * FH:(RING + 1) * FH].rearrange("p (c t) -> p c t", c=FH // P)
        YB_AT = (RING + 1) * FH
        yb = [ring[:, YB_AT + n * D:YB_AT + (n + 1) * D] for n in range(RING)]
        XG_AT = YB_AT + RING * D
        xg = [ring[:, XG_AT + n * ROW:XG_AT + (n + 1) * ROW] for n in range(RING)]
        xt_hi = at("xt_hi", AT_TABS, [P, DT, P], F32R)
        xt_lo = at("xt_lo", AT_TABS + D * 4, [P, DT, P], F32R)
        f_bias = at("f_bias", AT_TABS + 2 * D * 4, [P, BCOLS], F32R)
        bhot = [at(f"bhot{n}", AT_BHOT + n * P * 4, [P, P], F32R) for n in range(RING)]

        xn2_dram = nc.dram_tensor("xn2_dram", [B * L, ROW], F32).ap()
        out_rows = out.rearrange("b l d -> (b l) d")
        ps = [ctx.enter_context(nc.psum_tensor(f"ps{n}", [P, 512], F32)) for n in range(8)]

        s_cst, s_watt, s_small, s_fb = sem("s_cst"), sem("s_watt"), sem("s_small"), sem("s_fb")
        s_x = [sem(f"s_xin{b}") for b in range(B)]
        s_c = [sem(f"s_cin{b}") for b in range(B)]
        s_uvc, s_uvx = sem("s_uvc"), sem("s_uvx")
        s_xn, s_xbo = sem("s_xn"), sem("s_xbo")
        s_var, s_sd = sem("s_var"), sem("s_sd")
        s_fill, s_evac = sem("s_fill"), sem("s_evac")
        s_bias = sem("s_bias")
        s_prod, s_heads, s_pt = sem("s_prod"), sem("s_heads"), sem("s_pt")
        s_corr, s_ceo = sem("s_corr"), sem("s_ceo")
        s_neg, s_exp, s_wuv = sem("s_neg"), sem("s_exp"), sem("s_wuv")
        s_wtr, s_wt, s_wsp, s_wse, s_wtab = sem("s_wtr"), sem("s_wt"), sem("s_wsp"), sem("s_wse"), sem("s_wtab")
        s_yre, s_yim, s_vb = sem("s_yre"), sem("s_yim"), sem("s_vb")
        s_z, s_zc, s_zt, s_o, s_x1 = sem("s_z"), sem("s_zc"), sem("s_zt"), sem("s_o"), sem("s_x1")
        s_xn2, s_gt, s_gtc, s_lg = sem("s_xn2"), sem("s_gt"), sem("s_gtc"), sem("s_lg")
        s_m12, s_rexp, s_hot, s_rank = sem("s_m12"), sem("s_rexp"), sem("s_hot"), sem("s_rank")
        s_wcol, s_rowd, s_outd = sem("s_wcol"), sem("s_rowd"), sem("s_outd")
        s_slot, s_idxp, s_idx = sem("s_slot"), sem("s_idxp"), sem("s_idx")
        v_step, p_step = sem("v_step"), sem("p_step")
        s_raw = [sem(f"s_raw{n}") for n in range(6)]
        s_hi, s_lo, s_w2, s_xth, s_gate = sem("s_hi"), sem("s_lo"), sem("s_w2"), sem("s_xth"), sem("s_gate")
        s_rstd, s_warm, s_used, s_zt2 = sem("s_rstd"), sem("s_warm"), sem("s_used"), sem("s_zt2")
        s_xg = [sem(f"s_xg{n}") for n in range(RING)]
        s_xtp, s_xtc, s_bh = sem("s_xtp"), sem("s_xtc"), sem("s_bh")
        s_h1, s_h0, s_sil, s_act = sem("s_h1"), sem("s_h0"), sem("s_sil"), sem("s_act")
        s_atp, s_atc, s_yp, s_yb = sem("s_atp"), sem("s_atc"), sem("s_yp"), sem("s_yb")
        s_sc = sem("s_sc")

        block = ctx.enter_context(nc.Block())

        def chain(eng, step):
            n = [0]

            def link(ins):
                n[0] += 1
                ins.then_inc(step, 1)
                eng.wait_ge(step, n[0])
            return link

        N_C, N_X, N_QK = DT * B, 2 * DT * B, 4 * DT * B
        FILLS = N_QK + 2 * B

        @block.sync
        def _(sp):
            cv = ctx_in.rearrange("b (a p) d -> b p a d", p=P)
            xv = x.rearrange("b (a p) d -> b p a d", p=P)
            for b in range(B):
                sp.dma_start(cs[:, b * TPB:(b + 1) * TPB, :], cv[b]).then_inc(s_c[b], 16)
                sp.dma_start(xs[:, b * TPB:(b + 1) * TPB, :], xv[b]).then_inc(s_x[b], 16)
            for n in range(2 * EARLY):
                if n >= 4:
                    sp.wait_ge(s_lo, n - 3)
                sp.dma_start(raw_a[n % 4], w_01[n // 2][:, (n % 2) * HALF_E:(n % 2 + 1) * HALF_E]).then_inc(
                    s_raw[n % 4], 16)
            sp.wait_ge(s_lo, 2 * EARLY)
            sp.dma_start(bias_raw[0:E, :], b_ffn).then_inc(s_fb, 16)
            sp.dma_start(bias_raw[32:32 + E, :], b_ffn).then_inc(s_fb, 16)
            for n in range(2 * EARLY, 2 * E):
                m = n - 2 * EARLY
                if m == 0:
                    sp.wait_ge(s_o, TILES // 2)
                if m == 2:
                    ov = out.rearrange("b (a p) d -> b p a d", p=P)
                    for b in range(B):
                        sp.wait_ge(s_x1, 2 * (b + 1))
                        sp.dma_start(ov[b], xs[:, b * TPB:(b + 1) * TPB, :]).then_inc(s_outd, 16)
                if m >= 2:
                    sp.wait_ge(s_lo, n - 1)
                sp.dma_start(raw_b[m % 2], w_01[n // 2][:, (n % 2) * HALF_E:(n % 2 + 1) * HALF_E]).then_inc(
                    s_raw[4 + m % 2], 16)
            sp.wait_ge(s_wcol, 1)
            sp.dma_start(xn2_dram.rearrange("(t p) r -> p t r", p=P), xn2).then_inc(s_rowd, 16)

        @block.gpsimd
        def _(pool):
            link = chain(pool, p_step)

            def split_lo(n, raw):
                pool.wait_ge(s_hi, n + 1)
                c = slice(n * HALF_E, (n + 1) * HALF_E)
                nc.gpsimd.tensor_tensor(wl[:, c], raw[:, :], wh[:, c].bitcast(F32), ALU.subtract).then_inc(s_lo, 1)

            for b in range(B):
                pool.wait_ge(s_c[b], 16)
                lo, hi = cs[:, b * TPB:b * TPB + 2, :], cs[:, b * TPB + 2:b * TPB + 4, :]
                nc.gpsimd.tensor_tensor(uv_c[:, b, 0], lo, hi, ALU.add).then_inc(s_uvc, 1)
                nc.gpsimd.tensor_tensor(uv_c[:, b, 1], lo, hi, ALU.subtract).then_inc(s_uvc, 1)
            pool.wait_ge(s_small, 16 * 5)
            nc.gpsimd.tensor_scalar(qk_bias[:, :, :], qk_bias[:, :, :], float(L), None, ALU.mult).then_inc(s_bias, 1)
            nc.gpsimd.tensor_scalar(v_bias[:, :], v_bias[:, :], float(L), None, ALU.mult).then_inc(s_bias, 1)
            for n in range(2 * EARLY):
                split_lo(n, raw_a[n % 4])
            pool.wait_ge(s_xn, B)
            for t in range(TILES):
                nc.gpsimd.tensor_tensor(xs[:, t, :], xs[:, t, :], o_bias[:, :], ALU.add).then_inc(s_xbo, 1)
            def y_im(b):
                v = v_spec[:, b].rearrange("p (o r) (h e) -> p o r h e", o=2, e=HD)
                w = w_spec[:, :, b * H:(b + 1) * H].rearrange("p (o r) h -> p o r h", o=2)
                wim = w[:, :, 1, :].unsqueeze(3).broadcast_to([P, 2, H, HD])
                wre2 = w_re2[:, :, b * H:(b + 1) * H].unsqueeze(3).broadcast_to([P, 2, H, HD])
                t3 = y_tmp[2].rearrange("p (o h e) -> p o h e", o=2, e=HD)
                t4 = y_tmp[3].rearrange("p (o h e) -> p o h e", o=2, e=HD)
                yim = y_spec[b % 2].rearrange("p (o r) (h e) -> p o r h e", o=2, e=HD)[:, :, 1]
                for o in range(2):
                    nc.gpsimd.tensor_tensor(t3[:, o], v[:, o, 0], wim[:, o], ALU.mult)
                    ins = nc.gpsimd.tensor_tensor(t4[:, o], v[:, o, 1], wre2[:, o], ALU.mult)
                link(ins)
                if b >= 2:
                    pool.wait_ge(s_z, DT * (b - 1))
                for o in range(2):
                    ins = nc.gpsimd.tensor_tensor(yim[:, o], t3[:, o], t4[:, o], ALU.add)
                ins.then_inc(s_yim, 1)
                pool.wait_ge(s_yim, b + 1)

            def z_second(b):
                for jt in range(DT):
                    n = b * DT + jt
                    pool.wait_ge(s_zc, n + 1)
                    z = z_tmp[n % 4]
                    nc.gpsimd.tensor_tensor(zt[:, jt, b, HALF:L], z[:, 0:HALF], z[:, HALF:L],
                                            ALU.subtract).then_inc(s_zt2, 1)

            pool.wait_ge(s_wtab, 1)
            pool.wait_ge(s_vb, 1)
            y_im(0)
            for b in range(B):
                if b + 1 < B:
                    y_im(b + 1)
                z_second(b)
            pool.wait_ge(s_o, TILES // 2)
            for n in range(2 * EARLY, 2 * E):
                split_lo(n, raw_b[n % 2])
            def gather(i):
                nc.gpsimd.indirect_dma_start(
                    out=xg[i % RING], out_offset=None, in_=xn2_dram,
                    in_offset=bass.IndirectOffsetOnAxis(idx[:, 0, i:i + 1], axis=0)).then_inc(s_xg[i % RING], 16)

            pool.wait_ge(s_idx, 1)
            pool.wait_ge(s_rowd, 16)
            for i in range(RING):
                gather(i)
            pool.wait_ge(s_gate, 1)
            gather(RING)
            pool.wait_ge(s_outd, 16 * B)
            for i in range(BLOCKS):
                if i + RING + 1 < BLOCKS:
                    pool.wait_ge(s_gate, i + 2)
                    gather(i + RING + 1)
                pool.wait_ge(s_yb, i + 1)
                if i:
                    pool.wait_ge(s_sc, 16 * i)
                nc.gpsimd.indirect_dma_start(
                    out=out_rows, out_offset=bass.IndirectOffsetOnAxis(idx[:, 1, i:i + 1], axis=0),
                    in_=yb[i % RING], in_offset=None, bounds_check=B * L - 1, oob_is_err=False,
                    compute_op=ALU.add).then_inc(s_sc, 16)
            pool.wait_ge(s_sc, 16 * BLOCKS)

        @block.scalar
        def _(act):
            act.dma_start(tab[:, :], tabs).then_inc(s_cst, 16)
            act.dma_start(cst[:, :], const).then_inc(s_cst, 16)
            act.dma_start(w_att[:, :, :, :].rearrange("p n c j -> p n (c j)"),
                          wqkvo.rearrange("n p m -> p n m")).then_inc(s_watt, 16)
            act.dma_start(qk_bias[:, :, :].rearrange("p n c -> p (n c)"), bqk).then_inc(s_small, 16)
            act.dma_start(v_bias[:, :], bvo[0:1, :]).then_inc(s_small, 16)
            act.dma_start(o_bias[:, :], bvo[1:2, :].broadcast_to([P, D])).then_inc(s_small, 16)
            act.dma_start(gw[:, :, :], gate_w.rearrange("(c p) e -> p c e", p=P)).then_inc(s_small, 16)
            act.dma_start(gb[:, :], gate_b.broadcast_to([P, E])).then_inc(s_small, 16)

            def copy(o, i):
                return nc.scalar.activation(o, i, ACT.Copy)

            def split_hi(n, raw, ready, count):
                act.wait_ge(ready, count)
                copy(wh[:, n * HALF_E:(n + 1) * HALF_E], raw[:, :]).then_inc(s_hi, 1)

            def root(n):
                act.wait_ge(s_var, n + 1)
                b = n % B
                nc.scalar.activation(sd[:, b * TPB:(b + 1) * TPB], var[:, b * TPB:(b + 1) * TPB],
                                     ACT.Sqrt).then_inc(s_sd, 1)

            def norm(n, src, dst, done):
                b = n % B
                act.wait_ge(s_rstd, n + 1)
                for t in range(b * TPB, (b + 1) * TPB):
                    ins = nc.scalar.activation(dst[:, t, 0:D], src[:, t, :], ACT.Identity,
                                               scale=rstd[:, t:t + 1], bias=nmr[:, t:t + 1])
                ins.then_inc(done, 1)

            def evacuate(n):
                act.wait_ge(s_fill, n + 1)
                bank = ps[n % 4]
                if n < N_C:
                    dst = c_spec[:, n % DT, n // DT, :]
                elif n < N_X:
                    m = n - N_C
                    if m == 0:
                        act.wait_ge(s_uvc, 2 * B)
                    dst = x_spec[:, m % DT, m // DT, :]
                elif n < N_QK:
                    b, m = divmod(n - N_X, 2 * DT)
                    if b == 0 and m == 0:
                        act.wait_ge(s_uvx, 2 * B)
                    if b >= 2 and m == 0:
                        act.wait_ge(s_used, b - 1)
                    dst = (k_spec, q_spec)[m // DT][b % 2][:, m % DT, :]
                else:
                    m = n - N_QK
                    dst = v_spec[:, m // 2, 2 * (m % 2):2 * (m % 2) + 2, :].rearrange("p k j -> p (k j)")
                copy(dst, bank[:, :]).then_inc(s_evac, 1)

            def warm_up(func, n):
                act.wait_ge(s_warm, n)
                nc.scalar.activation(warm[:, :], warm[:, :], func).then_inc(s_warm, 1)

            root(0)
            for b in range(B):
                if b + 1 < B:
                    evacuate(2 * b)
                    root(b + 1)
                norm(b, xs, xn, s_xn)
                if b + 1 < B:
                    evacuate(2 * b + 1)
            warm_up(ACT.Exp, 1)
            for n in range(N_C - 2, N_QK):
                evacuate(n)
                if n >= N_X and n % 2 == 0:
                    m = (n - N_X) // 2
                    split_hi(m, raw_a[m % 4], s_raw[m % 4], 16 * (m // 4 + 1))
            act.wait_ge(s_heads, B)
            copy(pt[:, :, :].rearrange("p k n -> p (k n)"), ps[4][:, 0:KINDS * NPAIR]).then_inc(s_pt, 1)
            act.wait_ge(s_corr, 1)
            nc.scalar.activation(c_eo, ps[5][0:NPAIR, :], ACT.Copy, scale=1.0 / HD).then_inc(s_ceo, 1)
            for n in range(N_QK, N_QK + 3):
                evacuate(n)
            act.wait_ge(s_neg, 1)
            nc.scalar.activation(c_exp, corr[:, 0:L], ACT.Exp, bias=t_neg[0:NPAIR, 0:1]).then_inc(s_exp, 1)
            nc.scalar.activation(t_exp[0:NPAIR, 0:TOPK], top8[0:NPAIR, 0:TOPK], ACT.Exp,
                                 bias=t_neg[0:NPAIR, 0:1]).then_inc(s_exp, 1)
            warm_up(ACT.Sqrt, 2)
            for n in range(N_QK + 3, FILLS):
                evacuate(n)
            act.wait_ge(s_wtr, 1)
            copy(w_t[:, :, :].rearrange("p c n -> p (c n)"), ps[6][:, 0:4 * NPAIR]).then_inc(s_wt, 1)
            act.wait_ge(s_wsp, 1)
            copy(w_spec[:, :, :].rearrange("p k n -> p (k n)"), ps[7][:, 0:KINDS * NPAIR]).then_inc(s_wse, 1)

            def z_out(b):
                for n in range(b * DT, (b + 1) * DT):
                    act.wait_ge(s_z, n + 1)
                    if n >= 4:
                        act.wait_ge(s_zt, n - 3)
                        act.wait_ge(s_zt2, n - 3)
                    copy(z_tmp[n % 4], ps[n % 4][:, :]).then_inc(s_zc, 1)

            def gate_out(b):
                for n in (2 * b, 2 * b + 1):
                    act.wait_ge(s_gt, n + 1)
                    if n == 0:
                        act.wait_ge(s_lo, 2 * EARLY)
                    if n >= 2:
                        act.wait_ge(s_lg, n - 1)
                    copy(gate_t[:, n % 2].rearrange("p c t -> p (c t)"), ps[n % 2][:, :]).then_inc(s_gtc, 1)

            for b in range(3):
                z_out(b)
            root(B)
            z_out(3)
            norm(B, xs, xn2, s_xn2)
            for b in range(1, B):
                root(B + b)
                if b > 1:
                    gate_out(b - 2)
                norm(B + b, xs, xn2, s_xn2)
            gate_out(B - 2)
            gate_out(B - 1)
            warm_up(ACT.Exp, 3)
            act.wait_ge(s_m12, 1)
            nc.scalar.activation(r16[:, 3, :], r16[:, 2, :], ACT.Exp).then_inc(s_rexp, 1)
            warm_up(ACT.Silu, 4)
            for n in range(2 * EARLY, 2 * E):
                split_hi(n, raw_b[n % 2], s_raw[4 + n % 2], 16 * ((n - 2 * EARLY) // 2 + 1))
            def xt_out(i, n):
                e = act.value_load(eb_i[0:1, bass.ds(i, 1)], min_val=0, max_val=E - 1)
                act.wait_ge(s_xtp, i + 1)
                copy(xt_hi[:, :, :].rearrange("p c t -> p (c t)"), ps[4][:, 0:D]).then_inc(s_xth, 1)
                if not (isinstance(i, int) and i < RING):
                    act.wait_ge(s_yb, i - RING + 1)
                copy(gate_w_of[n][:, :], xg[n][:, bass.ds(D + e, 1)]).then_inc(s_gate, 1)

            def silu(i, n):
                act.wait_ge(s_h1, i + 1)
                nc.scalar.activation(sil[n], ps[0][:, :], ACT.Silu).then_inc(s_sil, 1)

            def y_out(i, n):
                act.wait_ge(s_yp, i + 1)
                act.wait_ge(s_gate, i + 1)
                nc.scalar.activation(yb[n], ps[6][:, 0:D], ACT.Copy, scale=gate_w_of[n][:, :]).then_inc(s_yb, 1)

            act.wait_ge(s_outd, 16 * B)
            act.dma_start(w2[:, 0:E * W2 // 2].rearrange("p (e w) -> p e w", w=W2),
                          w_2[0:E // 2].rearrange("e p w -> p e w")).then_inc(s_w2, 16)
            act.wait_ge(s_idxp, 1)
            act.dma_start(w2[:, E * W2 // 2:].rearrange("p (e w) -> p e w", w=W2),
                          w_2[E // 2:E].rearrange("e p w -> p e w")).then_inc(s_w2, 16)
            act.wait_ge(s_slot, 2)
            xt_out(0, 0)
            silu(0, 0)
            xt_out(1, 1)

            def step(i, n, ahead=RING, reused=True):
                if ahead > 1:
                    silu(i + 1, (n + 1) % RING)
                if ahead > 2:
                    xt_out(i + 2, (n + 2) % RING)
                if reused:
                    act.wait_ge(s_sc, 16 * (i + 1 - RING))
                y_out(i, n)

            for n in range(RING):
                step(n, n, reused=False)
            with act.Fori(RING, BLOCKS - RING, RING) as i0:
                for n in range(RING):
                    step(i0 + n, n)
            for n in range(RING):
                step(BLOCKS - RING + n, n, ahead=RING - n)

        @block.vector
        def _(dve):
            link = chain(dve, v_step)
            tt, ts = nc.vector.tensor_tensor, nc.vector.tensor_scalar

            def ln_stats(b, src):
                for t in range(b * TPB, (b + 1) * TPB):
                    ins = nc.vector.bn_stats(stats[:, t, :], src[:, t, :])
                link(ins)
                for t in range(b * TPB, (b + 1) * TPB):
                    ins = nc.vector.bn_aggr(moments[:, t, :], stats[:, t, :])
                link(ins)
                c = slice(b * TPB, (b + 1) * TPB)
                ts(var[:, c], moments[:, c, 1], EPS, None, ALU.add).then_inc(s_var, 1)

            def ln_scale(n):
                b = n % B
                c = slice(b * TPB, (b + 1) * TPB)
                dve.wait_ge(s_sd, n + 1)
                link(nc.vector.reciprocal(rstd[:, c], sd[:, c]))
                link(tt(ltmp[:, c], rstd[:, c], rstd[:, c], ALU.mult))
                link(tt(ltmp[:, c], ltmp[:, c], var[:, c], ALU.mult))
                link(ts(ltmp[:, c], ltmp[:, c], -0.5, 1.5, ALU.mult, ALU.add))
                link(tt(rstd[:, c], rstd[:, c], ltmp[:, c], ALU.mult))
                nc.vector.scalar_tensor_tensor(out=nmr[:, c], in0=moments[:, c, 0], scalar=-1.0,
                                               in1=rstd[:, c], op0=ALU.mult, op1=ALU.mult).then_inc(s_rstd, 1)

            def uv(b):
                dve.wait_ge(s_xn, b + 1)
                lo, hi = xn[:, b * TPB:b * TPB + 2, :], xn[:, b * TPB + 2:b * TPB + 4, :]
                tt(uv_x[:, b, 0], lo, hi, ALU.add).then_inc(s_uvx, 1)
                tt(uv_x[:, b, 1], lo, hi, ALU.subtract).then_inc(s_uvx, 1)

            nc.vector.memset(warm[:, :], 0.0).then_inc(s_warm, 1)
            for b in range(B):
                dve.wait_ge(s_x[b], 16)
                ln_stats(b, xs)
                if b:
                    ln_scale(b - 1)
                if b > 1:
                    uv(b - 2)
            ln_scale(B - 1)
            uv(B - 2)
            uv(B - 1)

            dve.wait_ge(s_bias, 2)
            for b in range(B):
                dve.wait_ge(s_evac, N_X + 2 * DT * (b + 1))
                q, k = q_spec[b % 2], k_spec[b % 2]
                tt(q[:, :, 0], q[:, :, 0], qk_bias[:, 0, :], ALU.add)
                tt(k[:, :, 0], k[:, :, 0], qk_bias[:, 1, :], ALU.add)
                link(nc.vector.tensor_copy(nyq[:, :], k[:, :, P]))
                link(nc.vector.memset(k[:, :, P:P + 1], 0.0))
                link(tt(same, q, k, ALU.mult))
                link(nc.vector.tensor_copy(k[:, :, 0], nyq[:, :]))
                for jt in range(DT):
                    qs = q[:, jt].rearrange("p (o r f) -> p o r f", o=2, r=2)
                    ks = k[:, jt].rearrange("p (o r f) -> p o r f", o=2, r=2)
                    ss = cross[:, jt].rearrange("p (o r f) -> p o r f", o=2, r=2)
                    tt(ss[:, :, 0], qs[:, :, 1], ks[:, :, 0], ALU.mult)
                    ins = tt(ss[:, :, 1], qs[:, :, 0], ks[:, :, 1], ALU.mult)
                ins.then_inc(s_used, 1)
                if b >= 2:
                    dve.wait_ge(s_heads, b - 1)
                dve.wait_ge(s_used, b + 1)
                for src, r, op in ((same, 0, ALU.add), (cross, 1, ALU.subtract)):
                    v = src.rearrange("p c (o r f) -> p c o r f", o=2, r=2)
                    for jt in range(DT):
                        o = prod[b % 2][:, jt].rearrange("p (o r) f -> p o r f", o=2)
                        tt(o[:, :, r], v[:, jt, :, 0], v[:, jt, :, 1], op).then_inc(s_prod, 1)
                dve.wait_ge(s_prod, 2 * DT * (b + 1))

            nc.vector.memset(corr[:, L:W_], PAD)
            link(nc.vector.memset(top3[0:NPAIR, :], PAD))
            dve.wait_ge(s_ceo, 1)
            tt(corr[:, 0:HALF], c_eo[:, 0:HALF], c_eo[:, HALF:L], ALU.add)
            link(tt(corr[:, HALF:L], c_eo[:, 0:HALF], c_eo[:, HALF:L], ALU.subtract))
            link(nc.vector.max(top8[0:NPAIR, :], corr[:, 0:L]))
            ts(t_neg[0:NPAIR, 0:1], top8[0:NPAIR, 0:1], -1.0, None, ALU.mult).then_inc(s_neg, 1)
            link(nc.vector.tensor_copy(top3[0:NPAIR, 0:TOPK], top8[0:NPAIR, 0:TOPK]))
            link(nc.vector.match_replace(rest, top3[0:NPAIR, :], corr, 3.0e38))
            tt(c_mask, rest[:, 0:L], corr[:, 0:L], ALU.not_equal)
            dve.wait_ge(s_exp, 2)
            link(nc.vector.tensor_reduce(t_exp[0:NPAIR, 3:4], t_exp[0:NPAIR, 0:TOPK], AX_X, ALU.add))
            link(nc.vector.reciprocal(t_neg[0:NPAIR, 1:2], t_exp[0:NPAIR, 3:4]))
            link(nc.vector.scalar_tensor_tensor(out=c_w, in0=c_mask, scalar=t_neg[0:NPAIR, 1:2], in1=c_exp,
                                                op0=ALU.mult, op1=ALU.mult))
            tt(w_uv[:, 0:HALF], c_w[:, 0:HALF], c_w[:, HALF:L], ALU.add).then_inc(s_wuv, 1)
            tt(w_uv[:, HALF:L], c_w[:, 0:HALF], c_w[:, HALF:L], ALU.subtract).then_inc(s_wuv, 1)
            dve.wait_ge(s_evac, FILLS)
            for b in range(B):
                ins = tt(v_spec[0:1, b, 0, :], v_spec[0:1, b, 0, :], v_bias[:, :], ALU.add)
            ins.then_inc(s_vb, 1)
            dve.wait_ge(s_wse, 1)
            link(nc.vector.tensor_copy(w_re2[:, :, :],
                                       w_spec[:, :, :].rearrange("p (o r) n -> p o r n", o=2)[:, :, 0]))
            link(nc.vector.tensor_copy(w_re2[0:1, 0, :], w_spec[0:1, 1, :]))
            nc.vector.memset(w_spec[0:1, 1, :], 0.0).then_inc(s_wtab, 1)
            dve.wait_ge(s_wtab, 1)
            dve.wait_ge(s_vb, 1)

            def y_re(b):
                v = v_spec[:, b].rearrange("p (o r) (h e) -> p o r h e", o=2, e=HD)
                w = w_spec[:, :, b * H:(b + 1) * H].rearrange("p (o r) h -> p o r h", o=2)
                t1 = y_tmp[0].rearrange("p (o h e) -> p o h e", o=2, e=HD)
                t2 = y_tmp[1].rearrange("p (o h e) -> p o h e", o=2, e=HD)
                yre = y_spec[b % 2].rearrange("p (o r) (h e) -> p o r h e", o=2, e=HD)[:, :, 0]
                for o in range(2):
                    wre = w[:, o, 0, :].unsqueeze(2).broadcast_to([P, H, HD])
                    wim = w[:, o, 1, :].unsqueeze(2).broadcast_to([P, H, HD])
                    tt(t1[:, o], v[:, o, 0], wre, ALU.mult)
                    ins = tt(t2[:, o], v[:, o, 1], wim, ALU.mult)
                link(ins)
                if b >= 2:
                    dve.wait_ge(s_z, DT * (b - 1))
                for o in range(2):
                    ins = tt(yre[:, o], t1[:, o], t2[:, o], ALU.subtract)
                ins.then_inc(s_yre, 1)
                dve.wait_ge(s_yre, b + 1)

            def z_first(b):
                for jt in range(DT):
                    n = b * DT + jt
                    dve.wait_ge(s_zc, n + 1)
                    z = z_tmp[n % 4]
                    tt(zt[:, jt, b, 0:HALF], z[:, 0:HALF], z[:, HALF:L], ALU.add).then_inc(s_zt, 1)

            def residual(b):
                for m in range(2):
                    n = 2 * b + m
                    dve.wait_ge(s_o, n + 1)
                    v = xs[:, 2 * n:2 * n + 2, :].rearrange("p t d -> p (t d)")
                    tt(v, v, ps[4 + n % 4][:, :], ALU.add).then_inc(s_x1, 1)
                dve.wait_ge(s_x1, 2 * (b + 1))
                ln_stats(b, xs)

            dve.wait_ge(s_xbo, TILES)
            y_re(0)
            y_re(1)
            z_first(0)
            y_re(2)
            z_first(1)
            residual(0)
            y_re(3)
            z_first(2)
            ln_scale(B)
            residual(1)
            z_first(3)
            ln_scale(B + 1)
            residual(2)
            ln_scale(B + 2)
            residual(3)
            ln_scale(B + 3)

            dve.wait_ge(s_fb, 32)
            dve.wait_ge(s_z, DT * B)
            nc.vector.memset(f_bias[:, :].bitcast(F32), 0.0)
            for r in (0, 32):
                ins = nc.vector.tensor_copy(bias_hi[r:r + E, :], bias_raw[r:r + E, :])
            link(ins)
            nc.vector.tensor_copy(f_bias[0:E, :], bias_hi[0:E, :])
            link(tt(f_bias[32:32 + E, :], bias_raw[32:32 + E, :], bias_hi[32:32 + E, :].bitcast(F32), ALU.subtract))

            def te(a):
                return a.rearrange("p (t e) -> p t e", e=E)

            def over_e(a):
                return a.unsqueeze(2).broadcast_to([P, TILES, E])

            def over_t(a):
                return a.unsqueeze(1).broadcast_to([P, TILES, E])

            dve.wait_ge(s_lg, TILES // 2)
            link(tt(te(lg), te(ps[2][:, 0:TILES * E]), over_t(gb[:, :]), ALU.add))
            for src, mask, k in ((lg, m1, 0), (lg2, m2, 1)):
                link(nc.vector.tensor_reduce(r16[:, k, :], te(src), AX_X, ALU.max))
                link(tt(te(rtmp), te(src), over_e(r16[:, k, :]), ALU.is_equal))
                link(nc.vector.scalar_tensor_tensor(out=te(cand), in0=te(rtmp), scalar=-float(E),
                                                    in1=over_t(iota[:, 0:E]), op0=ALU.mult, op1=ALU.add))
                link(nc.vector.tensor_reduce(r16[:, 4 + k, :], te(cand), AX_X, ALU.min))
                link(tt(te(mask), te(cand), over_e(r16[:, 4 + k, :]), ALU.is_equal))
                if k == 0:
                    link(nc.vector.scalar_tensor_tensor(out=lg2, in0=mask, scalar=PAD, in1=lg,
                                                        op0=ALU.mult, op1=ALU.add))
            tt(r16[:, 2, :], r16[:, 1, :], r16[:, 0, :], ALU.subtract).then_inc(s_m12, 1)
            link(tt(rtmp, m1, m2, ALU.add))
            nc.vector.tensor_copy(cand, rtmp).then_inc(s_hot, 1)
            dve.wait_ge(s_rexp, 1)
            link(ts(r16[:, 4, :], r16[:, 3, :], 1.0, None, ALU.add))
            link(nc.vector.reciprocal(r16[:, 5, :], r16[:, 4, :]))
            link(tt(r16[:, 6, :], r16[:, 3, :], r16[:, 5, :], ALU.mult))
            tt(te(cum_a), te(m1), over_e(r16[:, 5, :]), ALU.mult)
            link(tt(te(cum_b), te(m2), over_e(r16[:, 6, :]), ALU.mult))
            dve.wait_ge(s_xn2, B)
            tt(xn2[:, :, D:ROW], te(cum_a), te(cum_b), ALU.add).then_inc(s_wcol, 1)
            dve.wait_ge(s_wcol, 1)
            dve.wait_ge(s_rank, 1)
            nc.vector.tensor_copy(rank, ps[3][:, 0:P])
            nc.vector.tensor_copy(tot, ps[3][:, P:2 * P])
            link(nc.vector.tensor_copy(cum_a, ps[3][:, P:2 * P]))
            src, dst = cum_a, cum_b
            sh = 1
            while sh < TILES:
                w = sh * E
                nc.vector.tensor_copy(dst[:, 0:w], src[:, 0:w])
                link(tt(dst[:, w:], src[:, w:], src[:, 0:TILES * E - w], ALU.add))
                src, dst = dst, src
                sh *= 2
            n_e = src[:, (TILES - 1) * E:TILES * E]
            nb3 = nbt[:, :].rearrange("p (e t) -> p e t", e=E)
            link(tt(nb3, n_e.unsqueeze(2).broadcast_to([P, E, TILES]),
                    thresholds.unsqueeze(1).broadcast_to([P, E, TILES]), ALU.is_gt))
            link(nc.vector.tensor_reduce(r8[:, 0, :], nb3, AX_X, ALU.add))
            a, o = r8[:, 1, :], r8[:, 2, :]
            link(nc.vector.tensor_copy(a, r8[:, 0, :]))
            sh = 1
            while sh < E:
                nc.vector.tensor_copy(o[:, 0:sh], a[:, 0:sh])
                link(tt(o[:, sh:], a[:, sh:], a[:, 0:E - sh], ALU.add))
                a, o = o, a
                sh *= 2
            ends = a
            eb3 = eb_t.rearrange("p (n e) -> p n e", e=E)
            tt(eb3, ends.unsqueeze(1).broadcast_to([P, BLOCKS_PAD, E]),
               iota[:, 0:BLOCKS_PAD].unsqueeze(2).broadcast_to([P, BLOCKS_PAD, E]), ALU.is_le)
            link(tt(r8[:, 3, :], ends, r8[:, 0, :], ALU.subtract))
            link(nc.vector.tensor_reduce(eb[:, :], eb3, AX_X, ALU.add))
            link(ts(eb[:, :], eb[:, :], float(E - 1), None, ALU.min))
            nc.vector.tensor_copy(eb_i[:, :], eb[:, :]).then_inc(s_slot, 1)
            ts(e_hot[:, :], eb[:, :], bias_row, None, ALU.is_equal).then_inc(s_slot, 1)
            link(tt(rank, rank, src, ALU.add))
            link(tt(rank, rank, tot, ALU.subtract))
            link(nc.vector.scalar_tensor_tensor(out=te(rank), in0=over_t(r8[:, 3, :]), scalar=float(P),
                                                in1=te(rank), op0=ALU.mult, op1=ALU.add))
            for k, mask in enumerate((m1, m2)):
                link(tt(rtmp, mask, rank, ALU.mult))
                link(nc.vector.tensor_reduce(slot_f[:, k * TILES:(k + 1) * TILES], te(rtmp), AX_X, ALU.add))
            link(nc.vector.tensor_copy(slot_i[:, 0, :], slot_f[:, :]))
            nc.vector.tensor_single_scalar(slot_i[:, 1, :], slot_i[:, 0, :], 7, ALU.arith_shift_right)
            link(nc.vector.tensor_single_scalar(slot_i[:, 2, :], slot_i[:, 0, :], P - 1, ALU.bitwise_and))
            link(nc.vector.tensor_copy(slot_b[:, :, :], slot_i[:, 1:3, :]))
            NS = 2 * TILES
            link(tt(blk_hot[:, :, 0, :], slot_b[:, 0, :].unsqueeze(2).broadcast_to([P, NS, BLOCKS]),
                    iota[:, 0:BLOCKS].unsqueeze(1).broadcast_to([P, NS, BLOCKS]), ALU.is_equal))
            ts(blk_hot[:, :, 1, :], blk_hot[:, :, 0, :], part_no, None, ALU.mult)
            for k in range(2):
                sl = slice(k * TILES, (k + 1) * TILES)
                tt(blk_hot[:, sl, 2, :], blk_hot[:, sl, 0, :],
                   tile_no.unsqueeze(2).broadcast_to([P, TILES, BLOCKS]), ALU.mult)
            for k in range(2):
                sl = slice(k * TILES, (k + 1) * TILES)
                tt(pos_hot[:, sl, :], slot_b[:, 1, sl].unsqueeze(2).broadcast_to([P, TILES, P]),
                   iota.unsqueeze(1).broadcast_to([P, TILES, P]), ALU.is_equal).then_inc(s_slot, 1)
            nc.vector.memset(idx[:, :, BLOCKS:BLOCKS_PAD], 0)
            dve.wait_ge(s_idxp, 1)
            link(nc.vector.tensor_copy(idx_f[:, :, :].rearrange("p v s -> p (v s)"), ps[3][:, 0:3 * BLOCKS]))
            link(nc.vector.scalar_tensor_tensor(out=idx_f[:, 1, :], in0=idx_f[:, 2, :], scalar=float(P),
                                                in1=idx_f[:, 1, :], op0=ALU.mult, op1=ALU.add))
            nc.vector.tensor_copy(idx[:, 0, 0:BLOCKS], idx_f[:, 1, :])
            link(ts(idx_f[:, 0, :], idx_f[:, 0, :], -FAR, FAR, ALU.mult, ALU.add))
            link(tt(idx_f[:, 1, :], idx_f[:, 1, :], idx_f[:, 0, :], ALU.add))
            nc.vector.tensor_copy(idx[:, 1, 0:BLOCKS], idx_f[:, 1, :]).then_inc(s_idx, 1)

            def bias_hot(i, n):
                ts(bhot[n][:, :], ones, e_hot[:, bass.ds(i, 1)], None, ALU.mult).then_inc(s_bh, 1)

            def xt_low(i):
                dve.wait_ge(s_xth, i + 1)
                tt(xt_lo[:, :, :].rearrange("p c t -> p (c t)"), ps[4][:, 0:D],
                   xt_hi[:, :, :].rearrange("p c t -> p (c t)").bitcast(F32), ALU.subtract).then_inc(s_xtc, 1)

            def gate(i, n):
                dve.wait_ge(s_sil, i + 1)
                dve.wait_ge(s_h0, i + 1)
                tt(sil[n], sil[n], ps[2][:, :], ALU.mult).then_inc(s_act, 1)

            def act_out(i, n):
                dve.wait_ge(s_atp, i + 1)
                nc.vector.tensor_copy(act_t.rearrange("p c t -> p (c t)"), ps[5][:, :]).then_inc(s_atc, 1)

            bias_hot(0, 0)
            xt_low(0)
            gate(0, 0)
            bias_hot(1, 1)
            xt_low(1)

            def step(i, n, ahead=RING):
                act_out(i, n)
                if ahead > 1:
                    gate(i + 1, (n + 1) % RING)
                if ahead > 2:
                    bias_hot(i + 2, (n + 2) % RING)
                    xt_low(i + 2)

            with dve.Fori(0, BLOCKS - RING, RING) as i0:
                for n in range(RING):
                    step(i0 + n, n)
            for n in range(RING):
                step(BLOCKS - RING + n, n, ahead=RING - n)

        @block.tensor
        def _(pe):
            mm = nc.tensor.matmul
            fills = [0]

            def fill_start():
                if fills[0] >= 4:
                    pe.wait_ge(s_evac, fills[0] - 3)
                bank = ps[fills[0] % 4]
                fills[0] += 1
                return bank

            def spectra(uv, ready):
                for b in range(B):
                    pe.wait_ge(ready, 2 * (b + 1))
                    for dt in range(DT):
                        bank = fill_start()
                        for o in range(2):
                            for c in range(2):
                                ins = mm(bank[:, o * 256:(o + 1) * 256], uv[:, b, o, c, dt * P:(dt + 1) * P],
                                         fwd[:, o, c, :], start=(c == 0), stop=(c == 1))
                        ins.then_inc(s_fill, 1)

            pe.wait_ge(s_cst, 32)
            spectra(uv_c, s_uvc)
            spectra(uv_x, s_uvx)
            pe.wait_ge(s_watt, 16)

            def heads(b):
                for r in range(2):
                    for jt in range(DT):
                        pe.wait_ge(s_prod, 2 * DT * b + DT * r + jt + 1)
                        for o in range(2):
                            k = 2 * o + r
                            dst = ps[4][:, k * NPAIR + b * H + jt * 8:k * NPAIR + b * H + jt * 8 + 8]
                            ins = mm(dst, prod[b % 2][:, jt, k, :], head_sum[:, 0:8], start=True, stop=True)
                ins.then_inc(s_heads, 1)

            pe.wait_ge(s_evac, N_X)
            for b in range(B):
                for w, spec in ((wk, c_spec), (wq, x_spec)):
                    for jt in range(DT):
                        bank = fill_start()
                        for dt in range(DT):
                            ins = mm(bank[:, :], w[:, dt, jt * P:(jt + 1) * P], spec[:, dt, b, :],
                                     start=(dt == 0), stop=(dt == DT - 1))
                        ins.then_inc(s_fill, 1)
                if b:
                    heads(b - 1)
            heads(B - 1)
            pe.wait_ge(s_pt, 1)
            for o in range(2):
                for r in range(2):
                    ins = mm(ps[5][0:NPAIR, o * 256:(o + 1) * 256], pt[:, 2 * o + r, :], inv[:, 2 * o + r, :],
                             start=(r == 0), stop=(r == 1))
            ins.then_inc(s_corr, 1)
            for b in range(B):
                for o in range(2):
                    bank = fill_start()
                    for r in range(2):
                        k = 2 * o + r
                        for dt in range(DT):
                            ins = mm(bank[:, r * 256:(r + 1) * 256], c_spec[:, dt, b, k * P:(k + 1) * P],
                                     wv[:, dt, :], start=(dt == 0), stop=(dt == DT - 1))
                    ins.then_inc(s_fill, 1)
            pe.wait_ge(s_wuv, 2)
            for c in range(4):
                ins = nc.tensor.transpose(ps[6][:, c * NPAIR:(c + 1) * NPAIR], w_uv[:, c * P:(c + 1) * P],
                                          ident[0:NPAIR, 0:NPAIR])
            ins.then_inc(s_wtr, 1)
            pe.wait_ge(s_wt, 1)
            for k in range(KINDS):
                o, r = divmod(k, 2)
                for c in range(2):
                    ins = mm(ps[7][:, k * NPAIR:(k + 1) * NPAIR], fwd[:, o, c, r * P:(r + 1) * P],
                             w_t[:, 2 * o + c, :], start=(c == 0), stop=(c == 1))
            ins.then_inc(s_wsp, 1)

            def back(b):
                pe.wait_ge(s_yre, b + 1)
                pe.wait_ge(s_yim, b + 1)
                for jt in range(DT):
                    n = b * DT + jt
                    if n >= 4:
                        pe.wait_ge(s_zc, n - 3)
                    for o in range(2):
                        for r in range(2):
                            ins = mm(ps[n % 4][:, o * 256:(o + 1) * 256],
                                     y_spec[b % 2][:, 2 * o + r, jt * P:(jt + 1) * P], inv[:, 2 * o + r, :],
                                     start=(r == 0), stop=(r == 1))
                    ins.then_inc(s_z, 1)

            def out_proj(b):
                pe.wait_ge(s_zt, DT * (b + 1))
                pe.wait_ge(s_zt2, DT * (b + 1))
                for m in range(2):
                    n = 2 * b + m
                    if n == 3:
                        pe.wait_ge(s_wse, 1)
                    if n >= 4:
                        pe.wait_ge(s_x1, n - 3)
                    for t in range(2):
                        for jt in range(DT):
                            at = (2 * m + t) * P
                            ins = mm(ps[4 + n % 4][:, t * 256:(t + 1) * 256], zt[:, jt, b, at:at + P], wo[:, jt, :],
                                     start=(jt == 0), stop=(jt == DT - 1))
                    ins.then_inc(s_o, 1)

            for b in range(B):
                back(b)
                if b:
                    out_proj(b - 1)
            out_proj(B - 1)

            def gate_rows(n):
                pe.wait_ge(s_gtc, n + 1)
                for t in range(2):
                    for c in range(DT):
                        ins = mm(ps[2][:, (2 * n + t) * E:(2 * n + t + 1) * E], gate_t[:, n % 2, t * DT + c, :],
                                 gw[:, c, :], start=(c == 0), stop=(c == DT - 1))
                ins.then_inc(s_lg, 1)

            pe.wait_ge(s_zc, DT * B)
            pe.wait_ge(s_small, 16 * 5)
            for n in range(TILES // 2):
                pe.wait_ge(s_xn2, n // 2 + 1)
                if n >= 2:
                    pe.wait_ge(s_gtc, n - 1)
                for t in range(2):
                    for c in range(DT):
                        ins = nc.tensor.transpose(ps[n % 2][:, (t * DT + c) * P:(t * DT + c + 1) * P],
                                                  xn2[:, 2 * n + t, c * P:(c + 1) * P], ident)
                ins.then_inc(s_gt, 1)
                if n:
                    gate_rows(n - 1)
            gate_rows(TILES // 2 - 1)
            pe.wait_ge(s_hot, 1)
            mm(ps[3][:, 0:P], before, cand, start=True, stop=True)
            mm(ps[3][:, P:2 * P], ones, cand, start=True, stop=True).then_inc(s_rank, 1)
            NS = 2 * TILES
            for n in range(NS):
                if n % TILES == 0:
                    pe.wait_ge(s_slot, 3 + n // TILES)
                ins = mm(ps[3][:, 0:3 * BLOCKS], pos_hot[:, n, :], blk_hot[:, n].rearrange("p v s -> p (v s)"),
                         start=(n == 0), stop=(n == NS - 1))
            ins.then_inc(s_idxp, 1)

            def xt_in(i, n, rows):
                pe.wait_ge(s_xg[n], rows)
                if not (isinstance(i, int) and i == 0):
                    pe.wait_ge(s_xtc, i)
                for c in range(DT):
                    ins = nc.tensor.transpose(ps[4][:, c * P:(c + 1) * P], xg[n][:, c * P:(c + 1) * P], ident)
                ins.then_inc(s_xtp, 1)

            def hidden(half, n, bank, e, done):
                mm(bank[:, :], bhot[n][:, :], f_bias[:, half * FH:(half + 1) * FH], start=True, stop=False)
                for c in range(DT):
                    cols = bass.ds(e * W01 + (half * DT + c) * FH, FH)
                    mm(bank[:, :], xt_hi[:, c, :], wl[:, cols], start=False, stop=False)
                    mm(bank[:, :], xt_hi[:, c, :], wh[:, cols], start=False, stop=False)
                    ins = mm(bank[:, :], xt_lo[:, c, :], wh[:, cols], start=False, stop=(c == DT - 1))
                ins.then_inc(done, 1)

            def act_in(i, n):
                pe.wait_ge(s_act, i + 1)
                for c in range(FH // P):
                    ins = nc.tensor.transpose(ps[5][:, c * P:(c + 1) * P], sil[n][:, c * P:(c + 1) * P], ident)
                ins.then_inc(s_atp, 1)

            def y_in(i, n, e):
                if not (isinstance(i, int) and i == 0):
                    pe.wait_ge(s_yb, i)
                mm(ps[6][:, 0:D], bhot[n][:, :], f_bias[:, 2 * FH:BCOLS], start=True, stop=False)
                pe.wait_ge(s_atc, i + 1)
                for c in range(FH // P):
                    ins = mm(ps[6][:, 0:D], act_t[:, c, :], w2[:, bass.ds(e * W2 + c * D, D)],
                             start=False, stop=(c == FH // P - 1))
                ins.then_inc(s_yp, 1)

            def expert(i):
                return pe.value_load(eb_i[0:1, bass.ds(i, 1)], min_val=0, max_val=E - 1)

            def h1_part(i, n, e):
                pe.wait_ge(s_bh, i + 1)
                pe.wait_ge(s_xtc, i + 1)
                if not (isinstance(i, int) and i == 0):
                    pe.wait_ge(s_sil, i)
                hidden(1, n, ps[0], e, s_h1)

            def h0_part(i, n, e):
                if not (isinstance(i, int) and i == 0):
                    pe.wait_ge(s_act, i)
                hidden(0, n, ps[2], e, s_h0)

            def step(i, n, turn, ahead=RING):
                m, k = (n + 1) % RING, (n + 2) % RING
                if ahead > 1:
                    e = expert(i + 1)
                    h1_part(i + 1, m, e)
                act_in(i, n)
                if ahead > 1:
                    h0_part(i + 1, m, e)
                if ahead > 2:
                    xt_in(i + 2, k, 16 * (turn + (2 if n + 2 >= RING else 1)))
                y_in(i, n, expert(i))

            pe.wait_ge(s_lo, 2 * E)
            pe.wait_ge(s_slot, 2)
            xt_in(0, 0, 16)
            e = expert(0)
            h1_part(0, 0, e)
            h0_part(0, 0, e)
            xt_in(1, 1, 16)
            pe.wait_ge(s_w2, 32)
            for n in range(RING):
                step(n, n, 0)
            with pe.Fori(RING, BLOCKS - RING, RING) as i0:
                for n in range(RING):
                    step(i0 + n, n, i0 // RING)
            for n in range(RING):
                step(BLOCKS - RING + n, n, BLOCKS // RING - 1, ahead=RING - n)


_OUTS = [((B, L, D), "float32")]


def tables():
    import numpy as np
    c, tab = np.zeros((P, C_END)), np.zeros((P, C_TABS))
    f, t = np.arange(P), np.arange(HALF)
    fe, fo = 2 * f, 2 * f + 1
    fwd = np.zeros((2, HALF, 2, P))
    inv = np.zeros((KINDS, P, HALF))
    for o, fr in ((0, fe), (1, fo)):
        ang = 2 * np.pi * ((t[:, None] * fr[None, :]) % L) / L
        fwd[o, :, 0], fwd[o, :, 1] = np.cos(ang), -np.sin(ang)
        inv[2 * o], inv[2 * o + 1] = 2 * np.cos(ang.T) / L, -2 * np.sin(ang.T) / L
    alt = (-1.0) ** t
    fwd[0, :, 1, 0] = alt
    inv[0, 0] = 1.0 / L
    inv[1, 0] = alt / L
    tab[:, C_FWD:C_INV] = fwd.reshape(2, 2, P, 2 * P).transpose(2, 0, 1, 3).reshape(P, -1)
    tab[:, C_INV:C_TABS] = inv.transpose(1, 0, 2).reshape(P, -1)
    c[:, C_ID:C_IND] = np.eye(P)
    c[:, C_IND:C_IND + 8] = np.arange(P)[:, None] // HD == np.arange(8)[None]
    c[:, C_IND + 8:C_TRI] = -c[:, C_IND:C_IND + 8]
    c[:, C_TRI:C_ONE] = np.arange(P)[:, None] < np.arange(P)[None]
    c[:, C_ONE:C_IOTA] = 1
    c[:, C_IOTA:C_PART] = np.arange(P)[None]
    c[:, C_PART] = np.arange(P)
    c[:, C_THR:C_TILE] = np.arange(TILES)[None] * P
    c[:, C_TILE:C_ROW] = np.arange(TILES)[None]
    c[:, C_ROW] = -1
    c[0:E, C_ROW] = c[32:32 + E, C_ROW] = np.arange(E)
    return tab.astype(np.float32), c.astype(np.float32)


def kernel(**inputs):
    import numpy as _np
    import concourse.bacc as _bacc
    from concourse import mybir as _mybir
    from concourse.bass_utils import run_bass_kernel_spmd as _run

    a = {k: _np.asarray(v) for k, v in inputs.items()}

    def rows(w):
        return w.T.reshape(-1, P, w.shape[0]).transpose(1, 0, 2).reshape(P, -1)

    tabs, const = tables()
    arrays = {
        "x": a["x"], "ctx": a["ctx_1024"],
        "wqkvo": _np.stack([rows(a[f"L0_xattn_W{n}"]) for n in "qkvo"]),
        "bqk": _np.stack([a["L0_xattn_bq"].reshape(DT, P), a["L0_xattn_bk"].reshape(DT, P)]).reshape(2 * DT, P).T,
        "bvo": _np.stack([a["L0_xattn_bv"], a["L0_xattn_bo"]]),
        "gate_w": a["L0_ffn_gate_w"].T, "gate_b": a["L0_ffn_gate_b"].reshape(1, E),
        "w_01": _np.stack([_np.concatenate([rows(a["L0_ffn_w0"][e]), rows(a["L0_ffn_w1"][e])], 1) for e in range(E)]),
        "w_2": _np.stack([rows(a["L0_ffn_w2"][e]) for e in range(E)]),
        "b_ffn": _np.concatenate([a["L0_ffn_b0"], a["L0_ffn_b1"], a["L0_ffn_b2"]], 1),
        "tabs": tabs, "const": const,
    }
    nc = _bacc.Bacc("TRN2", target_bir_lowering=False, num_devices=1)
    feed, args = {}, []
    for name, arr in arrays.items():
        arr = _np.ascontiguousarray(arr)
        feed[f"in_{name}"] = arr
        args.append(nc.dram_tensor(f"in_{name}", arr.shape, _mybir.dt.from_np(arr.dtype), kind="ExternalInput").ap())
    for i, (shape, dtype) in enumerate(_OUTS):
        args.append(nc.dram_tensor(f"out_{i}", shape, _mybir.dt.from_np(_np.dtype(dtype)), kind="ExternalOutput").ap())
    build(nc, *args)
    r = _run(nc, [feed], core_ids=[0])
    return r.results[0]["out_0"]
```

```python
from contextlib import ExitStack

import concourse.bass as bass
from concourse import mybir

P = 128
ALU = mybir.AluOpType
ACT = mybir.ActivationFunctionType
F32 = mybir.dt.float32
F32R = mybir.dt.float32r
BF16 = mybir.dt.bfloat16
I32 = mybir.dt.int32
AX_X = mybir.AxisListType.X

B, L, D = 4, 512, 256
H, HD = 16, 16
E, FH = 8, 512
TOPK = 3
HALF = L // 2
DT = D // P
TILES = B * L // P
TPB = L // P
NPAIR = B * H
EPS = 1e-5
KINDS = 4

BLOCKS = (2 * B * L + E * (P - 1)) // P
RING = 3
BLOCKS_PAD = BLOCKS + 2
W01 = 2 * DT * FH
W2 = (FH // P) * D
BCOLS = 2 * FH + D
FAR = 4096.0
HOTS = 3
PAD = -3.0e38

C_FWD = 0
C_INV = C_FWD + 3 * 256
C_TABS = C_INV + KINDS * 256
C_ID = 0
C_IND = C_ID + P
C_TRI = C_IND + 16
C_ONE = C_TRI + P
C_IOTA = C_ONE + P
C_PART = C_IOTA + P
C_THR = C_PART + 1
C_TILE = C_THR + TILES
C_ROW = C_TILE + TILES
C_END = C_ROW + 1


def build(nc, x, ctx_in, wqkvo, bqk, bvo, gate_w, gate_b, w_01, w_2, b_ffn, tabs, const, out):
    with ExitStack() as ctx:
        def sem(name):
            return ctx.enter_context(nc.semaphore(name))

        KB16 = TILES * D * 4
        AT_WH, AT_WL, AT_W2 = 0, E * W01 * 4, 2 * E * W01 * 4
        AT_C, AT_F = AT_WH + E * W01 * 2, AT_WH + E * W01 * 2 + KB16
        AT_D, AT_E = AT_WL + E * W01 * 2, AT_WL + E * W01 * 2 + KB16
        AT_XS, AT_G = AT_W2, AT_W2 + KB16
        AT_B = AT_W2 + E * W2 * 4
        AT_TABS = AT_B + TILES * D * 4
        AT_WATT = AT_TABS + C_TABS * 4
        AT_RT = AT_WATT + 4 * DT * D * 4
        AT_BHOT = AT_RT + 12 * TILES * E * 4
        AT_CST = AT_BHOT + RING * P * 4
        AT_SMALL = (AT_CST + C_END * 4 + 31) // 32 * 32
        base = (nc.sbuf_base + 31) // 32 * 32

        def at(name, offset, shape, dt=F32):
            return nc.alloc_sbuf_tensor_at(name, shape, dt, offset=base + offset)

        small_at = [AT_SMALL]

        def small(name, shape, dt=F32):
            t = at(name, small_at[0], shape, dt)
            n = 4
            for m in shape[1:]:
                n *= m
            small_at[0] += (n + 31) // 32 * 32
            return t

        wh = at("wh", AT_WH, [P, E * W01], F32R)
        wl = at("wl", AT_WL, [P, E * W01], F32R)
        w2 = at("w2", AT_W2, [P, E * W2])
        tab = at("tab", AT_TABS, [P, C_TABS])
        cst = at("cst", AT_CST, [P, C_END])
        fwd_even = tab[:, C_FWD:C_FWD + 256].rearrange("p (r g f) -> p r g f", r=2, g=2)
        fwd_odd = tab[:, C_FWD + 256:C_INV].rearrange("p (c n) -> p c n", c=2)
        inv = tab[:, C_INV:C_TABS].rearrange("p (k n) -> p k n", k=KINDS)
        ident = cst[:, C_ID:C_IND]
        head_sum = cst[:, C_IND:C_TRI]
        before = cst[:, C_TRI:C_ONE]
        ones = cst[:, C_ONE:C_IOTA]
        iota = cst[:, C_IOTA:C_PART]
        part_no = cst[:, C_PART:C_THR]
        thresholds = cst[:, C_THR:C_TILE]
        tile_no = cst[:, C_TILE:C_ROW]
        bias_row = cst[:, C_ROW:C_END]

        w_att = at("w_att", AT_WATT, [P, 4, DT, D])
        wq, wk, wv, wo = (w_att[:, n] for n in range(4))
        gw = small("gw", [P, DT, E])
        gb = small("gb", [P, E])
        qk_bias = small("qk_bias", [P, 2, DT])
        v_bias = at("v_bias", AT_RT, [1, D])
        o_bias = at("o_bias", AT_RT + 1024, [P, D])
        pt = at("pt", AT_RT + 2048, [P, KINDS, NPAIR])
        w_t = at("w_t", AT_RT + 3072, [P, 4, NPAIR])
        w_spec = at("w_spec", AT_RT + 4096, [P, KINDS, NPAIR])
        w_re2 = at("w_re2", AT_RT + 5120, [P, 2, NPAIR])

        xs = at("xs", AT_XS, [P, TILES, D])
        buf_b = at("buf_b", AT_B, [P, TILES * D])
        buf_c = at("buf_c", AT_C, [P, TILES * D])
        buf_d = at("buf_d", AT_D, [P, TILES * D])
        buf_e = at("buf_e", AT_E, [P, TILES * D])
        buf_f = at("buf_f", AT_F, [P, TILES * D])
        buf_g = at("buf_g", AT_G, [P, TILES * D])
        raw_w = at("raw_w", AT_WL, [P, E * W01])
        HALF_E = DT * FH
        EARLY = 4
        EXPERTS = [*range(EARLY), 5, 4, 6, 7]
        HALVES = [2 * e + m for e in EXPERTS for m in range(2)]
        N_EARLY, N_MID = 2 * EARLY, 2 * EARLY + 2

        xn = buf_b[:, 0:TILES * D].rearrange("p (t d) -> p t d", d=D)
        v_spec = buf_b[:, 0:B * KINDS * D].rearrange("p (b k j) -> p b k j", b=B, k=KINDS)
        xn2 = xn
        cs = buf_c[:, :].rearrange("p (t d) -> p t d", d=D)
        x_spec = buf_c[:, :].rearrange("p (c b f) -> p c b f", c=DT, b=B)
        uv_x = buf_d[:, :].rearrange("p (b o c d) -> p b o c d", b=B, o=2, c=2)
        q_spec = [buf_d[:, b * 1024:(b + 1) * 1024].rearrange("p (c f) -> p c f", c=DT) for b in range(B)]
        k_spec = [buf_g[:, b * 1024:(b + 1) * 1024].rearrange("p (c f) -> p c f", c=DT) for b in range(B)]
        y_tmp = [buf_d[:, n * 512:n * 512 + 512] for n in range(4)]
        c_spec = buf_e[:, :].rearrange("p (c b f) -> p c b f", c=DT, b=B)
        zt = buf_e[:, :].rearrange("p (c b t) -> p c b t", c=DT, b=B)
        uv_c = buf_f[:, :].rearrange("p (b o c d) -> p b o c d", b=B, o=2, c=2)
        same, cross = (buf_f[:, n * 1024:n * 1024 + 1024].rearrange("p (c f) -> p c f", c=DT) for n in range(2))
        prod = [buf_f[:, 2048 + n * 1024:3072 + n * 1024].rearrange("p (c k f) -> p c k f", c=DT, k=KINDS)
                for n in range(2)]
        y_spec = [buf_f[:, n * 1024:n * 1024 + 1024].rearrange("p (k j) -> p k j", k=KINDS) for n in range(2)]
        z_tmp = [buf_c[:, n * 512:n * 512 + 512] for n in range(4)]

        W_ = L + 8
        corr = buf_f[0:NPAIR, 0:W_]
        rest = buf_f[0:NPAIR, W_:2 * W_]
        c_eo = buf_f[0:NPAIR, 2 * W_:2 * W_ + L]
        c_exp = buf_f[0:NPAIR, 3 * W_:3 * W_ + L]
        c_mask = buf_f[0:NPAIR, 4 * W_:4 * W_ + L]
        c_w = buf_f[0:NPAIR, 5 * W_:5 * W_ + L]
        w_uv = buf_f[0:NPAIR, 6 * W_:6 * W_ + L]
        top8 = small("top8", [P, 8])
        top3 = small("top3", [P, 8])
        t_neg = small("t_neg", [P, 4])
        t_exp = small("t_exp", [P, 4])
        nyq = small("nyq", [P, DT])

        stats = small("stats", [P, TILES, 6])
        moments = small("moments", [P, TILES, 2])
        ln = small("ln", [P, 5, TILES])
        var, sd, rstd, nmr, ltmp = (ln[:, n] for n in range(5))
        warm = small("warm", [P, 1])
        zeros = buf_e[:, 0:512]

        rt = at("rt", AT_RT, [P, 10, TILES * E])
        lg, lg2, m1, m2 = (rt[:, n] for n in range(4))
        rank, rtmp, cand = (rt[:, n] for n in range(7, 10))
        up_to = at("up_to", AT_RT + 4 * TILES * E * 4, [P, 2 * E, E])
        up_to_sum = at("up_to_sum", AT_RT + 10 * TILES * E * 4, [P, 2 * E, E])
        r16 = small("r16", [P, 9, TILES])
        r8 = small("r8", [P, 3, E])
        nbt = small("nbt", [P, E * TILES])
        slot_f = small("slot_f", [P, 2 * TILES])
        slot_i = small("slot_i", [P, 3, 2 * TILES], I32)
        slot_b = small("slot_b", [P, 2, 2 * TILES])
        iota_b = small("iota_b", [P, P], BF16)
        tile_b = small("tile_b", [P, TILES], BF16)
        before_b = at("before_b", AT_BHOT + 2 * P * 4, [P, P], BF16)
        ones_b = at("ones_b", AT_BHOT + 2 * P * 4 + P * 2, [P, P], BF16)
        pairs_b = small("pairs_b", [P, TILES * E], BF16)
        g_part = small("g_part", [P, HOTS, 2 * TILES], BF16)
        g_rest = small("g_rest", [P, 2 * TILES])
        NS = 2 * TILES
        hots = at("hots", AT_B, [P, NS * (P + HOTS * BLOCKS)], BF16)
        pos_hot = hots[:, 0:NS * P].rearrange("p (n s) -> p n s", s=P)
        blk_hot = hots[:, NS * P:].rearrange("p (v n s) -> p v n s", v=HOTS, s=BLOCKS)
        eb_t = at("eb_t", AT_WATT + 4096, [P, BLOCKS_PAD * E])[:, :]
        eb = small("eb", [P, BLOCKS_PAD])
        eb_i = small("eb_i", [P, BLOCKS_PAD], I32)
        e_hot = small("e_hot", [P, BLOCKS_PAD])
        idx_f = small("idx_f", [P, 3, BLOCKS])
        slot_gate = small("slot_gate", [P, BLOCKS_PAD])
        idx = small("idx", [P, 2, BLOCKS_PAD], I32)
        GT = 4
        gate_t = at("gate_t", AT_WATT, [P, GT * 2 * D])[:, :].rearrange("p (n c t) -> p n c t", n=GT, c=DT * 2)
        bias_raw = buf_g[0:64, 1024:1024 + BCOLS]
        bias_hi = at("bias_hi", AT_G + 4 * (1024 + BCOLS), [64, BCOLS], F32R)

        sil = [at(f"sil{n}", o, [P, FH])[:, :]
               for n, o in enumerate((AT_RT + W2 * 4, AT_WATT + 2 * RING * D * 4, AT_B))]
        act_hi = at("act_hi", AT_B + RING * FH * 4, [P, FH // P, P], F32R)
        act_lo = at("act_lo", AT_B + (RING + 1) * FH * 4, [P, FH // P, P], F32R)
        w2_hi = at("w2_hi", AT_B + (RING + 2) * FH * 4, [P, W2], F32R)
        w2_lo = at("w2_lo", AT_RT, [P, W2], F32R)
        w2_hi_last = at("w2_hi_last", AT_B + FH * 4, [P, W2], F32R)
        w2_lo_last = wl[:, 0:W2]
        xg = [at(f"xg{n}", AT_WATT + n * D * 4, [P, D])[:, :] for n in range(RING)]
        yb = [at(f"yb{n}", AT_WATT + (RING + n) * D * 4, [P, D])[:, :] for n in range(RING)]
        f_bias = at("f_bias", AT_TABS, [P, BCOLS], F32R)
        xt_hi = at("xt_hi", AT_TABS + BCOLS * 4, [P, DT, P], F32R)
        xt_lo = at("xt_lo", AT_TABS + (BCOLS + D) * 4, [P, DT, P], F32R)
        bhot = [at(f"bhot{n}", AT_BHOT + n * P * 4, [P, P], F32R) for n in range(RING)]

        xn2_dram = nc.dram_tensor("xn2_dram", [B * L, D], F32).ap()
        out_rows = out.rearrange("b l d -> (b l) d")
        ps = [ctx.enter_context(nc.psum_tensor(f"ps{n}", [P, 512], F32)) for n in range(8)]

        lg_t = [at(f"lg_t{n}", o, [E, 2 * P])[:, :] for n, o in enumerate((AT_RT + 10 * TILES * E * 4, AT_BHOT))]
        gate_bank = [ps[n] for n in (0, 1, 3, 4)]
        logit_bank = [ps[2], ps[5]]

        s_fzero, s_xn2v = sem("s_fzero"), sem("s_xn2v")
        s_fwd, s_inv, s_zeros = sem("s_fwd"), sem("s_inv"), sem("s_zeros")
        s_wk = sem("s_wk")
        s_cst, s_watt, s_small, s_fb = sem("s_cst"), sem("s_watt"), sem("s_small"), sem("s_fb")
        s_x = [sem(f"s_xin{b}") for b in range(B)]
        s_c = [sem(f"s_cin{b}") for b in range(B)]
        s_uvc0, s_uvc, s_uvd, s_uvx = sem("s_uvc0"), sem("s_uvc"), sem("s_uvd"), sem("s_uvx")
        s_xn, s_xbo = sem("s_xn"), sem("s_xbo")
        s_var, s_sd = sem("s_var"), sem("s_sd")
        s_fill, s_evac = sem("s_fill"), sem("s_evac")
        s_bias = sem("s_bias")
        s_prod, s_heads, s_pt = sem("s_prod"), sem("s_heads"), sem("s_pt")
        s_corr, s_ceo = sem("s_corr"), sem("s_ceo")
        s_neg, s_exp, s_wuv = sem("s_neg"), sem("s_exp"), sem("s_wuv")
        s_wtr, s_wt, s_wsp, s_wse, s_wtab = sem("s_wtr"), sem("s_wt"), sem("s_wsp"), sem("s_wse"), sem("s_wtab")
        s_yre, s_yim, s_yim0, s_vb = sem("s_yre"), sem("s_yim"), sem("s_yim0"), sem("s_vb")
        s_z, s_zc, s_zt, s_o, s_x1 = sem("s_z"), sem("s_zc"), sem("s_zt"), sem("s_o"), sem("s_x1")
        s_xn2, s_gt, s_gtc, s_lg = sem("s_xn2"), sem("s_gt"), sem("s_gtc"), sem("s_lg")
        s_lgr, s_lgc, s_bhi = sem("s_lgr"), sem("s_lgc"), sem("s_bhi")
        s_m12, s_rexp, s_hot = sem("s_m12"), sem("s_rexp"), sem("s_hot")
        s_count, s_rank = sem("s_count"), sem("s_rank")
        s_rowd, s_outd = sem("s_rowd"), sem("s_outd")
        s_slot, s_idxp, s_idx = sem("s_slot"), sem("s_idxp"), sem("s_idx")
        s_fbias, s_blkhot, s_tilehot, s_parthot = sem("s_fbias"), sem("s_blkhot"), sem("s_tilehot"), sem("s_parthot")
        s_eb = sem("s_eb")
        s_gparts, s_gp, s_gs = sem("s_gparts"), sem("s_gp"), sem("s_gs")
        s_gsplit, s_gpool = sem("s_gsplit"), sem("s_gpool")
        v_step, p_step = sem("v_step"), sem("p_step")
        s_raw = [sem(f"s_raw{e}") for e in range(E)]
        s_hi, s_lo, s_w2, s_xth = sem("s_hi"), sem("s_lo"), sem("s_w2"), sem("s_xth")
        s_rstd, s_warm, s_used, s_zt2 = sem("s_rstd"), sem("s_warm"), sem("s_used"), sem("s_zt2")
        s_xg = [sem(f"s_xg{n}") for n in range(RING)]
        s_xtp, s_xtc, s_bh = sem("s_xtp"), sem("s_xtc"), sem("s_bh")
        s_h1, s_h0, s_sil, s_act = sem("s_h1"), sem("s_h0"), sem("s_sil"), sem("s_act")
        s_w2h, s_w2l, s_atp, s_ath, s_atl = sem("s_w2h"), sem("s_w2l"), sem("s_atp"), sem("s_ath"), sem("s_atl")
        s_yp, s_yb = sem("s_yp"), sem("s_yb")
        s_sc = sem("s_sc")

        block = ctx.enter_context(nc.Block())

        def chain(eng, step):
            n = [0]

            def link(ins):
                n[0] += 1
                ins.then_inc(step, 1)
                eng.wait_ge(step, n[0])
            return link

        def fold(op, link, src, uv, b, done):
            lo, hi = src[:, b * TPB:b * TPB + 2, :], src[:, b * TPB + 2:b * TPB + 4, :]
            op(uv[:, b, 1], lo, hi, ALU.subtract).then_inc(done, 1)
            link(op(lo, lo, hi, ALU.add))
            op(uv[:, b, 0, 0], lo[:, 0], lo[:, 1], ALU.add).then_inc(done, 1)
            op(uv[:, b, 0, 1], lo[:, 0], lo[:, 1], ALU.subtract).then_inc(done, 1)

        ORDER = [("c", b, i) for b in range(B) for i in range(DT)]
        STEPS = [("k", 0), ("x", 0), ("k", 1), ("x", 1), ("q", 0), ("k", 2), ("x", 2), ("q", 1),
                 ("x", 3), ("q", 2), ("k", 3), ("q", 3)]
        ORDER += [(kind, b, i) for kind, b in STEPS for i in range(DT)]
        N_QK = len(ORDER)
        ORDER += [("v", b, i) for b in range(B) for i in range(2)]

        def until(kind, b):
            return max(n for n, f in enumerate(ORDER) if f[:2] == (kind, b)) + 1

        V_AHEAD = 2
        FILL_BANKS = [ps[n] for n in (0, 1, 2, 3, 6, 7)]
        NB = len(FILL_BANKS)
        FILLS = len(ORDER)

        @block.sync
        def _(sp):
            cv = ctx_in.rearrange("b (a p) d -> b p a d", p=P)
            xv = x.rearrange("b (a p) d -> b p a d", p=P)
            for b in range(B + 1):
                if b < B:
                    sp.dma_start(cs[:, b * TPB:(b + 1) * TPB, :], cv[b]).then_inc(s_c[b], 16)
                if b:
                    sp.dma_start(xs[:, (b - 1) * TPB:b * TPB, :], xv[b - 1]).then_inc(s_x[b - 1], 16)
                if b == 2:
                    sp.dma_start(w_att[:, 1].rearrange("p c j -> p (c j)"), wqkvo[1]).then_inc(s_wk, 16)
            sp.dma_start(w_att[:, 0].rearrange("p c j -> p (c j)"), wqkvo[0]).then_inc(s_watt, 16)
            sp.dma_start(w_att[:, 2:4].rearrange("p n c j -> p n (c j)"),
                         wqkvo[2:4].rearrange("n p m -> p n m")).then_inc(s_watt, 16)
            sp.dma_start(cst[:, :], const).then_inc(s_cst, 16)
            sp.dma_start(tab[:, C_INV:C_TABS], tabs[:, C_INV:C_TABS]).then_inc(s_inv, 16)
            def raw_in(e):
                sp.dma_start(raw_w[:, e * W01:(e + 1) * W01], w_01[e]).then_inc(s_raw[e], 16)

            for e in EXPERTS[0:EARLY]:
                raw_in(e)
            sp.wait_ge(s_used, B)
            raw_in(EXPERTS[EARLY])
            sp.dma_start(bias_raw[0:E, :], b_ffn).then_inc(s_fb, 16)
            sp.dma_start(bias_raw[32:32 + E, :], b_ffn).then_inc(s_fb, 16)
            sp.wait_ge(s_yre, 2 * B)
            sp.wait_ge(s_yim, 2 * B - 1)
            raw_in(EXPERTS[EARLY + 1])
            sp.wait_ge(s_o, TILES // 2)
            raw_in(EXPERTS[EARLY + 2])
            raw_in(EXPERTS[EARLY + 3])
            ov = out.rearrange("b (a p) d -> b p a d", p=P)
            nv = xn2_dram.rearrange("(b a p) d -> b p a d", b=B, p=P)
            for b in range(B + 1):
                if b < B:
                    sp.wait_ge(s_x1, 2 * (b + 1))
                    sp.dma_start(ov[b], xs[:, b * TPB:(b + 1) * TPB, :]).then_inc(s_outd, 16)
                if b:
                    sp.wait_ge(s_xn2, b)
                    if b == B:
                        sp.wait_ge(s_xn2v, 1)
                    sp.dma_start(nv[b - 1], xn2[:, (b - 1) * TPB:b * TPB, :]).then_inc(s_rowd, 16)
            sp.wait_ge(s_outd, 16 * B)
            sp.dma_start(w2[:, 0:E * W2 // 2].rearrange("p (e w) -> p e w", w=W2),
                         w_2[0:E // 2].rearrange("e p w -> p e w")).then_inc(s_w2, 16)
            sp.wait_ge(s_fbias, 2)
            sp.dma_start(w2[:, E * W2 // 2:].rearrange("p (e w) -> p e w", w=W2),
                         w_2[E // 2:E].rearrange("e p w -> p e w")).then_inc(s_w2, 16)

        @block.gpsimd
        def _(pool):
            link = chain(pool, p_step)

            def split_lo(k):
                pool.wait_ge(s_hi, k + 1)
                c = slice(HALVES[k] * HALF_E, (HALVES[k] + 1) * HALF_E)
                nc.gpsimd.tensor_tensor(wl[:, c], raw_w[:, c], wh[:, c].bitcast(F32), ALU.subtract).then_inc(s_lo, 1)

            for b in range(2, B):
                pool.wait_ge(s_c[b], 16)
                total = uv_x[:, b, 1]
                add = nc.gpsimd.tensor_tensor
                link(add(total, cs[:, b * TPB:b * TPB + 2, :], cs[:, b * TPB + 2:b * TPB + 4, :], ALU.add))
                add(uv_c[:, b, 0, 0], total[:, 0], total[:, 1], ALU.add).then_inc(s_uvc, 1)
                add(uv_c[:, b, 0, 1], total[:, 0], total[:, 1], ALU.subtract).then_inc(s_uvc, 1)
            pool.wait_ge(s_small, 16 * 5)
            nc.gpsimd.tensor_scalar(qk_bias[:, :, :], qk_bias[:, :, :], float(L), None, ALU.mult).then_inc(s_bias, 1)
            nc.gpsimd.tensor_scalar(v_bias[:, :], v_bias[:, :], float(L), None, ALU.mult).then_inc(s_bias, 1)
            for k in range(N_EARLY):
                split_lo(k)
            pool.wait_ge(s_xn, B)
            for t in range(TILES):
                nc.gpsimd.tensor_tensor(xs[:, t, :], xs[:, t, :], o_bias[:, :], ALU.add).then_inc(s_xbo, 1)
            def y_im(b):
                pool.wait_ge(s_vb, b + 1)
                v = v_spec[:, b].rearrange("p (o r) (h e) -> p o r h e", o=2, e=HD)
                w = w_spec[:, :, b * H:(b + 1) * H].rearrange("p (o r) h -> p o r h", o=2)
                wim = w[:, :, 1, :].unsqueeze(3).broadcast_to([P, 2, H, HD])
                wre2 = w_re2[:, :, b * H:(b + 1) * H].unsqueeze(3).broadcast_to([P, 2, H, HD])
                t3 = y_tmp[2].rearrange("p (o h e) -> p o h e", o=2, e=HD)
                t4 = y_tmp[3].rearrange("p (o h e) -> p o h e", o=2, e=HD)
                yim = y_spec[b % 2].rearrange("p (o r) (h e) -> p o r h e", o=2, e=HD)[:, :, 1]
                halves = range(2) if b else range(1)
                for o in halves:
                    if b == 1 and o == 1:
                        pool.wait_ge(s_yim0, 1)
                    nc.gpsimd.tensor_tensor(t3[:, o], v[:, o, 0], wim[:, o], ALU.mult)
                    ins = nc.gpsimd.tensor_tensor(t4[:, o], v[:, o, 1], wre2[:, o], ALU.mult)
                link(ins)
                if b >= 2:
                    pool.wait_ge(s_z, DT * (b - 1))
                for o in halves:
                    nc.gpsimd.tensor_tensor(yim[:, o], t3[:, o], t4[:, o], ALU.add).then_inc(s_yim, 1)
                pool.wait_ge(s_yim, 2 * b + 1)

            def z_second(b):
                for jt in range(DT):
                    n = b * DT + jt
                    pool.wait_ge(s_zc, n + 1)
                    z = z_tmp[n % 4]
                    nc.gpsimd.tensor_tensor(zt[:, jt, b, HALF:L], z[:, 0:HALF], z[:, HALF:L],
                                            ALU.subtract).then_inc(s_zt2, 1)

            pool.wait_ge(s_wtab, 1)
            y_im(0)
            for b in range(B):
                if b + 1 < B:
                    y_im(b + 1)
                z_second(b)
            for k in range(N_EARLY, 2 * E - 1):
                split_lo(k)
                if k == N_MID:
                    pool.wait_ge(s_bhi, 1)
                    pool.wait_ge(s_lo, k + 1)
                    nc.gpsimd.tensor_tensor(f_bias[32:32 + E, :], bias_raw[32:32 + E, :],
                                            bias_hi[32:32 + E, :].bitcast(F32), ALU.subtract).then_inc(s_fbias, 1)
                    pool.wait_ge(s_fbias, 2)
            pool.wait_ge(s_blkhot, 1)
            for k in range(2):
                sl = slice(k * TILES, (k + 1) * TILES)
                nc.gpsimd.tensor_tensor(blk_hot[:, 1, sl], blk_hot[:, 2, sl],
                                        tile_b[:, :].unsqueeze(2).broadcast_to([P, TILES, BLOCKS]),
                                        ALU.mult).then_inc(s_tilehot, 1)
            split_lo(2 * E - 1)
            def gather(i):
                nc.gpsimd.indirect_dma_start(
                    out=xg[i % RING], out_offset=None, in_=xn2_dram,
                    in_offset=bass.IndirectOffsetOnAxis(idx[:, 0, i:i + 1], axis=0)).then_inc(s_xg[i % RING], 16)

            pool.wait_ge(s_idx, 1)
            pool.wait_ge(s_rowd, 16 * B)
            for i in range(RING):
                gather(i)
            pool.wait_ge(s_xtp, 1)
            gather(RING)
            pool.wait_ge(s_gsplit, 1)
            nc.gpsimd.tensor_tensor(blk_hot[:, 1, 0:TILES], blk_hot[:, 2, 0:TILES],
                                    g_part[:, 1, 0:TILES].unsqueeze(2).broadcast_to([P, TILES, BLOCKS]),
                                    ALU.mult).then_inc(s_gpool, 1)
            pool.wait_ge(s_outd, 16 * B)
            pool.wait_ge(s_idx, 2)
            for i in range(BLOCKS):
                if i + RING + 1 < BLOCKS:
                    pool.wait_ge(s_xtp, i + 2)
                    gather(i + RING + 1)
                pool.wait_ge(s_yb, i + 1)
                if i:
                    pool.wait_ge(s_sc, 16 * i)
                nc.gpsimd.indirect_dma_start(
                    out=out_rows, out_offset=bass.IndirectOffsetOnAxis(idx[:, 1, i:i + 1], axis=0),
                    in_=yb[i % RING], in_offset=None, bounds_check=B * L - 1, oob_is_err=False,
                    compute_op=ALU.add).then_inc(s_sc, 16)
            pool.wait_ge(s_sc, 16 * BLOCKS)

        @block.scalar
        def _(act):
            act.dma_start(tab[:, 0:C_INV], tabs[:, 0:C_INV]).then_inc(s_fwd, 16)
            act.dma_start(qk_bias[:, :, :].rearrange("p n c -> p (n c)"), bqk).then_inc(s_small, 16)
            act.dma_start(v_bias[:, :], bvo[0:1, :]).then_inc(s_small, 16)
            act.dma_start(o_bias[:, :], bvo[1:2, :].broadcast_to([P, D])).then_inc(s_small, 16)
            act.dma_start(gw[:, :, :], gate_w.rearrange("(c p) e -> p c e", p=P)).then_inc(s_small, 16)
            act.dma_start(gb[:, :], gate_b.broadcast_to([P, E])).then_inc(s_small, 16)

            def copy(o, i):
                return nc.scalar.activation(o, i, ACT.Copy)

            def split_hi(k):
                act.wait_ge(s_raw[HALVES[k] // 2], 16)
                c = slice(HALVES[k] * HALF_E, (HALVES[k] + 1) * HALF_E)
                copy(wh[:, c], raw_w[:, c]).then_inc(s_hi, 1)

            def root(n):
                act.wait_ge(s_var, n + 1)
                b = n % B
                nc.scalar.activation(sd[:, b * TPB:(b + 1) * TPB], var[:, b * TPB:(b + 1) * TPB],
                                     ACT.Sqrt).then_inc(s_sd, 1)

            def norm(n, src, dst, done, tiles=TPB):
                b = n % B
                act.wait_ge(s_rstd, n + 1)
                for t in range(b * TPB, b * TPB + tiles):
                    ins = nc.scalar.activation(dst[:, t, 0:D], src[:, t, :], ACT.Identity,
                                               scale=rstd[:, t:t + 1], bias=nmr[:, t:t + 1])
                ins.then_inc(done, 1)

            def evacuate(n):
                act.wait_ge(s_fill, n + 1)
                bank = FILL_BANKS[n % NB]
                kind, b, i = ORDER[n]
                if kind == "c":
                    dst = c_spec[:, i, b, :]
                elif kind == "x":
                    if b == 0 and i == 0:
                        act.wait_ge(s_uvc0, 6)
                        act.wait_ge(s_uvd, B - 2)
                        act.wait_ge(s_uvc, 2 * (B - 2))
                    dst = x_spec[:, i, b, :]
                elif kind == "k":
                    dst = k_spec[b][:, i, :]
                elif kind == "q":
                    dst = q_spec[b][:, i, :]
                else:
                    if b == 0 and i == 0:
                        act.wait_ge(s_uvx, 3 * B)
                    dst = v_spec[:, b, 2 * i:2 * i + 2, :].rearrange("p k j -> p (k j)")
                copy(dst, bank[:, :]).then_inc(s_evac, 1)

            def warm_up(func, n):
                act.wait_ge(s_warm, n)
                nc.scalar.activation(warm[:, :], warm[:, :], func).then_inc(s_warm, 1)

            done = [0]

            def evacuate_to(n):
                while done[0] < n:
                    evacuate(done[0])
                    done[0] += 1

            root(0)
            evacuate_to(3)
            root(1)
            evacuate_to(5)
            norm(0, xs, xn, s_xn)
            evacuate_to(6)
            root(2)
            norm(1, xs, xn, s_xn)
            evacuate_to(8)
            root(3)
            evacuate_to(8)
            norm(2, xs, xn, s_xn)
            evacuate_to(10)
            norm(3, xs, xn, s_xn)
            split = 0
            for n in range(11, N_QK + 1):
                evacuate_to(n)
                if n == until("x", B - 1):
                    warm_up(ACT.Exp, 1)
                if n % 2 == 0 and n > 12 and split < N_EARLY:
                    split_hi(split)
                    split += 1
            for n in range(N_QK, N_QK + V_AHEAD):
                evacuate(n)
            act.wait_ge(s_heads, B)
            copy(pt[:, :, :].rearrange("p k n -> p (k n)"), ps[4][:, 0:KINDS * NPAIR]).then_inc(s_pt, 1)
            act.wait_ge(s_corr, 1)
            nc.scalar.activation(c_eo, ps[5][0:NPAIR, :], ACT.Copy, scale=1.0 / HD).then_inc(s_ceo, 1)
            evacuate(N_QK + V_AHEAD)
            act.wait_ge(s_neg, 1)
            nc.scalar.activation(c_exp, corr[:, 0:L], ACT.Exp, bias=t_neg[0:NPAIR, 0:1]).then_inc(s_exp, 1)
            nc.scalar.activation(t_exp[0:NPAIR, 0:TOPK], top8[0:NPAIR, 0:TOPK], ACT.Exp,
                                 bias=t_neg[0:NPAIR, 0:1]).then_inc(s_exp, 1)
            warm_up(ACT.Sqrt, 2)
            for n in range(V_AHEAD + 1, V_AHEAD + 3):
                evacuate(N_QK + n)
            act.wait_ge(s_wtr, 1)
            copy(w_t[:, :, :].rearrange("p c n -> p (c n)"), ps[5][:, 0:4 * NPAIR]).then_inc(s_wt, 1)
            evacuate(N_QK + V_AHEAD + 3)
            act.wait_ge(s_wsp, 1)
            copy(w_spec[:, 2:4, :].rearrange("p k n -> p (k n)"), ps[4][:, 2 * NPAIR:4 * NPAIR])
            for g in range(2):
                rows = slice(g * P // 2, (g + 1) * P // 2)
                at_g = (KINDS + 2 * g) * NPAIR
                ins = copy(w_spec[rows, 0:2, :].rearrange("p k n -> p (k n)"), ps[4][rows, at_g:at_g + 2 * NPAIR])
            ins.then_inc(s_wse, 1)
            for n in range(V_AHEAD + 4, 2 * B):
                evacuate(N_QK + n)
            for k in range(N_EARLY, N_MID):
                split_hi(k)

            def z_out(b):
                for n in range(b * DT, (b + 1) * DT):
                    act.wait_ge(s_z, n + 1)
                    if n >= 4:
                        act.wait_ge(s_zt, n - 3)
                        act.wait_ge(s_zt2, n - 3)
                    copy(z_tmp[n % 4], ps[n % 4][:, :]).then_inc(s_zc, 1)

            def gate_out(*b):
                for n in b:
                    act.wait_ge(s_gt, n + 1)
                    if n >= GT:
                        act.wait_ge(s_lgr, n - GT + 1)
                    copy(gate_t[:, n % GT].rearrange("p c t -> p (c t)"), gate_bank[n % GT][:, :]).then_inc(s_gtc, 1)

            for b in range(3):
                z_out(b)
            root(B)
            z_out(3)
            root(B + 1)
            norm(B, xs, xn2, s_xn2)
            act.wait_ge(s_zt, DT * B)
            act.wait_ge(s_zt2, DT * B)
            late = iter(range(N_MID, 2 * E))
            split_hi(next(late))
            norm(B + 1, xs, xn2, s_xn2)
            root(B + 2)
            gate_out(0, 1)
            norm(B + 2, xs, xn2, s_xn2)
            root(B + 3)
            gate_out(2, 3, 4)
            norm(B + 3, xs, xn2, s_xn2, TPB // 2)
            gate_out(5, 6, 7)
            split_hi(next(late))
            warm_up(ACT.Exp, 3)
            split_hi(next(late))
            split_hi(next(late))
            act.wait_ge(s_m12, 1)
            nc.scalar.activation(r16[:, 3, :], r16[:, 2, :], ACT.Exp).then_inc(s_rexp, 1)
            warm_up(ACT.Silu, 4)
            for k in late:
                split_hi(k)
            act.wait_ge(s_blkhot, 1)
            nc.scalar.activation(blk_hot[:, 0], blk_hot[:, 2], ACT.Copy, scale=part_no).then_inc(s_parthot, 1)

            def xt_out(i):
                act.wait_ge(s_xtp, i + 1)
                copy(xt_hi[:, :, :].rearrange("p c t -> p (c t)"), ps[4][:, 0:D]).then_inc(s_xth, 1)

            def expert(i):
                return act.value_load(eb_i[0:1, bass.ds(i, 1)], min_val=0, max_val=E - 1)

            def w2_high(i, e):
                if isinstance(i, int) and i == BLOCKS - 1:
                    copy(w2_hi_last[:, :], w2[:, bass.ds(e * W2, W2)]).then_inc(s_w2h, 1)
                    return
                if not (isinstance(i, int) and i == 0):
                    act.wait_ge(s_yp, i)
                copy(w2_hi[:, :], w2[:, bass.ds(e * W2, W2)]).then_inc(s_w2h, 1)

            def silu(i, n):
                act.wait_ge(s_h1, i + 1)
                nc.scalar.activation(sil[n], ps[0][:, :], ACT.Silu).then_inc(s_sil, 1)

            def act_high(i):
                act.wait_ge(s_atp, i + 1)
                copy(act_hi[:, :, :].rearrange("p c t -> p (c t)"), ps[5][:, :]).then_inc(s_ath, 1)

            def y_out(i, n):
                act.wait_ge(s_yp, i + 1)
                nc.scalar.activation(yb[n], ps[6][:, 0:D], ACT.Copy,
                                     scale=slot_gate[:, bass.ds(i, 1)]).then_inc(s_yb, 1)

            xt_out(0)
            silu(0, 0)
            xt_out(1)
            act.wait_ge(s_gs, 1)
            act.wait_ge(s_w2, 32)
            w2_high(0, expert(0))

            def step(i, n, ahead=RING, reused=True):
                if ahead > 1:
                    silu(i + 1, (n + 1) % RING)
                act_high(i)
                if ahead > 2:
                    xt_out(i + 2)
                if ahead > 1:
                    w2_high(i + 1, expert(i + 1))
                if reused:
                    act.wait_ge(s_sc, 16 * (i + 1 - RING))
                y_out(i, n)

            for n in range(RING):
                step(n, n, reused=False)
            with act.Fori(RING, BLOCKS - RING, RING) as i0:
                for n in range(RING):
                    step(i0 + n, n)
            for n in range(RING):
                step(BLOCKS - RING + n, n, ahead=RING - n)

        @block.vector
        def _(dve):
            link = chain(dve, v_step)
            tt, ts = nc.vector.tensor_tensor, nc.vector.tensor_scalar

            def ln_stats(b, src):
                for t in range(b * TPB, (b + 1) * TPB):
                    ins = nc.vector.bn_stats(stats[:, t, :], src[:, t, :])
                link(ins)
                for t in range(b * TPB, (b + 1) * TPB):
                    ins = nc.vector.bn_aggr(moments[:, t, :], stats[:, t, :])
                link(ins)
                c = slice(b * TPB, (b + 1) * TPB)
                ts(var[:, c], moments[:, c, 1], EPS, None, ALU.add).then_inc(s_var, 1)

            def ln_scale(n):
                b = n % B
                c = slice(b * TPB, (b + 1) * TPB)
                dve.wait_ge(s_sd, n + 1)
                link(nc.vector.reciprocal(rstd[:, c], sd[:, c]))
                link(tt(ltmp[:, c], rstd[:, c], rstd[:, c], ALU.mult))
                link(tt(ltmp[:, c], ltmp[:, c], var[:, c], ALU.mult))
                link(ts(ltmp[:, c], ltmp[:, c], -0.5, 1.5, ALU.mult, ALU.add))
                link(tt(rstd[:, c], rstd[:, c], ltmp[:, c], ALU.mult))
                nc.vector.scalar_tensor_tensor(out=nmr[:, c], in0=moments[:, c, 0], scalar=-1.0,
                                               in1=rstd[:, c], op0=ALU.mult, op1=ALU.mult).then_inc(s_rstd, 1)

            def c_difference(b):
                dve.wait_ge(s_c[b], 16)
                tt(uv_c[:, b, 1], cs[:, b * TPB:b * TPB + 2, :], cs[:, b * TPB + 2:b * TPB + 4, :],
                   ALU.subtract).then_inc(s_uvd, 1)

            def uv(b):
                dve.wait_ge(s_xn, b + 1)
                if b >= 2:
                    dve.wait_ge(s_uvc, 2 * (b - 1))
                fold(tt, link, xn, uv_x, b, s_uvx)

            nc.vector.memset(zeros, 0.0).then_inc(s_zeros, 1)
            nc.vector.memset(warm[:, :], 0.0).then_inc(s_warm, 1)
            dve.wait_ge(s_c[0], 16)
            for b in range(2):
                if b:
                    dve.wait_ge(s_c[b], 16)
                fold(tt, link, cs, uv_c, b, s_uvc0)
            for b in range(B):
                dve.wait_ge(s_x[b], 16)
                ln_stats(b, xs)
                if b < 2:
                    c_difference(b + 2)
                if b:
                    ln_scale(b - 1)
                if b > 1:
                    uv(b - 2)
            ln_scale(B - 1)
            uv(B - 2)
            uv(B - 1)

            dve.wait_ge(s_bias, 2)
            for b in range(B):
                dve.wait_ge(s_evac, until("q", b))
                q, k = q_spec[b], k_spec[b]
                tt(q[:, :, 0], q[:, :, 0], qk_bias[:, 0, :], ALU.add)
                tt(k[:, :, 0], k[:, :, 0], qk_bias[:, 1, :], ALU.add)
                link(nc.vector.tensor_copy(nyq[:, :], k[:, :, P]))
                link(nc.vector.memset(k[:, :, P:P + 1], 0.0))
                link(tt(same, q, k, ALU.mult))
                link(nc.vector.tensor_copy(k[:, :, 0], nyq[:, :]))
                for jt in range(DT):
                    qs = q[:, jt].rearrange("p (o r f) -> p o r f", o=2, r=2)
                    ks = k[:, jt].rearrange("p (o r f) -> p o r f", o=2, r=2)
                    ss = cross[:, jt].rearrange("p (o r f) -> p o r f", o=2, r=2)
                    tt(ss[:, :, 0], qs[:, :, 1], ks[:, :, 0], ALU.mult)
                    ins = tt(ss[:, :, 1], qs[:, :, 0], ks[:, :, 1], ALU.mult)
                ins.then_inc(s_used, 1)
                if b >= 2:
                    dve.wait_ge(s_heads, b - 1)
                dve.wait_ge(s_used, b + 1)
                for src, r, op in ((same, 0, ALU.add), (cross, 1, ALU.subtract)):
                    v = src.rearrange("p c (o r f) -> p c o r f", o=2, r=2)
                    for jt in range(DT):
                        o = prod[b % 2][:, jt].rearrange("p (o r) f -> p o r f", o=2)
                        tt(o[:, :, r], v[:, jt, :, 0], v[:, jt, :, 1], op).then_inc(s_prod, 1)
                dve.wait_ge(s_prod, 2 * DT * (b + 1))

            dve.wait_ge(s_heads, B)
            nc.vector.memset(corr[:, L:W_], PAD)
            link(nc.vector.memset(top3[0:NPAIR, :], PAD))
            dve.wait_ge(s_ceo, 1)
            tt(corr[:, 0:HALF], c_eo[:, 0:HALF], c_eo[:, HALF:L], ALU.add)
            link(tt(corr[:, HALF:L], c_eo[:, 0:HALF], c_eo[:, HALF:L], ALU.subtract))
            link(nc.vector.max(top8[0:NPAIR, :], corr[:, 0:L]))
            ts(t_neg[0:NPAIR, 0:1], top8[0:NPAIR, 0:1], -1.0, None, ALU.mult).then_inc(s_neg, 1)
            link(nc.vector.tensor_copy(top3[0:NPAIR, 0:TOPK], top8[0:NPAIR, 0:TOPK]))
            link(nc.vector.match_replace(rest, top3[0:NPAIR, :], corr, 3.0e38))
            tt(c_mask, rest[:, 0:L], corr[:, 0:L], ALU.not_equal)
            dve.wait_ge(s_exp, 2)
            link(nc.vector.tensor_reduce(t_exp[0:NPAIR, 3:4], t_exp[0:NPAIR, 0:TOPK], AX_X, ALU.add))
            link(nc.vector.reciprocal(t_neg[0:NPAIR, 1:2], t_exp[0:NPAIR, 3:4]))
            link(nc.vector.scalar_tensor_tensor(out=c_w, in0=c_mask, scalar=t_neg[0:NPAIR, 1:2], in1=c_exp,
                                                op0=ALU.mult, op1=ALU.mult))
            tt(w_uv[:, HALF:L], c_w[:, 0:HALF], c_w[:, HALF:L], ALU.subtract).then_inc(s_wuv, 1)
            link(tt(c_w[:, 0:HALF], c_w[:, 0:HALF], c_w[:, HALF:L], ALU.add))
            tt(w_uv[:, 0:P], c_w[:, 0:P], c_w[:, P:HALF], ALU.add).then_inc(s_wuv, 1)
            tt(w_uv[:, P:HALF], c_w[:, 0:P], c_w[:, P:HALF], ALU.subtract).then_inc(s_wuv, 1)
            def value_bias(b):
                dve.wait_ge(s_evac, until("v", b))
                tt(v_spec[0:1, b, 0, :], v_spec[0:1, b, 0, :], v_bias[:, :], ALU.add).then_inc(s_vb, 1)

            value_bias(0)
            value_bias(1)
            nc.vector.tensor_copy(iota_b[:, :], iota)
            nc.vector.tensor_copy(tile_b[:, :], tile_no)
            nc.vector.tensor_copy(before_b[:, :], before)
            nc.vector.tensor_copy(ones_b[:, :], ones)
            dve.wait_ge(s_wse, 1)
            link(nc.vector.tensor_copy(w_re2[:, :, :],
                                       w_spec[:, :, :].rearrange("p (o r) n -> p o r n", o=2)[:, :, 0]))
            link(nc.vector.tensor_copy(w_re2[0:1, 0, :], w_spec[0:1, 1, :]))
            nc.vector.memset(w_spec[0:1, 1, :], 0.0).then_inc(s_wtab, 1)
            dve.wait_ge(s_wtab, 1)

            def y_re(b):
                dve.wait_ge(s_vb, b + 1)
                v = v_spec[:, b].rearrange("p (o r) (h e) -> p o r h e", o=2, e=HD)
                w = w_spec[:, :, b * H:(b + 1) * H].rearrange("p (o r) h -> p o r h", o=2)
                t1 = y_tmp[0].rearrange("p (o h e) -> p o h e", o=2, e=HD)
                t2 = y_tmp[1].rearrange("p (o h e) -> p o h e", o=2, e=HD)
                yre = y_spec[b % 2].rearrange("p (o r) (h e) -> p o r h e", o=2, e=HD)[:, :, 0]
                for o in range(2):
                    wre = w[:, o, 0, :].unsqueeze(2).broadcast_to([P, H, HD])
                    wim = w[:, o, 1, :].unsqueeze(2).broadcast_to([P, H, HD])
                    tt(t1[:, o], v[:, o, 0], wre, ALU.mult)
                    ins = tt(t2[:, o], v[:, o, 1], wim, ALU.mult)
                link(ins)
                if b >= 2:
                    dve.wait_ge(s_z, DT * (b - 1))
                for o in range(2):
                    tt(yre[:, o], t1[:, o], t2[:, o], ALU.subtract).then_inc(s_yre, 1)
                if b == 0:
                    t3, t4 = (y_tmp[n].rearrange("p (o h e) -> p o h e", o=2, e=HD)[:, 1] for n in (2, 3))
                    tt(t3, v[:, 1, 0], w[:, 1, 1, :].unsqueeze(2).broadcast_to([P, H, HD]), ALU.mult)
                    link(tt(t4, v[:, 1, 1], w_re2[:, 1, 0:H].unsqueeze(2).broadcast_to([P, H, HD]), ALU.mult))
                    yim = y_spec[0].rearrange("p (o r) (h e) -> p o r h e", o=2, e=HD)[:, 1, 1]
                    tt(yim, t3, t4, ALU.add).then_inc(s_yim0, 1)
                dve.wait_ge(s_yre, 2 * (b + 1))

            def z_first(b):
                for jt in range(DT):
                    n = b * DT + jt
                    dve.wait_ge(s_zc, n + 1)
                    z = z_tmp[n % 4]
                    tt(zt[:, jt, b, 0:HALF], z[:, 0:HALF], z[:, HALF:L], ALU.add).then_inc(s_zt, 1)

            def residual(b, before_stats=None):
                for m in range(2):
                    n = 2 * b + m
                    dve.wait_ge(s_o, n + 1)
                    v = xs[:, 2 * n:2 * n + 2, :].rearrange("p t d -> p (t d)")
                    tt(v, v, ps[4 + n % 4][:, :], ALU.add).then_inc(s_x1, 1)
                if before_stats is not None:
                    ln_scale(before_stats)
                dve.wait_ge(s_x1, 2 * (b + 1))
                ln_stats(b, xs)

            dve.wait_ge(s_xbo, TILES)
            y_re(0)
            y_re(1)
            value_bias(2)
            value_bias(3)
            e_row = iota[:, 0:E].unsqueeze(2).broadcast_to([P, E, E])
            e_col = iota[:, 0:E].unsqueeze(1).broadcast_to([P, E, E])
            tt(up_to[:, 0:E, :], e_row, e_col, ALU.is_gt)
            tt(up_to[:, E:2 * E, :], e_row, e_col, ALU.is_ge)
            z_first(0)
            y_re(2)
            z_first(1)
            nc.vector.memset(f_bias[:, 0:C_INV].bitcast(F32), 0.0).then_inc(s_fzero, 1)
            residual(0)
            y_re(3)
            z_first(2)
            ln_scale(B)
            residual(1)
            z_first(3)
            ln_scale(B + 1)
            dve.wait_ge(s_z, DT * B)
            nc.vector.memset(f_bias[:, C_INV:BCOLS].bitcast(F32), 0.0).then_inc(s_fzero, 1)
            residual(2)
            residual(3, before_stats=B + 2)

            def logits_out(*tiles):
                for n in tiles:
                    dve.wait_ge(s_lgr, n + 1)
                    if n >= 2:
                        dve.wait_ge(s_lg, n - 1)
                    nc.vector.tensor_copy(lg_t[n % 2], logit_bank[n % 2][0:E, 0:2 * P]).then_inc(s_lgc, 1)

            logits_out(0, 1)
            ln_scale(B + 3)
            dve.wait_ge(s_rstd, 2 * B)
            for t in range(TILES - TPB // 2, TILES):
                ins = ts(xn2[:, t, :], xs[:, t, :], rstd[:, t:t + 1], nmr[:, t:t + 1], ALU.mult, ALU.add)
            ins.then_inc(s_xn2v, 1)
            logits_out(2, 3)
            dve.wait_ge(s_fb, 32)
            for h in (0, 32):
                ins = nc.vector.tensor_copy(bias_hi[h:h + E, :], bias_raw[h:h + E, :])
            ins.then_inc(s_bhi, 1)
            logits_out(4, 5)
            dve.wait_ge(s_bhi, 1)
            dve.wait_ge(s_fzero, 2)
            nc.vector.tensor_copy(f_bias[0:E, :], bias_hi[0:E, :]).then_inc(s_fbias, 1)
            logits_out(6, 7)

            def bias_hot(i, n):
                ts(bhot[n][:, :], ones, e_hot[:, bass.ds(i, 1)], None, ALU.mult).then_inc(s_bh, 1)

            def xt_low(i):
                dve.wait_ge(s_xth, i + 1)
                tt(xt_lo[:, :, :].rearrange("p c t -> p (c t)"), ps[4][:, 0:D],
                   xt_hi[:, :, :].rearrange("p c t -> p (c t)").bitcast(F32), ALU.subtract).then_inc(s_xtc, 1)

            def gate(i, n):
                dve.wait_ge(s_sil, i + 1)
                dve.wait_ge(s_h0, i + 1)
                tt(sil[n], sil[n], ps[2][:, :], ALU.mult).then_inc(s_act, 1)

            def w2_low(i):
                e = dve.value_load(eb_i[0:1, bass.ds(i, 1)], min_val=0, max_val=E - 1)
                dve.wait_ge(s_w2h, i + 1)
                hi, lo = w2_hi[:, :], w2_lo[:, :]
                if isinstance(i, int) and i == BLOCKS - 1:
                    dve.wait_ge(s_h0, BLOCKS)
                    hi, lo = w2_hi_last[:, :], w2_lo_last
                tt(lo, w2[:, bass.ds(e * W2, W2)], hi.bitcast(F32), ALU.subtract).then_inc(s_w2l, 1)

            def act_low(i):
                dve.wait_ge(s_ath, i + 1)
                tt(act_lo[:, :, :].rearrange("p c t -> p (c t)"), ps[5][:, :],
                   act_hi[:, :, :].rearrange("p c t -> p (c t)").bitcast(F32), ALU.subtract).then_inc(s_atl, 1)

            def te(a):
                return a.rearrange("p (t e) -> p t e", e=E)

            def over_e(a):
                return a.unsqueeze(2).broadcast_to([P, TILES, E])

            def over_t(a):
                return a.unsqueeze(1).broadcast_to([P, TILES, E])

            dve.wait_ge(s_lg, TILES // 2)
            link(tt(te(lg), te(ps[6][:, 0:TILES * E]), over_t(gb[:, :]), ALU.add))
            for src, mask, k in ((lg, m1, 0), (lg2, m2, 1)):
                link(nc.vector.tensor_reduce(r16[:, k, :], te(src), AX_X, ALU.max))
                link(tt(te(rtmp), te(src), over_e(r16[:, k, :]), ALU.is_equal))
                link(nc.vector.scalar_tensor_tensor(out=te(cand), in0=te(rtmp), scalar=-float(E),
                                                    in1=over_t(iota[:, 0:E]), op0=ALU.mult, op1=ALU.add))
                link(nc.vector.tensor_reduce(r16[:, 4 + k, :], te(cand), AX_X, ALU.min))
                link(tt(te(mask), te(cand), over_e(r16[:, 4 + k, :]), ALU.is_equal))
                if k == 0:
                    link(nc.vector.scalar_tensor_tensor(out=lg2, in0=mask, scalar=PAD, in1=lg,
                                                        op0=ALU.mult, op1=ALU.add))
            tt(r16[:, 2, :], r16[:, 1, :], r16[:, 0, :], ALU.subtract).then_inc(s_m12, 1)
            tt(pairs_b[:, :], m1, m2, ALU.add).then_inc(s_hot, 1)
            dve.wait_ge(s_rexp, 1)
            link(ts(r16[:, 4, :], r16[:, 3, :], 1.0, None, ALU.add))
            link(nc.vector.reciprocal(r16[:, 5, :], r16[:, 4, :]))
            link(tt(r16[:, 6, :], r16[:, 3, :], r16[:, 5, :], ALU.mult))
            dve.wait_ge(s_count, 1)
            n_e = ps[6][:, 0:E]
            nb3 = nbt[:, :].rearrange("p (e t) -> p e t", e=E)
            link(tt(nb3, n_e.unsqueeze(2).broadcast_to([P, E, TILES]),
                    thresholds.unsqueeze(1).broadcast_to([P, E, TILES]), ALU.is_gt))
            link(nc.vector.tensor_reduce(r8[:, 0, :], nb3, AX_X, ALU.add))
            link(tt(up_to_sum[:, :, :], up_to[:, :, :],
                    r8[:, 0, :].unsqueeze(1).broadcast_to([P, 2 * E, E]), ALU.mult))
            link(nc.vector.tensor_reduce(r8[:, 1:3, :].rearrange("p k e -> p (k e)"), up_to_sum[:, :, :],
                                         AX_X, ALU.add))
            starts, ends = r8[:, 1, :], r8[:, 2, :]
            dve.wait_ge(s_rank, 1)
            link(nc.vector.scalar_tensor_tensor(out=te(rank), in0=over_t(starts), scalar=float(P),
                                                in1=te(ps[3][:, 0:P]), op0=ALU.mult, op1=ALU.add))
            link(tt(rt[:, 8:10, :], rt[:, 2:4, :], rank.unsqueeze(1).broadcast_to([P, 2, TILES * E]), ALU.mult))
            link(nc.vector.tensor_reduce(slot_f[:, :], rt[:, 8:10, :].rearrange("p k (t e) -> p (k t) e", e=E),
                                         AX_X, ALU.add))
            link(nc.vector.tensor_copy(slot_i[:, 0, :], slot_f[:, :]))
            nc.vector.tensor_single_scalar(slot_i[:, 1, :], slot_i[:, 0, :], 7, ALU.arith_shift_right)
            link(nc.vector.tensor_single_scalar(slot_i[:, 2, :], slot_i[:, 0, :], P - 1, ALU.bitwise_and))
            link(nc.vector.tensor_copy(slot_b[:, :, :], slot_i[:, 1:3, :]))
            dve.wait_ge(s_rowd, 16 * B)
            hot = blk_hot[:, 2]
            tt(hot, slot_b[:, 0, :].unsqueeze(2).broadcast_to([P, NS, BLOCKS]),
               iota_b[:, 0:BLOCKS].unsqueeze(1).broadcast_to([P, NS, BLOCKS]), ALU.is_equal).then_inc(s_blkhot, 1)
            for k in range(2):
                sl = slice(k * TILES, (k + 1) * TILES)
                tt(pos_hot[:, sl, :], slot_b[:, 1, sl].unsqueeze(2).broadcast_to([P, TILES, P]),
                   iota_b[:, :].unsqueeze(1).broadcast_to([P, TILES, P]), ALU.is_equal).then_inc(s_slot, 1)
            eb3 = eb_t.rearrange("p (n e) -> p n e", e=E)
            link(tt(eb3, ends.unsqueeze(1).broadcast_to([P, BLOCKS_PAD, E]),
                    iota[:, 0:BLOCKS_PAD].unsqueeze(2).broadcast_to([P, BLOCKS_PAD, E]), ALU.is_le))
            nc.vector.memset(idx[:, :, BLOCKS:BLOCKS_PAD], 0)
            nc.vector.memset(slot_gate[:, BLOCKS:BLOCKS_PAD], 0)
            dve.wait_ge(s_idxp, 1)
            nc.vector.tensor_copy(idx_f[:, 2, :], ps[3][:, 0:BLOCKS])
            link(ts(idx_f[:, 0, :], ps[3][:, BLOCKS:2 * BLOCKS], float(P), -float(P), ALU.mult, ALU.add))
            link(tt(idx_f[:, 0, :], idx_f[:, 0, :], idx_f[:, 2, :], ALU.add))
            ts(idx[:, 0, 0:BLOCKS], idx_f[:, 0, :], 0.0, None, ALU.max).then_inc(s_idx, 1)
            link(ts(idx_f[:, 1, :], idx_f[:, 0, :], 0.0, FAR, ALU.is_lt, ALU.mult))
            tt(idx[:, 1, 0:BLOCKS], idx_f[:, 1, :], idx_f[:, 0, :], ALU.add).then_inc(s_idx, 1)
            link(nc.vector.tensor_reduce(eb[:, :], eb3, AX_X, ALU.add))
            link(ts(eb[:, :], eb[:, :], float(E - 1), None, ALU.min))
            nc.vector.tensor_copy(eb_i[:, :], eb[:, :]).then_inc(s_eb, 1)
            ts(e_hot[:, :], eb[:, :], bias_row, None, ALU.is_equal).then_inc(s_eb, 1)
            dve.wait_ge(s_eb, 2)
            link(nc.vector.tensor_copy(g_part[:, 0, :], r16[:, 5:7, :].rearrange("p k t -> p (k t)")))
            link(tt(g_rest[:, :], r16[:, 5:7, :].rearrange("p k t -> p (k t)"), g_part[:, 0, :], ALU.subtract))
            link(nc.vector.tensor_copy(g_part[:, 1, :], g_rest[:, :]))
            link(tt(g_rest[:, :], g_rest[:, :], g_part[:, 1, :], ALU.subtract))
            nc.vector.tensor_copy(g_part[:, 2, :], g_rest[:, :]).then_inc(s_gsplit, 1)
            dve.wait_ge(s_gsplit, 1)

            def gate_part(v, first=0):
                tt(blk_hot[:, v, first:], hot[:, first:],
                   g_part[:, v, first:].unsqueeze(2).broadcast_to([P, NS - first, BLOCKS]),
                   ALU.mult).then_inc(s_gparts, 1)

            bias_hot(0, 0)
            bias_hot(1, 1)
            xt_low(0)
            gate_part(0)
            gate_part(1, first=TILES)
            dve.wait_ge(s_gparts, 2)
            dve.wait_ge(s_gpool, 1)
            gate_part(2)
            gate(0, 0)
            xt_low(1)
            dve.wait_ge(s_gp, 1)
            nc.vector.tensor_reduce(slot_gate[:, 0:BLOCKS],
                                    ps[3][:, 0:HOTS * BLOCKS].rearrange("p (v s) -> p s v", v=HOTS),
                                    AX_X, ALU.add).then_inc(s_gs, 1)
            w2_low(0)

            def step(i, n, ahead=RING):
                act_low(i)
                if ahead > 1:
                    gate(i + 1, (n + 1) % RING)
                if ahead > 2:
                    bias_hot(i + 2, (n + 2) % RING)
                    xt_low(i + 2)
                if ahead > 1:
                    w2_low(i + 1)

            with dve.Fori(0, BLOCKS - RING, RING) as i0:
                for n in range(RING):
                    step(i0 + n, n)
            for n in range(RING):
                step(BLOCKS - RING + n, n, ahead=RING - n)

        @block.tensor
        def _(pe):
            mm = nc.tensor.matmul
            fills = [0]

            def fill_start():
                if fills[0] >= NB:
                    pe.wait_ge(s_evac, fills[0] - NB + 1)
                bank = FILL_BANKS[fills[0] % NB]
                fills[0] += 1
                return bank

            def spectra(b, uv, odd, n_odd, even_sums, n_even):
                for dt in range(DT):
                    bank = fill_start()
                    pe.wait_ge(odd, n_odd)
                    for c in range(2):
                        mm(bank[:, 256:512], uv[:, b, 1, c, dt * P:(dt + 1) * P], fwd_odd[:, c, :],
                           start=(c == 0), stop=(c == 1))
                    pe.wait_ge(even_sums, n_even)
                    even = bank[:, 0:256].rearrange("p (r g f) -> p r g f", r=2, g=2)
                    for g in range(2):
                        ins = mm(even[:, :, g, :], uv[:, b, 0, g, dt * P:(dt + 1) * P], fwd_even[:, :, g, :],
                                 start=True, stop=True)
                    ins.then_inc(s_fill, 1)

            def project(b, w, spec):
                for jt in range(DT):
                    bank = fill_start()
                    for dt in range(DT):
                        ins = mm(bank[:, :], w[:, dt, jt * P:(jt + 1) * P], spec[:, dt, b, :],
                                 start=(dt == 0), stop=(dt == DT - 1))
                    ins.then_inc(s_fill, 1)

            def keep_warm(count, bank, rows=cst[:, 0:512]):
                for _ in range(count):
                    mm(bank[:, :], rows[:, 0:P], rows, start=True, stop=True)

            pe.wait_ge(s_zeros, 1)
            keep_warm(2, ps[7], zeros)
            pe.wait_ge(s_fwd, 16)
            for b in range(B):
                if b < 2:
                    spectra(b, uv_c, s_uvc0, 3 * b + 1, s_uvc0, 3 * b + 3)
                else:
                    spectra(b, uv_c, s_uvd, b - 1, s_uvc, 2 * (b - 1))
            pe.wait_ge(s_wk, 16)
            def heads(b):
                for r in range(2):
                    for jt in range(DT):
                        pe.wait_ge(s_prod, 2 * DT * b + DT * r + jt + 1)
                        for o in range(2):
                            k = 2 * o + r
                            dst = ps[4][:, k * NPAIR + b * H + jt * 8:k * NPAIR + b * H + jt * 8 + 8]
                            ins = mm(dst, prod[b % 2][:, jt, k, :], head_sum[:, 0:8], start=True, stop=True)
                ins.then_inc(s_heads, 1)

            for kind, b in STEPS:
                if kind == "k":
                    pe.wait_ge(s_evac, until("c", b))
                    project(b, wk, c_spec)
                elif kind == "x":
                    spectra(b, uv_x, s_uvx, 3 * b + 1, s_uvx, 3 * b + 3)
                else:
                    if b == 0:
                        pe.wait_ge(s_watt, 32)
                    pe.wait_ge(s_evac, until("x", b))
                    project(b, wq, x_spec)
                    if b == 1:
                        pe.wait_ge(s_cst, 16)
                        heads(0)
            heads(1)
            def values(n):
                b, o = divmod(n, 2)
                bank = fill_start()
                for r in range(2):
                    k = 2 * o + r
                    for dt in range(DT):
                        ins = mm(bank[:, r * 256:(r + 1) * 256], c_spec[:, dt, b, k * P:(k + 1) * P],
                                 wv[:, dt, :], start=(dt == 0), stop=(dt == DT - 1))
                ins.then_inc(s_fill, 1)

            values(0)
            heads(2)
            for n in range(1, V_AHEAD):
                values(n)
            heads(3)
            keep_warm(1, ps[5])
            pe.wait_ge(s_pt, 1)
            pe.wait_ge(s_inv, 16)
            for o in range(2):
                for r in range(2):
                    ins = mm(ps[5][0:NPAIR, o * 256:(o + 1) * 256], pt[:, 2 * o + r, :], inv[:, 2 * o + r, :],
                             start=(r == 0), stop=(r == 1))
            ins.then_inc(s_corr, 1)
            for n in range(V_AHEAD, V_AHEAD + 3):
                values(n)
            pe.wait_ge(s_wuv, 3)
            for c in range(4):
                ins = nc.tensor.transpose(ps[5][:, c * NPAIR:(c + 1) * NPAIR], w_uv[:, c * P:(c + 1) * P],
                                          ident[0:NPAIR, 0:NPAIR])
            ins.then_inc(s_wtr, 1)
            values(V_AHEAD + 3)
            pe.wait_ge(s_wt, 1)
            for r in range(2):
                for g in range(2):
                    mm(ps[4][:, (KINDS + 2 * g + r) * NPAIR:(KINDS + 2 * g + r + 1) * NPAIR], fwd_even[:, r],
                       w_t[:, g, :], start=True, stop=True)
                for c in range(2):
                    ins = mm(ps[4][:, (2 + r) * NPAIR:(3 + r) * NPAIR], fwd_odd[:, c, r * P:(r + 1) * P],
                             w_t[:, 2 + c, :], start=(c == 0), stop=(c == 1))
            ins.then_inc(s_wsp, 1)

            for n in range(V_AHEAD + 4, 2 * B):
                values(n)

            def back(b):
                for jt in range(DT):
                    n = b * DT + jt
                    if n < 4:
                        pe.wait_ge(s_evac, FILLS - 3 + n)
                    if n >= 4:
                        pe.wait_ge(s_zc, n - 3)
                    for o in range(2):
                        if jt == 0:
                            pe.wait_ge(s_yre, 2 * b + o + 1)
                            if b == 0 and o == 1:
                                pe.wait_ge(s_yim0, 1)
                            else:
                                pe.wait_ge(s_yim, max(2 * b + o, 1))
                        for r in range(2):
                            ins = mm(ps[n % 4][:, o * 256:(o + 1) * 256],
                                     y_spec[b % 2][:, 2 * o + r, jt * P:(jt + 1) * P], inv[:, 2 * o + r, :],
                                     start=(r == 0), stop=(r == 1))
                    ins.then_inc(s_z, 1)

            def out_proj(b):
                pe.wait_ge(s_zt, DT * (b + 1))
                pe.wait_ge(s_zt2, DT * (b + 1))
                for m in range(2):
                    n = 2 * b + m
                    if n == 0:
                        pe.wait_ge(s_wse, 1)
                    if n >= 4:
                        pe.wait_ge(s_x1, n - 3)
                    for t in range(2):
                        for jt in range(DT):
                            at = (2 * m + t) * P
                            ins = mm(ps[4 + n % 4][:, t * 256:(t + 1) * 256], zt[:, jt, b, at:at + P], wo[:, jt, :],
                                     start=(jt == 0), stop=(jt == DT - 1))
                    ins.then_inc(s_o, 1)

            for b in range(B):
                back(b)
                if b:
                    out_proj(b - 1)
            out_proj(B - 1)

            def rows_across(*steps):
                for n in steps:
                    pe.wait_ge(s_xn2, n // 2 + 1)
                    if n == TILES // 2 - 1:
                        pe.wait_ge(s_xn2v, 1)
                    if n == 3:
                        pe.wait_ge(s_x1, 5)
                    if n >= GT:
                        pe.wait_ge(s_gtc, n - GT + 1)
                    for t in range(2):
                        for c in range(DT):
                            ins = nc.tensor.transpose(gate_bank[n % GT][:, (t * DT + c) * P:(t * DT + c + 1) * P],
                                                      xn2[:, 2 * n + t, c * P:(c + 1) * P], ident)
                    ins.then_inc(s_gt, 1)

            def logits(*steps):
                for n in steps:
                    pe.wait_ge(s_gtc, n + 1)
                    if n == 1:
                        pe.wait_ge(s_x1, 6)
                    if n >= 2:
                        pe.wait_ge(s_lgc, n - 1)
                    rows = gate_t[:, n % GT].rearrange("p (t c) s -> p c t s", t=2)
                    for c in range(DT):
                        ins = mm(logit_bank[n % 2][0:E, 0:2 * P], gw[:, c, :], rows[:, c], start=(c == 0),
                                 stop=(c == DT - 1))
                    ins.then_inc(s_lgr, 1)

            def logits_back(*steps):
                for n in steps:
                    if n == 0:
                        pe.wait_ge(s_x1, 7)
                    pe.wait_ge(s_lgc, n + 1)
                    for t in range(2):
                        ins = nc.tensor.transpose(ps[6][:, (2 * n + t) * E:(2 * n + t + 1) * E],
                                                  lg_t[n % 2][:, t * P:(t + 1) * P], ident[0:E, 0:E])
                    ins.then_inc(s_lg, 1)

            pe.wait_ge(s_zc, DT * B)
            pe.wait_ge(s_small, 16 * 5)
            rows_across(0, 1, 2)
            logits(0)
            rows_across(3)
            logits(1)
            rows_across(4)
            logits(2)
            rows_across(5)
            logits(3)
            logits_back(0, 1)
            rows_across(6, 7)
            logits(4)
            logits_back(2, 3)
            logits(5)
            logits_back(4)
            logits(6)
            logits_back(5)
            logits(7)
            logits_back(6, 7)
            keep_warm(4, ps[7])
            pe.wait_ge(s_hot, 1)
            for t in range(TILES):
                ins = mm(ps[6][:, 0:E], ones_b[:, :], pairs_b[:, t * E:(t + 1) * E], start=(t == 0),
                         stop=(t == TILES - 1))
            ins.then_inc(s_count, 1)
            mm(ps[3][:, 0:P], before_b[:, :], pairs_b[:, :], start=True, stop=False)
            for t in range(1, TILES):
                ins = mm(ps[3][:, t * E:P], ones_b[:, :], pairs_b[:, 0:P - t * E], start=False,
                         stop=(t == TILES - 1))
            ins.then_inc(s_rank, 1)
            pe.wait_ge(s_blkhot, 1)
            keep_warm(2, ps[7])
            for n in range(NS):
                if n % TILES == 0:
                    pe.wait_ge(s_slot, 1 + n // TILES)
                    pe.wait_ge(s_parthot, 1)
                    pe.wait_ge(s_tilehot, 1 + n // TILES)
                ins = mm(ps[3][:, 0:2 * BLOCKS], pos_hot[:, n, :], blk_hot[:, 0:2, n, :],
                         start=(n == 0), stop=(n == NS - 1))
            ins.then_inc(s_idxp, 1)

            def slot_gates():
                pe.wait_ge(s_gparts, HOTS)
                pe.wait_ge(s_gpool, 1)
                for n in range(NS):
                    ins = mm(ps[3][:, 0:HOTS * BLOCKS], pos_hot[:, n, :], blk_hot[:, :, n, :],
                             start=(n == 0), stop=(n == NS - 1))
                ins.then_inc(s_gp, 1)

            def xt_in(i, n, rows):
                pe.wait_ge(s_xg[n], rows)
                if not (isinstance(i, int) and i == 0):
                    pe.wait_ge(s_xtc, i)
                for c in range(DT):
                    ins = nc.tensor.transpose(ps[4][:, c * P:(c + 1) * P], xg[n][:, c * P:(c + 1) * P], ident)
                ins.then_inc(s_xtp, 1)

            def hidden(half, n, bank, e, done):
                mm(bank[:, :], bhot[n][:, :], f_bias[:, half * FH:(half + 1) * FH], start=True, stop=False)
                for c in range(DT):
                    cols = bass.ds(e * W01 + (half * DT + c) * FH, FH)
                    mm(bank[:, :], xt_hi[:, c, :], wl[:, cols], start=False, stop=False)
                    mm(bank[:, :], xt_hi[:, c, :], wh[:, cols], start=False, stop=False)
                    ins = mm(bank[:, :], xt_lo[:, c, :], wh[:, cols], start=False, stop=(c == DT - 1))
                ins.then_inc(done, 1)

            def act_in(i, n):
                pe.wait_ge(s_act, i + 1)
                for c in range(FH // P):
                    ins = nc.tensor.transpose(ps[5][:, c * P:(c + 1) * P], sil[n][:, c * P:(c + 1) * P], ident)
                ins.then_inc(s_atp, 1)

            def y_in(i, n):
                if not (isinstance(i, int) and i == 0):
                    pe.wait_ge(s_yb, i)
                mm(ps[6][:, 0:D], bhot[n][:, :], f_bias[:, 2 * FH:BCOLS], start=True, stop=False)
                if isinstance(i, int) and i == BLOCKS - 1:
                    pe.wait_ge(s_ath, BLOCKS)
                    pe.wait_ge(s_w2l, BLOCKS)
                    for c in range(FH // P):
                        cols = slice(c * D, (c + 1) * D)
                        mm(ps[6][:, 0:D], act_hi[:, c, :], w2_lo_last[:, cols], start=False, stop=False)
                        mm(ps[6][:, 0:D], act_hi[:, c, :], w2_hi_last[:, cols], start=False, stop=False)
                    pe.wait_ge(s_atl, BLOCKS)
                    for c in range(FH // P):
                        ins = mm(ps[6][:, 0:D], act_lo[:, c, :], w2_hi_last[:, c * D:(c + 1) * D], start=False,
                                 stop=(c == FH // P - 1))
                    ins.then_inc(s_yp, 1)
                    return
                pe.wait_ge(s_atl, i + 1)
                pe.wait_ge(s_w2l, i + 1)
                for c in range(FH // P):
                    cols = slice(c * D, (c + 1) * D)
                    mm(ps[6][:, 0:D], act_hi[:, c, :], w2_lo[:, cols], start=False, stop=False)
                    mm(ps[6][:, 0:D], act_hi[:, c, :], w2_hi[:, cols], start=False, stop=False)
                    ins = mm(ps[6][:, 0:D], act_lo[:, c, :], w2_hi[:, cols], start=False, stop=(c == FH // P - 1))
                ins.then_inc(s_yp, 1)

            def expert(i):
                return pe.value_load(eb_i[0:1, bass.ds(i, 1)], min_val=0, max_val=E - 1)

            def h1_part(i, n, e):
                pe.wait_ge(s_bh, i + 1)
                pe.wait_ge(s_xtc, i + 1)
                if not (isinstance(i, int) and i == 0):
                    pe.wait_ge(s_sil, i)
                hidden(1, n, ps[0], e, s_h1)

            def h0_part(i, n, e):
                if not (isinstance(i, int) and i == 0):
                    pe.wait_ge(s_act, i)
                hidden(0, n, ps[2], e, s_h0)

            def step(i, n, turn, ahead=RING):
                m, k = (n + 1) % RING, (n + 2) % RING
                if ahead > 1:
                    e = expert(i + 1)
                    h1_part(i + 1, m, e)
                act_in(i, n)
                if ahead > 1:
                    h0_part(i + 1, m, e)
                if ahead > 2:
                    xt_in(i + 2, k, 16 * (turn + (2 if n + 2 >= RING else 1)))
                y_in(i, n)

            keep_warm(4, ps[7])
            pe.wait_ge(s_eb, 2)
            xt_in(0, 0, 16)
            pe.wait_ge(s_lo, 2 * E)
            e = expert(0)
            h1_part(0, 0, e)
            h0_part(0, 0, e)
            xt_in(1, 1, 16)
            slot_gates()
            for n in range(RING):
                step(n, n, 0)
            with pe.Fori(RING, BLOCKS - RING, RING) as i0:
                for n in range(RING):
                    step(i0 + n, n, i0 // RING)
            for n in range(RING):
                step(BLOCKS - RING + n, n, BLOCKS // RING - 1, ahead=RING - n)


_OUTS = [((B, L, D), "float32")]


def tables():
    import numpy as np
    c, tab = np.zeros((P, C_END)), np.zeros((P, C_TABS))
    f, t = np.arange(P), np.arange(HALF)
    fe, fo = np.concatenate([4 * f[:P // 2], 4 * f[:P // 2] + 2]), 2 * f + 1
    fwd_even, fwd_odd = np.zeros((P, 2, P)), np.zeros((HALF, 2, P))
    inv = np.zeros((KINDS, P, HALF))
    for o, fr in ((0, fe), (1, fo)):
        ang = 2 * np.pi * ((t[:, None] * fr[None, :]) % L) / L
        table = (fwd_even, fwd_odd)[o]
        table[:, 0], table[:, 1] = np.cos(ang)[:len(table)], -np.sin(ang)[:len(table)]
        inv[2 * o], inv[2 * o + 1] = 2 * np.cos(ang.T) / L, -2 * np.sin(ang.T) / L
    alt = (-1.0) ** t
    fwd_even[:, 1, 0] = alt[:P]
    inv[0, 0] = 1.0 / L
    inv[1, 0] = alt / L
    tab[:, C_FWD:C_FWD + 256] = fwd_even.reshape(P, -1)
    tab[:, C_FWD + 256:C_INV] = fwd_odd.reshape(2, P, 2 * P).transpose(1, 0, 2).reshape(P, -1)
    tab[:, C_INV:C_TABS] = inv.transpose(1, 0, 2).reshape(P, -1)
    c[:, C_ID:C_IND] = np.eye(P)
    c[:, C_IND:C_IND + 8] = np.arange(P)[:, None] // HD == np.arange(8)[None]
    c[:, C_IND + 8:C_TRI] = -c[:, C_IND:C_IND + 8]
    c[:, C_TRI:C_ONE] = np.arange(P)[:, None] < np.arange(P)[None]
    c[:, C_ONE:C_IOTA] = 1
    c[:, C_IOTA:C_PART] = np.arange(P)[None]
    c[:, C_PART] = np.arange(P)
    c[:, C_THR:C_TILE] = np.arange(TILES)[None] * P
    c[:, C_TILE:C_ROW] = np.arange(TILES)[None] + 1
    c[:, C_ROW] = -1
    c[0:E, C_ROW] = c[32:32 + E, C_ROW] = np.arange(E)
    return tab.astype(np.float32), c.astype(np.float32)


def kernel(**inputs):
    import numpy as _np
    import concourse.bacc as _bacc
    from concourse import mybir as _mybir
    from concourse.bass_utils import run_bass_kernel_spmd as _run

    a = {k: _np.asarray(v) for k, v in inputs.items()}

    def rows(w):
        return w.T.reshape(-1, P, w.shape[0]).transpose(1, 0, 2).reshape(P, -1)

    tabs, const = tables()
    arrays = {
        "x": a["x"], "ctx": a["ctx_1024"],
        "wqkvo": _np.stack([rows(a[f"L0_xattn_W{n}"]) for n in "qkvo"]),
        "bqk": _np.stack([a["L0_xattn_bq"].reshape(DT, P), a["L0_xattn_bk"].reshape(DT, P)]).reshape(2 * DT, P).T,
        "bvo": _np.stack([a["L0_xattn_bv"], a["L0_xattn_bo"]]),
        "gate_w": a["L0_ffn_gate_w"].T, "gate_b": a["L0_ffn_gate_b"].reshape(1, E),
        "w_01": _np.stack([_np.concatenate([rows(a["L0_ffn_w0"][e]), rows(a["L0_ffn_w1"][e])], 1) for e in range(E)]),
        "w_2": _np.stack([rows(a["L0_ffn_w2"][e]) for e in range(E)]),
        "b_ffn": _np.concatenate([a["L0_ffn_b0"], a["L0_ffn_b1"], a["L0_ffn_b2"]], 1),
        "tabs": tabs, "const": const,
    }
    nc = _bacc.Bacc("TRN2", target_bir_lowering=False, num_devices=1)
    feed, args = {}, []
    for name, arr in arrays.items():
        arr = _np.ascontiguousarray(arr)
        feed[f"in_{name}"] = arr
        args.append(nc.dram_tensor(f"in_{name}", arr.shape, _mybir.dt.from_np(arr.dtype), kind="ExternalInput").ap())
    for i, (shape, dtype) in enumerate(_OUTS):
        args.append(nc.dram_tensor(f"out_{i}", shape, _mybir.dt.from_np(_np.dtype(dtype)), kind="ExternalOutput").ap())
    build(nc, *args)
    r = _run(nc, [feed], core_ids=[0])
    return r.results[0]["out_0"]
```
